# Optimizing a Trainium2 kernel written in Bass

```python
import numpy as np
import jax
import jax.numpy as jnp

def _softmax(x, axis=-1):
    return jax.nn.softmax(x, axis=axis)

def _gelu(x):
    return jax.nn.gelu(x, approximate=True)

def _silu(x):
    return jax.nn.silu(x)

def _sigmoid(x):
    return jax.nn.sigmoid(x)

def _layernorm(x, axis=-1, eps=1e-05):
    m = jnp.mean(x, axis=axis, keepdims=True)
    v = jnp.var(x, axis=axis, keepdims=True)
    return (x - m) / jnp.sqrt(v + eps)

def _scatter_add(tgt, idx, src, axis=0):
    return tgt.at[idx].add(src)

def _segment_sum(src, seg, n):
    return jax.ops.segment_sum(src, seg, n)
kernel_name = 'mk_gnn_resnorm_d4_gnn_r8_4a4dd9'

def setup_inputs(seed: int=0):
    np.random.seed(seed)
    _w = jnp.asarray

    def _rec_inputs():
        import jax
        import jax.numpy as jnp
        _gk = jax.random.key(seed)
        x = -0.000202 + 1 * jax.random.normal(jax.random.fold_in(_gk, 1), (6250, 128), jnp.float32)
        _s = jax.random.randint(jax.random.fold_in(_gk, 2), (50000,), 0, 6250, jnp.int32)
        _d = jax.random.randint(jax.random.fold_in(_gk, 3), (50000,), 0, 6250, jnp.int32)
        _loop = jnp.arange(6250, dtype=jnp.int32)
        src = jnp.concatenate([_s, _d, _loop])
        dst = jnp.concatenate([_d, _s, _loop])
        _o = jnp.argsort(dst, stable=True)
        src = src[_o]
        dst = dst[_o]
        edge_attr_64 = 0.000189758 + 1.00013 * jax.random.normal(jax.random.fold_in(_gk, 12), (106250, 64), jnp.float32)
        node_vec = jax.random.uniform(jax.random.fold_in(_gk, 14), (6250,), jnp.float32, 0.0, 49999)
        return (x, src, dst, edge_attr_64, node_vec)
    x, src, dst, edge_attr_64, node_vec = _rec_inputs()

    def _L0_gnn_setup():
        import jax, jax.numpy as jnp
        import numpy as np
        import math
        N = 6250
        E = 50000
        D_IN = 128
        D_H = 512
        N_CLS = 128
        EPS = 1e-05

        def _layernorm(h, g, b):
            m = jnp.mean(h, axis=-1, keepdims=True)
            v = jnp.mean(jnp.square(h - m), axis=-1, keepdims=True)
            return (h - m) * jax.lax.rsqrt(v + EPS) * g + b

        def _graph_conv(x, src, dst, ew, W_rel, b_rel, W_root):
            msg = x[src] * ew[:, None]
            agg = jax.ops.segment_max(msg, dst, num_segments=N)
            agg = jnp.where(jnp.isfinite(agg), agg, 0.0)
            return agg @ W_rel.T + b_rel + x @ W_root.T
        key = jax.random.key(seed)
        ks = jax.random.split(key, 12)
        x = jax.random.normal(ks[0], (N, D_IN), dtype=jnp.float32)
        ei = jax.random.randint(ks[1], (2, E), 0, N, dtype=jnp.int32)
        src, dst = (ei[0], ei[1])
        src = jnp.where(src == dst, (src + 1) % N, src)
        edge_index = jnp.stack([src, dst])
        pos = jnp.arange(N, dtype=jnp.float32)
        s = 0.02
        params = dict(Wrel1=jax.random.normal(ks[2], (D_H, D_IN), jnp.float32) * s, brel1=jnp.zeros((D_H,), jnp.float32), Wroot1=jax.random.normal(ks[3], (D_H, D_IN), jnp.float32) * s, g1=jnp.ones((D_H,), jnp.float32), b1=jnp.zeros((D_H,), jnp.float32), Wrel2=jax.random.normal(ks[4], (D_H, D_H), jnp.float32) * s, brel2=jnp.zeros((D_H,), jnp.float32), Wroot2=jax.random.normal(ks[5], (D_H, D_H), jnp.float32) * s, g2=jnp.ones((D_H,), jnp.float32), b2=jnp.zeros((D_H,), jnp.float32), Wcls=jax.random.normal(ks[6], (N_CLS, D_H), jnp.float32) * s, bcls=jnp.full((N_CLS,), -math.log((1 - 0.01) / 0.01), jnp.float32))
        return dict(x=x, edge_index=edge_index, pos=pos, **params)
    _L0_gnn_all = _L0_gnn_setup()
    _L0_gnn_in = {k: v for k, v in _L0_gnn_all.items() if k in ('Wrel1', 'brel1', 'Wroot1', 'g1', 'b1', 'Wrel2', 'brel2', 'Wroot2', 'g2', 'b2', 'Wcls', 'bcls')}
    del _L0_gnn_all

    def _L1_gnn_setup():
        import jax, jax.numpy as jnp
        import numpy as np
        N = 12500
        E = 200000
        IN_CH = 128
        OUT_CH = 128
        key = jax.random.key(seed)
        k1, k2, k3, k4, k5, k6 = jax.random.split(key, 6)
        x = jax.random.normal(k1, (N, IN_CH), dtype=jnp.float32)
        src = jax.random.randint(k2, (E,), 0, N, dtype=jnp.int32)
        dst = jax.random.randint(k3, (E,), 0, N, dtype=jnp.int32)
        bound = 1.0 / np.sqrt(IN_CH)
        W1 = jax.random.uniform(k4, (OUT_CH, IN_CH), minval=-bound, maxval=bound, dtype=jnp.float32)
        b1 = jax.random.uniform(k5, (OUT_CH,), minval=-bound, maxval=bound, dtype=jnp.float32)
        W2 = jax.random.uniform(k6, (OUT_CH, IN_CH), minval=-bound, maxval=bound, dtype=jnp.float32)
        return {'x': x, 'W1': W1, 'b1': b1, 'W2': W2, 'src': src, 'dst': dst}
    _L1_gnn_all = _L1_gnn_setup()
    _L1_gnn_in = {k: v for k, v in _L1_gnn_all.items() if k in ('W1', 'b1', 'W2')}
    del _L1_gnn_all

    def _L2_gnn_setup():
        import jax, jax.numpy as jnp
        import numpy as np
        N_NODES = 6250
        N_EDGES = 100000
        D_FEAT = 128
        key = jax.random.key(seed)
        k1, k2 = jax.random.split(key)
        x = jax.random.normal(k1, (N_NODES, D_FEAT), dtype=jnp.float32)
        edge_index = jax.random.randint(k2, (2, N_EDGES), 0, N_NODES, dtype=jnp.int64)
        return {'x': x, 'edge_index': edge_index}
    _L2_gnn_all = _L2_gnn_setup()
    _L2_gnn_in = {k: v for k, v in _L2_gnn_all.items() if k in ()}
    del _L2_gnn_all

    def _L3_gnn_setup():
        import jax, jax.numpy as jnp
        import numpy as np
        N, E, IN_DIM, OUT_DIM, EDGE_DIM, HEADS = (6250, 100000, 128, 128, 64, 4)
        C = OUT_DIM // HEADS
        NEG_SLOPE = 0.2
        EPS = 1e-05

        def _gatv2_graphnorm(x, edge_index, edge_attr, Wl, bl, Wr, br, We, att, bias_out, gn_weight, gn_bias, gn_mean_scale):
            src, dst = (edge_index[0], edge_index[1])
            n = x.shape[0]
            deg = jax.ops.segment_sum(jnp.ones((edge_attr.shape[0],), x.dtype), dst, num_segments=n)
            loop_attr = jax.ops.segment_sum(edge_attr, dst, num_segments=n) / jnp.maximum(deg, 1.0)[:, None]
            loop = jnp.arange(n, dtype=src.dtype)
            src_a = jnp.concatenate([src, loop])
            dst_a = jnp.concatenate([dst, loop])
            eattr = jnp.concatenate([edge_attr, loop_attr], axis=0)
            xl = (x @ Wl + bl).reshape(n, HEADS, C)
            xr = (x @ Wr + br).reshape(n, HEADS, C)
            ee = (eattr @ We).reshape(-1, HEADS, C)
            msg = xl[src_a] + xr[dst_a] + ee
            score = jnp.einsum('ehc,hc->eh', jax.nn.leaky_relu(msg, NEG_SLOPE), att)
            smax = jax.ops.segment_max(score, dst_a, num_segments=n)
            ex = jnp.exp(score - smax[dst_a])
            denom = jax.ops.segment_sum(ex, dst_a, num_segments=n)
            alpha = ex / (denom[dst_a] + 1e-16)
            out = jax.ops.segment_sum(alpha[:, :, None] * xl[src_a], dst_a, num_segments=n)
            out = out.reshape(n, HEADS * C) + bias_out
            mean = out.mean(axis=0)
            o = out - mean * gn_mean_scale
            var = (o * o).mean(axis=0)
            out = gn_weight * o / jnp.sqrt(var + EPS) + gn_bias
            return jax.nn.relu(out)
        key = jax.random.key(seed)
        ks = jax.random.split(key, 12)
        x = jax.random.normal(ks[0], (N, IN_DIM), dtype=jnp.float32)
        edge_index = jax.random.randint(ks[1], (2, E), 0, N, dtype=jnp.int64)
        edge_attr = jax.random.normal(ks[2], (E, EDGE_DIM), dtype=jnp.float32)
        s = 0.05
        Wl = jax.random.normal(ks[3], (IN_DIM, HEADS * C), dtype=jnp.float32) * s
        bl = jnp.zeros((HEADS * C,), dtype=jnp.float32)
        Wr = jax.random.normal(ks[4], (IN_DIM, HEADS * C), dtype=jnp.float32) * s
        br = jnp.zeros((HEADS * C,), dtype=jnp.float32)
        We = jax.random.normal(ks[5], (EDGE_DIM, HEADS * C), dtype=jnp.float32) * s
        att = jax.random.normal(ks[6], (HEADS, C), dtype=jnp.float32) * s
        bias_out = jnp.zeros((HEADS * C,), dtype=jnp.float32)
        gn_weight = jnp.ones((OUT_DIM,), dtype=jnp.float32)
        gn_bias = jnp.zeros((OUT_DIM,), dtype=jnp.float32)
        gn_mean_scale = jnp.ones((OUT_DIM,), dtype=jnp.float32)
        return dict(x=x, edge_index=edge_index, edge_attr=edge_attr, Wl=Wl, bl=bl, Wr=Wr, br=br, We=We, att=att, bias_out=bias_out, gn_weight=gn_weight, gn_bias=gn_bias, gn_mean_scale=gn_mean_scale)
    _L3_gnn_all = _L3_gnn_setup()
    _L3_gnn_in = {k: v for k, v in _L3_gnn_all.items() if k in ('Wl', 'bl', 'Wr', 'br', 'We', 'att', 'bias_out', 'gn_weight', 'gn_bias', 'gn_mean_scale')}
    del _L3_gnn_all
    return {'x': x, 'src': src, 'dst': dst, 'edge_attr_64': edge_attr_64, 'node_vec': node_vec, 'L0_gnn_Wrel1': _L0_gnn_in['Wrel1'], 'L0_gnn_brel1': _L0_gnn_in['brel1'], 'L0_gnn_Wroot1': _L0_gnn_in['Wroot1'], 'L0_gnn_g1': _L0_gnn_in['g1'], 'L0_gnn_b1': _L0_gnn_in['b1'], 'L0_gnn_Wrel2': _L0_gnn_in['Wrel2'], 'L0_gnn_brel2': _L0_gnn_in['brel2'], 'L0_gnn_Wroot2': _L0_gnn_in['Wroot2'], 'L0_gnn_g2': _L0_gnn_in['g2'], 'L0_gnn_b2': _L0_gnn_in['b2'], 'L0_gnn_Wcls': _L0_gnn_in['Wcls'], 'L0_gnn_bcls': _L0_gnn_in['bcls'], 'L1_gnn_W1': _L1_gnn_in['W1'], 'L1_gnn_b1': _L1_gnn_in['b1'], 'L1_gnn_W2': _L1_gnn_in['W2'], 'L3_gnn_Wl': _L3_gnn_in['Wl'], 'L3_gnn_bl': _L3_gnn_in['bl'], 'L3_gnn_Wr': _L3_gnn_in['Wr'], 'L3_gnn_br': _L3_gnn_in['br'], 'L3_gnn_We': _L3_gnn_in['We'], 'L3_gnn_att': _L3_gnn_in['att'], 'L3_gnn_bias_out': _L3_gnn_in['bias_out'], 'L3_gnn_gn_weight': _L3_gnn_in['gn_weight'], 'L3_gnn_gn_bias': _L3_gnn_in['gn_bias'], 'L3_gnn_gn_mean_scale': _L3_gnn_in['gn_mean_scale']}

def reference(x, src, dst, edge_attr_64, node_vec, L0_gnn_Wrel1, L0_gnn_brel1, L0_gnn_Wroot1, L0_gnn_g1, L0_gnn_b1, L0_gnn_Wrel2, L0_gnn_brel2, L0_gnn_Wroot2, L0_gnn_g2, L0_gnn_b2, L0_gnn_Wcls, L0_gnn_bcls, L1_gnn_W1, L1_gnn_b1, L1_gnn_W2, L3_gnn_Wl, L3_gnn_bl, L3_gnn_Wr, L3_gnn_br, L3_gnn_We, L3_gnn_att, L3_gnn_bias_out, L3_gnn_gn_weight, L3_gnn_gn_bias, L3_gnn_gn_mean_scale):
    import jax
    import jax.numpy as jnp

    def _L0_gnn_ref(x, edge_index, pos, Wrel1, brel1, Wroot1, g1, b1, Wrel2, brel2, Wroot2, g2, b2, Wcls, bcls):
        import jax, jax.numpy as jnp
        import numpy as np
        import math
        N = 6250
        E = 50000
        D_IN = 128
        D_H = 512
        N_CLS = 128
        EPS = 1e-05

        def _layernorm(h, g, b):
            m = jnp.mean(h, axis=-1, keepdims=True)
            v = jnp.mean(jnp.square(h - m), axis=-1, keepdims=True)
            return (h - m) * jax.lax.rsqrt(v + EPS) * g + b

        def _graph_conv(x, src, dst, ew, W_rel, b_rel, W_root):
            msg = x[src] * ew[:, None]
            agg = jax.ops.segment_max(msg, dst, num_segments=N)
            agg = jnp.where(jnp.isfinite(agg), agg, 0.0)
            return agg @ W_rel.T + b_rel + x @ W_root.T
        src, dst = (edge_index[0], edge_index[1])
        ew = 1.0 / (pos[src] - pos[dst])
        h = _graph_conv(x, src, dst, ew, Wrel1, brel1, Wroot1)
        h = jax.nn.relu(_layernorm(h, g1, b1))
        h = _graph_conv(h, src, dst, ew, Wrel2, brel2, Wroot2)
        h = jax.nn.relu(_layernorm(h, g2, b2))
        return h @ Wcls.T + bcls

    def _L1_gnn_ref(x, W1, b1, W2, src, dst):
        import jax, jax.numpy as jnp
        import numpy as np
        N = 12500
        E = 200000
        IN_CH = 128
        OUT_CH = 128
        n = x.shape[0]
        x1 = x @ W1.T + b1
        x2 = x @ W2.T
        deg = jax.ops.segment_sum(jnp.ones((src.shape[0],), dtype=x.dtype), dst, num_segments=n)[:, None]
        agg = jax.ops.segment_sum(x2[src], dst, num_segments=n)
        return (x1 - x2) * deg + agg

    def _L2_gnn_ref(x, edge_index):
        import jax, jax.numpy as jnp
        import numpy as np
        N_NODES = 6250
        N_EDGES = 100000
        D_FEAT = 128
        msg = x[edge_index[1]]
        out = jax.ops.segment_sum(msg, edge_index[0], num_segments=x.shape[0])
        return out

    def _L3_gnn_ref(x, edge_index, edge_attr, Wl, bl, Wr, br, We, att, bias_out, gn_weight, gn_bias, gn_mean_scale):
        import jax, jax.numpy as jnp
        import numpy as np
        N, E, IN_DIM, OUT_DIM, EDGE_DIM, HEADS = (6250, 100000, 128, 128, 64, 4)
        C = OUT_DIM // HEADS
        NEG_SLOPE = 0.2
        EPS = 1e-05

        def _gatv2_graphnorm(x, edge_index, edge_attr, Wl, bl, Wr, br, We, att, bias_out, gn_weight, gn_bias, gn_mean_scale):
            src, dst = (edge_index[0], edge_index[1])
            n = x.shape[0]
            deg = jax.ops.segment_sum(jnp.ones((edge_attr.shape[0],), x.dtype), dst, num_segments=n)
            loop_attr = jax.ops.segment_sum(edge_attr, dst, num_segments=n) / jnp.maximum(deg, 1.0)[:, None]
            loop = jnp.arange(n, dtype=src.dtype)
            src_a = jnp.concatenate([src, loop])
            dst_a = jnp.concatenate([dst, loop])
            eattr = jnp.concatenate([edge_attr, loop_attr], axis=0)
            xl = (x @ Wl + bl).reshape(n, HEADS, C)
            xr = (x @ Wr + br).reshape(n, HEADS, C)
            ee = (eattr @ We).reshape(-1, HEADS, C)
            msg = xl[src_a] + xr[dst_a] + ee
            score = jnp.einsum('ehc,hc->eh', jax.nn.leaky_relu(msg, NEG_SLOPE), att)
            smax = jax.ops.segment_max(score, dst_a, num_segments=n)
            ex = jnp.exp(score - smax[dst_a])
            denom = jax.ops.segment_sum(ex, dst_a, num_segments=n)
            alpha = ex / (denom[dst_a] + 1e-16)
            out = jax.ops.segment_sum(alpha[:, :, None] * xl[src_a], dst_a, num_segments=n)
            out = out.reshape(n, HEADS * C) + bias_out
            mean = out.mean(axis=0)
            o = out - mean * gn_mean_scale
            var = (o * o).mean(axis=0)
            out = gn_weight * o / jnp.sqrt(var + EPS) + gn_bias
            return jax.nn.relu(out)
        return _gatv2_graphnorm(x, edge_index, edge_attr, Wl, bl, Wr, br, We, att, bias_out, gn_weight, gn_bias, gn_mean_scale)
    edge_index = jnp.stack([src, dst])
    x = _layernorm(x + _L0_gnn_ref(x, edge_index, node_vec, L0_gnn_Wrel1, L0_gnn_brel1, L0_gnn_Wroot1, L0_gnn_g1, L0_gnn_b1, L0_gnn_Wrel2, L0_gnn_brel2, L0_gnn_Wroot2, L0_gnn_g2, L0_gnn_b2, L0_gnn_Wcls, L0_gnn_bcls), axis=-1)
    x = _layernorm(x + _L1_gnn_ref(x, L1_gnn_W1, L1_gnn_b1, L1_gnn_W2, src, dst), axis=-1)
    x = _layernorm(x + _L2_gnn_ref(x, edge_index), axis=-1)
    x = _layernorm(x + _L3_gnn_ref(x, edge_index, edge_attr_64, L3_gnn_Wl, L3_gnn_bl, L3_gnn_Wr, L3_gnn_br, L3_gnn_We, L3_gnn_att, L3_gnn_bias_out, L3_gnn_gn_weight, L3_gnn_gn_bias, L3_gnn_gn_mean_scale), axis=-1)
    return x

_drawn_inputs = setup_inputs


def setup_inputs(seed=0):
    import zlib

    import numpy as np

    out = dict(_drawn_inputs(seed))
    spreads = {'L0_gnn_brel1': (0.0, 0.1),
     'L0_gnn_g1': (1.0, 0.2),
     'L0_gnn_b1': (0.0, 0.362),
     'L0_gnn_brel2': (0.0, 0.1),
     'L0_gnn_g2': (1.0, 0.2),
     'L0_gnn_b2': (0.0, 0.268),
     'L0_gnn_bcls': (-4.595119953155518, 0.2),
     'L3_gnn_bl': (0.0, 0.1),
     'L3_gnn_br': (0.0, 0.8),
     'L3_gnn_bias_out': (0.0, 0.1),
     'L3_gnn_gn_weight': (1.0, 0.2),
     'L3_gnn_gn_bias': (0.0, 0.1),
     'L3_gnn_gn_mean_scale': (1.0, 0.2)}
    factors = {'node_vec': 8.0, 'L0_gnn_Wrel1': 8.0, 'L3_gnn_Wr': 5.737, 'L3_gnn_We': 2.753}
    for name, (base, spread) in spreads.items():
        noise = np.random.default_rng([zlib.crc32(name.encode()), seed]).standard_normal(out[name].shape)
        drawn = base * np.exp(spread * noise) if base else spread * noise
        out[name] = jnp.asarray(drawn.astype(out[name].dtype))
    for name, factor in factors.items():
        out[name] = (out[name] * factor).astype(out[name].dtype)
    return out
```

```python
import concourse.bass as bass
from concourse import mybir
from contextlib import ExitStack

F32 = mybir.dt.float32
I32 = mybir.dt.int32
ALU = mybir.AluOpType
ACT = mybir.ActivationFunctionType
AX = mybir.AxisListType

N = 6250
E = 106250
F = 128
DH = 512
DE = 64
HEADS = 4
C = F // HEADS
P = 128
NT = -(-N // P)
NTP = NT + NT % 2
NP = NTP * P
EF = E // P
EREM = E - EF * P
ET = EF + 2
U = 16
GS = 4
NG = U // GS
STEPS = EF + 1 + NT - 1
TURNS = -(-STEPS // U)
SP_ = TURNS * U
KB = -(-SP_ // P)
PAD = 1 << 20
BIG = 3e38
HALFBIG = 1e38
EPS = 1e-5
W = 2 * F + 1


def wait(eng, sem, value):
    if isinstance(value, int) and value <= 0:
        return
    eng.wait_ge(sem, value)


def turns(eng, body, n, last=0):
    body(0)
    with eng.Fori(1, n) as it:
        body(it)


class Memory:

    def __init__(self, nc, ctx):
        self.nc, self.ctx, self.sems = nc, ctx, []
        ctx.callback(self.end)

    def end(self):
        if self.sems:
            self.nc.clear_and_free_semaphores(self.sems)
            self.nc.all_engine_barrier()

    def sb(self, name, shape, dt=F32):
        return self.ctx.enter_context(self.nc.sbuf_tensor(name, shape, dt))

    def bank(self, name):
        return self.ctx.enter_context(self.nc.psum_tensor(name, [P, 512], F32))

    def sem(self, name):
        self.sems.append(self.nc.alloc_semaphore(name))
        return self.sems[-1]


def bc_last(ap, n):
    return ap.unsqueeze(2).broadcast_to([ap.shape[0], ap.shape[1], n])


def bc_mid(ap, n):
    return ap.unsqueeze(1).broadcast_to([ap.shape[0], n, ap.shape[1]])


def prepare(nc, g, a):
    with ExitStack() as ctx:
        m = Memory(nc, ctx)
        padc = m.sb("padc", [2, 4 * P], I32)
        dst_i = m.sb("dst_i", [P, KB, P], I32)
        dst_f = m.sb("dst_f", [P, KB * P])
        less = m.sb("less", [P, KB * P])
        cnt = m.sb("cnt", [P, NT - 1])
        start_i = m.sb("start_i", [P, NT - 1], I32)
        first_i = m.sb("first_i", [P, NT - 1], I32)
        first_f = m.sb("first_f", [P, NT - 1])
        tile_no = m.sb("tile_no", [P, NT - 1])
        stepno = m.sb("stepno", [P, KB])
        le = m.sb("le", [P, NT - 1])
        T_f = m.sb("T_f", [P, KB])
        T_i = m.sb("T_i", [P, KB], I32)
        T128 = m.sb("T128", [P, KB])
        t_f = m.sb("t_f", [P, KB])
        t_i = m.sb("t_i", [P, KB], I32)
        rows = m.sb("rows", [P, KB, 4 * P], I32)
        rows_f = m.sb("rows_f", [P, KB, 4, P])
        flag = m.sb("flag", [P, KB, P])
        endf_r = m.sb("endf_r", [P, KB, P])
        drel_r = m.sb("drel_r", [P, KB, P])
        sgn = m.sb("sgn", [P, NTP, F])
        start_ps = m.bank("start_ps")
        tr_ps = [m.bank(f"tr_ps{i}") for i in range(2)]
        s_init = m.sem("s_init")
        s_x = m.sem("s_x")
        s_pos = m.sem("s_pos")
        s_padded = m.sem("s_padded")
        s_built = m.sem("s_built")
        s_dst = m.sem("s_dst")
        s_v = m.sem("s_v")
        s_start = m.sem("s_start")
        s_rows = m.sem("s_rows")
        s_tr = m.sem("s_tr")
        s_cp = m.sem("s_cp")
        s_out = m.sem("s_out")
        s_T = m.sem("s_T")
        s_Tl = m.sem("s_Tl")
        ct = g.ct
        V_X = 5
        V_CNT = V_X + NT - 1
        V_T = V_CNT + 4 + 5 * KB

        with nc.Block() as block:
            @block.gpsimd
            def _(p):
                p.iota(g.iota_n[:, :], [[1, P]], base=0, channel_multiplier=0,
                       allow_small_or_imprecise_dtypes=True).then_inc(s_init, 1)
                p.iota(g.iota_p[:, :], [[0, 1]], base=0, channel_multiplier=1,
                       allow_small_or_imprecise_dtypes=True).then_inc(s_init, 1)
                p.iota(tile_no[:, :], [[1, NT - 1]], base=1, channel_multiplier=0,
                       allow_small_or_imprecise_dtypes=True).then_inc(s_init, 1)
                p.iota(stepno[:, :], [[P, KB]], base=0, channel_multiplier=1,
                       allow_small_or_imprecise_dtypes=True).then_inc(s_init, 1)
                p.memset(g.ones[:, :], 1.0).then_inc(s_init, 1)
                p.memset(padc[:, 0:P], 0).then_inc(s_init, 1)
                p.memset(padc[:, P:4 * P], PAD).then_inc(s_init, 1)
                p.memset(dst_i[:, :, :], PAD).then_inc(s_init, 1)
                p.memset(g.x[:, :, :], 0.0).then_inc(s_init, 1)
                p.memset(g.posb[:, N:NP], 0.0).then_inc(s_init, 1)
                p.memset(g.ident[:, :], 0.0).then_inc(s_init, 1)
                p.wait_ge(s_init, 11)
                p.affine_select(out=g.ident[:, :], in_=g.ident[:, :], compare_op=ALU.not_equal, fill=1.0,
                                base=0, pattern=[[-1, P]], channel_multiplier=1).then_inc(s_init, 1)
                p.wait_ge(s_v, V_T)
                p.wait_ge(s_built, 16 * 7)
                for b in range(KB):
                    p.indirect_dma_start(out=rows[:, b, :], out_offset=None, in_=ct[:, :],
                                         in_offset=bass.IndirectOffsetOnAxis(ap=t_i[:, b:b + 1], axis=0)
                                         ).then_inc(s_rows, 16)

            @block.sync
            def _(s):
                s.wait_ge(s_init, 11)
                s.dma_start(ct[EF:EF + 2, :], padc[:, :]).then_inc(s_padded, 16)
                s.dma_start(ct[0:1, 2 * P:2 * P + 1], padc[0:1, P:P + 1]).then_inc(s_padded, 16)
                full = (ET // P) * P
                s.dma_start(dst_i[:, 0:ET // P, :],
                            a["dst"][0:full * P].rearrange("(b p e) -> p b e", p=P, e=P)).then_inc(s_dst, 16)
                s.dma_start(dst_i[0:EF - full, ET // P, :],
                            a["dst"][full * P:EF * P].rearrange("(p e) -> p e", e=P)).then_inc(s_dst, 16)
                s.dma_start(dst_i[EF - full:EF - full + 1, ET // P, 0:EREM],
                            a["dst"][EF * P:E].unsqueeze(0)).then_inc(s_dst, 16)
                s.wait_ge(s_padded, 32)
                s.dma_start(ct[0:EF, 0:P], a["src"][0:EF * P].rearrange("(t e) -> t e", e=P)).then_inc(s_built, 16)
                s.dma_start(ct[0:EF, P:2 * P], a["dst"][0:EF * P].rearrange("(t e) -> t e", e=P)).then_inc(s_built, 16)
                s.dma_start(ct[1:EF, 2 * P:3 * P],
                            a["dst"][P - 1:EF * P - 1].rearrange("(t e) -> t e", e=P)).then_inc(s_built, 16)
                s.dma_start(ct[0:EF, 3 * P:4 * P],
                            a["dst"][1:EF * P + 1].rearrange("(t e) -> t e", e=P)).then_inc(s_built, 16)
                s.dma_start(ct[0:1, 2 * P + 1:3 * P], a["dst"][0:P - 1].unsqueeze(0)).then_inc(s_built, 16)
                s.dma_start(ct[EF:EF + 1, 0:2 * P].rearrange("o (c e) -> o c e", c=2)[:, 0, 0:EREM],
                            a["src"][EF * P:E].unsqueeze(0)).then_inc(s_built, 16)
                for off, lo, n in ((P, 0, EREM), (2 * P, -1, EREM), (3 * P, 1, EREM - 1)):
                    s.dma_start(ct[EF:EF + 1, off:off + n],
                                a["dst"][EF * P + lo:EF * P + lo + n].unsqueeze(0)).then_inc(s_padded, 16)
                s.wait_ge(s_padded, 32 + 48)
                s.sem_inc(s_built, 16)
                s.wait_ge(s_v, V_T + 8)
                nb = SP_ // P
                for dst, srct in ((g.d0row, flag[:, :, :]), (g.drelrow, drel_r[:, :, :]), (g.srcrow, rows_f[:, :, 0, :])):
                    s.dma_start(dst[0:nb * P, :].rearrange("(b p) e -> p b e", p=P), srct[:, 0:nb, :]).then_inc(s_out, 16)
                    s.dma_start(dst[nb * P:SP_, :], srct[0:SP_ - nb * P, nb, :]).then_inc(s_out, 16)
                s.wait_ge(s_out, 96)

            @block.scalar
            def _(s):
                s.wait_ge(s_init, 10)
                s.dma_start(g.x[:, 0:NT - 1, :], a["x"][0:(NT - 1) * P, :].rearrange("(t p) f -> p t f", p=P)
                            ).then_inc(s_x, 16)
                s.dma_start(g.x[0:N - (NT - 1) * P, NT - 1, :], a["x"][(NT - 1) * P:N, :]).then_inc(s_x, 16)
                s.dma_start(g.posb[:, 0:N], a["node_vec"].partition_broadcast(P)).then_inc(s_pos, 16)
                s.dma_start(g.xp[0:N, 2 * F:2 * F + 1], a["node_vec"].unsqueeze(1)).then_inc(s_pos, 16)
                s.dma_start(g.xp[0:N, 0:F], a["x"][:, :]).then_inc(s_pos, 16)
                s.wait_ge(s_v, V_T)
                s.dma_start(g.trow[0:KB * P].rearrange("(b p) -> p b", p=P), T_i[:, :]).then_inc(s_T, 16)
                s.dma_start(g.erow[0:KB * P].rearrange("(b p) -> p b", p=P), t_i[:, :]).then_inc(s_T, 16)
                s.wait_ge(s_T, 32)
                s.dma_start(g.T[:, :], g.trow[0:SP_].unsqueeze(0)).then_inc(s_Tl, 16)
                s.dma_start(g.t[:, :], g.erow[0:SP_].unsqueeze(0)).then_inc(s_Tl, 16)
                s.dma_start(g.xp[:, F:2 * F].rearrange("(t p) f -> p t f", p=P), sgn[:, :, :]).then_inc(s_pos, 16)
                s.wait_ge(s_Tl, 32)
                s.wait_ge(s_pos, 64)

            @block.tensor
            def _(t):
                t.wait_ge(s_init, 12)
                t.wait_ge(s_v, V_CNT)
                t.matmul(start_ps[:, 0:NT - 1], g.ones[:, :], cnt[:, :], start=True, stop=True).then_inc(s_start, 1)
                t.wait_ge(s_v, V_T + 8)
                i = 0
                for b in range(KB):
                    for src in (rows_f[:, b, 0, :], drel_r[:, b, :], endf_r[:, b, :]):
                        wait(t, s_cp, i - 1)
                        t.transpose(tr_ps[i % 2][:, 0:P], src, g.ident[:, :]).then_inc(s_tr, 1)
                        i += 1

            @block.vector
            def _(v):
                done = 0

                def step(ins):
                    nonlocal done
                    ins.then_inc(s_v, 1)
                    done += 1

                def link(ins):
                    step(ins)
                    v.wait_ge(s_v, done)

                v.wait_ge(s_dst, 48)
                v.wait_ge(s_init, 12)
                v.wait_ge(s_x, 32)
                link(v.tensor_scalar(g.valid[:, :], g.ones[:, :], g.iota_p[:, :], None, ALU.mult))
                link(v.tensor_scalar(g.valid[:, :], g.valid[:, :], float(N - (NT - 1) * P), None, ALU.is_lt))
                link(v.tensor_copy(dst_f[:, :], dst_i[:, :, :].rearrange("p b e -> p (b e)")))
                link(v.tensor_scalar(sgn[:, :, :], g.x[:, :, :], 0.0, 0.5, ALU.is_ge, ALU.subtract))
                link(v.memset(less[:, :], 0.0))
                assert done == V_X
                for T in range(1, NT):
                    link(v.tensor_scalar(less[:, :], dst_f[:, :], float(T * P), 0.0, ALU.is_lt, ALU.add,
                                         accum_out=cnt[:, T - 1:T]))
                assert done == V_CNT
                v.wait_ge(s_start, 1)
                link(v.tensor_copy(start_i[:, :], start_ps[:, 0:NT - 1]))
                link(v.tensor_scalar(first_i[:, :], start_i[:, :], 7, None, ALU.arith_shift_right))
                link(v.tensor_copy(first_f[:, :], first_i[:, :]))
                link(v.tensor_tensor(first_f[:, :], first_f[:, :], tile_no[:, :], ALU.add))
                for b in range(KB):
                    col = slice(b, b + 1)
                    link(v.tensor_scalar(le[:, :], first_f[:, :], stepno[:, col], 0.0, ALU.is_le, ALU.add,
                                         accum_out=T_f[:, col]))
                    link(v.tensor_copy(T_i[:, col], T_f[:, col]))
                    link(v.tensor_tensor(t_f[:, col], stepno[:, col], T_f[:, col], ALU.subtract))
                    link(v.tensor_scalar(t_f[:, col], t_f[:, col], float(ET - 1), None, ALU.min))
                    link(v.tensor_copy(t_i[:, col], t_f[:, col]))
                assert done == V_T
                v.wait_ge(s_rows, 16 * KB)
                link(v.tensor_copy(rows_f[:, :, :, :], rows[:, :, :].rearrange("p b (c e) -> p b c e", c=4)))
                link(v.tensor_scalar(T128[:, :], T_f[:, :], float(P), None, ALU.mult))
                link(v.tensor_tensor(drel_r[:, :, :], rows_f[:, :, 1, :], bc_last(T128[:, :], P), ALU.subtract))
                link(v.tensor_tensor(endf_r[:, :, :], rows_f[:, :, 1, :], rows_f[:, :, 3, :], ALU.not_equal))
                link(v.tensor_tensor(flag[:, :, :], rows_f[:, :, 1, :], rows_f[:, :, 2, :], ALU.not_equal))
                link(v.tensor_scalar(flag[:, :, :], flag[:, :, :], -2.0, 1.0, ALU.mult, ALU.add))
                link(v.tensor_scalar(flag[:, :, :], flag[:, :, :], BIG, None, ALU.mult))
                link(v.tensor_scalar(T128[:, :], T_f[:, :], float(P), None, ALU.mult))
                assert done == V_T + 8
                i = 0
                for b in range(KB):
                    for to in (g.src_f, g.drel, g.endf):
                        v.wait_ge(s_tr, i + 1)
                        v.tensor_copy(to[:, b * P:(b + 1) * P], tr_ps[i % 2][:, 0:P]).then_inc(s_cp, 1)
                        i += 1
                v.wait_ge(s_cp, i)
                v.tensor_copy(g.src_i[:, :], g.src_f[:, :]).then_inc(s_cp, 1)


def max_pass(nc, g, tag, table, acc, counts):
    with ExitStack() as ctx:
        m = Memory(nc, ctx)
        ring = m.sb(f"ring{tag}", [P, U, W])
        idx = m.sb(f"idx{tag}", [P, U], I32)
        hot = m.sb(f"hot{tag}", [P, NG, GS, P])
        msg = m.sb(f"msg{tag}", [P, 2, GS, F])
        sgn = m.sb(f"sg{tag}", [P, 2, GS, F])
        run = m.sb(f"run{tag}", [P, 2, GS * P])
        ends = m.sb(f"ends{tag}", [P, 2, GS, F])
        reset = m.sb(f"reset{tag}", [P, 2, 2 * GS * P])
        posd = m.sb(f"posd{tag}", [P, GS])
        junk = m.sb(f"junk{tag}", [P, GS, P])
        nd = m.sb(f"nd{tag}", [P, GS])
        dz = m.sb(f"dz{tag}", [P, GS])
        wn = m.sb(f"wn{tag}", [P, GS])
        w2 = m.sb(f"w2{tag}", [P, GS])
        zs = m.sb(f"zs{tag}", [P, 2, GS])
        ones2 = m.sb(f"ones2{tag}", [P, NG, GS, 2])
        msgT = [m.bank(f"msgT{tag}{i}") for i in range(2)]
        runT = [m.bank(f"runT{tag}{i}") for i in range(2)]
        sel = [m.bank(f"sel{tag}{i}") for i in range(2)]
        cps = [m.bank(f"cps{tag}{i}") for i in range(2)]
        s_idx = m.sem(f"s_idx{tag}")
        s_go = m.sem(f"s_go{tag}")
        s_g = [m.sem(f"s_g{tag}{i}") for i in range(NG)]
        s_rst = [m.sem(f"s_rst{tag}{i}") for i in range(2)]
        s_hot = m.sem(f"s_hot{tag}")
        s_c = m.sem(f"s_c{tag}")
        s_z = m.sem(f"s_z{tag}")
        s_sg = m.sem(f"s_sg{tag}")
        s_m = m.sem(f"s_m{tag}")
        s_mT = m.sem(f"s_mT{tag}")
        s_run = m.sem(f"s_run{tag}")
        s_rT = m.sem(f"s_rT{tag}")
        s_e = m.sem(f"s_e{tag}")
        s_sel = m.sem(f"s_sel{tag}")
        s_acc = m.sem(f"s_acc{tag}")
        s_cnt = m.sem(f"s_cnt{tag}")
        s_ini = m.sem(f"s_ini{tag}")
        NCH = 4

        with nc.Block() as block:
            @block.gpsimd
            def _(p):
                def body(it):
                    for k in range(U):
                        q = k // GS
                        if k % GS == 0:
                            if not isinstance(it, int):
                                p.wait_ge(s_m, it * NG - NG + q + 1)
                                p.sem_inc(s_go, 1)
                            p.tensor_copy(idx[:, k:k + GS], g.src_i[:, bass.ds(it * U + k, GS)]).then_inc(s_idx, 1)
                            p.wait_ge(s_idx, it * NG + q + 1)
                            p.sem_inc(s_go, 1)
                        p.indirect_dma_start(out=ring[:, k, :], out_offset=None, in_=table,
                                             in_offset=bass.IndirectOffsetOnAxis(ap=idx[:, k:k + 1], axis=0)
                                             ).then_inc(s_g[k // GS], 16)
                turns(p, body, TURNS)

            @block.sync
            def _(s):
                def body(it):
                    for h in range(2):
                        if not isinstance(it, int):
                            s.wait_ge(s_run, it * NG - NG + 2 * h + 2)
                        rows = g.d0flat[bass.ds(it * (U * P) + h * (U * P // 2), U * P // 2)]
                        s.dma_start(reset[:, h, :], rows.partition_broadcast(P)).then_inc(s_rst[h], 16)
                turns(s, body, TURNS)

            @block.scalar
            def _(s):
                def ends_of(G, q):
                    wait(s, s_rT, G + 1)
                    wait(s, s_sel, G - 1)
                    for k in range(GS):
                        ins = s.activation(ends[:, q % 2, k, :], runT[q % 2][:, k * P:(k + 1) * P], ACT.Copy,
                                           scale=g.endf[:, bass.ds(G * GS + k, 1)])
                    ins.then_inc(s_e, 1)

                def body(it):
                    for q in range(NG):
                        G = it * NG + q
                        wait(s, s_g[q], 64 * (it + 1))
                        wait(s, s_z, G + 1)
                        wait(s, s_m, G - 1)
                        for k in range(GS):
                            ins = s.activation(sgn[:, q % 2, k, :], ring[:, q * GS + k, F:2 * F], ACT.Copy,
                                               scale=zs[:, q % 2, k:k + 1])
                        ins.then_inc(s_sg, 1)
                        if not (isinstance(it, int) and q < 1):
                            ends_of(G - 1, (q - 1) % NG)
                turns(s, body, TURNS)
                ends_of(TURNS * NG - 1, NG - 1)

            @block.tensor
            def _(t):
                def back(G, q):
                    wait(t, s_run, G + 1)
                    wait(t, s_e, G - 1)
                    for k in range(GS):
                        ins = t.transpose(runT[q % 2][:, k * P:(k + 1) * P], run[:, q % 2, k * P:(k + 1) * P],
                                          g.ident[:, :])
                    ins.then_inc(s_rT, 1)

                def select(G, q):
                    wait(t, s_e, G + 1)
                    wait(t, s_acc, (G - 1) * GS)
                    wait(t, s_cnt, (G - 1) * GS)
                    for k in range(GS):
                        t.matmul(sel[q % 2][:, k * P:(k + 1) * P], ends[:, q % 2, k, :], hot[:, q, k, :],
                                 start=True, stop=True)
                        ins = t.matmul(cps[q % 2][:, 2 * k:2 * k + 2], hot[:, q, k, :], ones2[:, q, k, :], start=True, stop=True)
                    ins.then_inc(s_sel, 1)

                def body(it):
                    for q in range(NG):
                        G = it * NG + q
                        first = isinstance(it, int)
                        wait(t, s_m, G + 1)
                        wait(t, s_run, G - 1)
                        for k in range(GS):
                            ins = t.transpose(msgT[q % 2][:, k * P:(k + 1) * P], msg[:, q % 2, k, :], g.ident[:, :])
                        ins.then_inc(s_mT, 1)
                        if not (first and q < 1):
                            back(G - 1, (q - 1) % NG)
                        if not (first and q < 2):
                            select(G - 2, (q - 2) % NG)
                turns(t, body, TURNS)
                GL = TURNS * NG
                back(GL - 1, NG - 1)
                select(GL - 2, NG - 2)
                select(GL - 1, NG - 1)

            @block.vector
            def _(v):
                v.memset(acc[:, :], 0.0).then_inc(s_ini, 1)
                v.memset(counts[:, :], 0.0).then_inc(s_ini, 1)
                v.memset(run[:, :, :], -BIG).then_inc(s_ini, 1)
                v.memset(ones2[:, :, :, :], 1.0).then_inc(s_ini, 1)
                v.wait_ge(s_ini, 4)
                tregs = [v.alloc_register(f"t{tag}{j}") for j in range(GS)]
                aregs = [v.alloc_register(f"a{tag}{j}") for j in range(GS)]

                def tiles_of(G, regs):
                    v.load(regs, g.T[0:1, bass.ds(G * GS, GS)])
                    return [v.snap(r, min_val=0, max_val=NT - 1) for r in regs]

                def scan(G, q, it_half, h):
                    wait(v, s_mT, G + 1)
                    if q % 2 == 0:
                        wait(v, s_rst[h], 16 * (it_half + 1))
                    wait(v, s_run, G)
                    wait(v, s_rT, G - 1)
                    v.tensor_tensor_scan(run[:, q % 2, :], reset[:, h, (q % 2) * GS * P:(q % 2 + 1) * GS * P],
                                         msgT[q % 2][:, :], run[:, (q + 1) % 2, GS * P - 1:GS * P],
                                         ALU.min, ALU.max).then_inc(s_run, 1)

                def add(G, q):
                    T = tiles_of(G, aregs)
                    wait(v, s_sel, G + 1)
                    for k in range(GS):
                        wait(v, s_acc, G * GS + k)
                        to = acc[:, bass.ds(T[k] * P, P)]
                        v.tensor_tensor(to, to, sel[q % 2][:, k * P:(k + 1) * P], ALU.add).then_inc(s_acc, 1)
                    for k in range(GS):
                        wait(v, s_cnt, G * GS + k)
                        to = counts[:, bass.ds(T[k] * 2, 2)]
                        v.tensor_tensor(to, to, cps[q % 2][:, 2 * k:2 * k + 2], ALU.add).then_inc(s_cnt, 1)

                def body(it):
                    first = isinstance(it, int)
                    for q in range(NG):
                        G = it * NG + q
                        wait(v, s_sel, G - NG + 1)
                        v.tensor_tensor(hot[:, q, :, :], bc_mid(g.iota_n[:, :], GS),
                                        bc_last(g.drel[:, bass.ds(G * GS, GS)], P), ALU.is_equal).then_inc(s_hot, 1)
                        T = tiles_of(G, tregs)
                        for k in range(GS):
                            ins = v.scalar_tensor_tensor(
                                out=junk[:, k, :], in0=g.iota_n[:, :], scalar=g.drel[:, bass.ds(G * GS + k, 1)],
                                in1=g.posb[:, bass.ds(T[k] * P, P)], op0=ALU.is_equal, op1=ALU.mult,
                                accum_out=posd[:, k:k + 1])
                        ins.then_inc(s_c, 1)
                        v.wait_ge(s_c, G * NCH + 1)
                        v.wait_ge(s_g[q], 64 * (it + 1))
                        wait(v, s_sg, G - 1)
                        poss = ring[:, q * GS:(q + 1) * GS, 2 * F]
                        v.tensor_tensor(nd[:, :], posd[:, :], poss, ALU.subtract).then_inc(s_c, 1)
                        v.wait_ge(s_c, G * NCH + 2)
                        v.tensor_scalar(zs[:, q % 2, :], nd[:, :], 0.0, BIG, ALU.is_equal, ALU.mult).then_inc(s_z, 1)
                        v.tensor_scalar(ones2[:, q, :, 1], nd[:, :], 0.0, None, ALU.is_equal)
                        v.scalar_tensor_tensor(out=dz[:, :], in0=nd[:, :], scalar=0.0, in1=nd[:, :],
                                               op0=ALU.is_equal, op1=ALU.add).then_inc(s_c, 1)
                        v.wait_ge(s_c, G * NCH + 3)
                        v.reciprocal(wn[:, :], dz[:, :]).then_inc(s_c, 1)
                        v.wait_ge(s_c, G * NCH + 4)
                        v.scalar_tensor_tensor(out=w2[:, :], in0=nd[:, :], scalar=0.0, in1=wn[:, :],
                                               op0=ALU.is_equal, op1=ALU.subtract).then_inc(s_hot, 1)
                        v.wait_ge(s_hot, 2 * (G + 1))
                        v.wait_ge(s_sg, G + 1)
                        wait(v, s_mT, G - 1)
                        for k in range(GS):
                            ins = v.scalar_tensor_tensor(
                                out=msg[:, q % 2, k, :], in0=ring[:, q * GS + k, 0:F], scalar=w2[:, k:k + 1],
                                in1=sgn[:, q % 2, k, :], op0=ALU.mult, op1=ALU.add)
                        ins.then_inc(s_m, 1)
                        if not (first and q < 1):
                            scan(G - 1, (q - 1) % NG, it if q else it - 1, ((q - 1) % NG) // 2)
                        if not (first and q < 3):
                            add(G - 3, (q - 3) % NG)
                turns(v, body, TURNS)
                GL = TURNS * NG
                scan(GL - 1, NG - 1, TURNS - 1, 1)
                for b in (3, 2, 1):
                    add(GL - b, NG - b)


class Events:

    def __init__(self, sem, names):
        self.sem, self.names = sem, names

    def value(self, it, name, j):
        return it * (2 * len(self.names)) + 2 * self.names.index(name) + j + 1

    def wait(self, eng, it, name, j):
        eng.wait_ge(self.sem, self.value(it, name, j))


class Chain:

    def __init__(self, eng, sem, it, per):
        self.eng, self.sem, self.base, self.per, self.n = eng, sem, it * per, per, 0

    def link(self, ins):
        self.n += 1
        ins.then_inc(self.sem, 1)
        self.eng.wait_ge(self.sem, self.base + self.n)

    def end(self):
        assert self.n == self.per, (self.n, self.per)


def nodes_layernorm(v, ch, x, tmp, mean, var, s_root):
    ch.link(v.tensor_reduce(mean, x, AX.X, ALU.add))
    ch.link(v.tensor_scalar(mean, mean, 1.0 / F, None, ALU.mult))
    ch.link(v.tensor_tensor(x, x, bc_last(mean, F), ALU.subtract))
    ch.link(v.tensor_tensor(tmp, x, x, ALU.mult))
    ch.link(v.tensor_reduce(var, tmp, AX.X, ALU.add))
    ch.link(v.tensor_scalar(var, var, 1.0 / F, EPS, ALU.mult, ALU.add))
    ready = ch.n
    v.wait_ge(s_root, 1)
    ch.link(v.reciprocal(var, var))
    ch.link(v.tensor_tensor(x, x, bc_last(var, F), ALU.mult))
    return ready


def root_of_variance(block, ready, s, var, s_root):
    @block.scalar
    def _(e):
        e.wait_ge(s, ready)
        e.activation(var[:, :], var[:, :], ACT.Sqrt).then_inc(s_root, 1)


HALF_TILES = NTP // 2


def layer0(nc, g, a, tag, first, second):
    both = first and second
    with ExitStack() as ctx:
        m = Memory(nc, ctx)
        KD = DH // P
        sb = lambda name, shape: m.sb(name + tag, shape)
        wrel1, wroot1 = sb("wrel1", [P, DH]), sb("wroot1", [P, DH])
        wroot2 = sb("wroot2", [P, KD, DH])
        wrel2 = sb("wrel2", [P, KD, DH])
        wcls = sb("wcls", [P, KD, F])
        w12 = sb("w12", [P, 2, F])
        vec = {n: sb(n, [P, DH]) for n in ("brel1", "g1", "b1", "brel2", "g2", "b2")}
        vec.update({n: sb(n, [P, F]) for n in ("bcls", "L1b1")})
        xs, xT = sb("xs", [P, 2, F]), sb("xT", [P, 2, P])
        low, finite = sb("low", [P, 2, P]), sb("finite", [P, 2, P])
        agg = sb("agg", [P, 2, P])
        h = [sb(f"h{i}", [P, 2, DH]) for i in range(2)]
        hT = [sb(f"hT{i}", [P, 2, DH]) for i in range(2)]
        hr = sb("hr", [P, 2, DH])
        agg2, low2 = sb("agg2", [P, 2, DH]), sb("low2", [P, 2, DH])
        y, yT = sb("y", [P, 2, F]), sb("yT", [P, 2, P])
        x2 = sb("x2", [P, 2, F])
        st, mv = sb("st", [P, 3, 2, 6]), sb("mv", [P, 3, 2, 2])
        root = sb("root", [P, 3, 2])
        tr = [m.bank(f"tr{tag}{j}") for j in range(2)]
        big = [m.bank(f"big{tag}{j}") for j in range(2)]
        small = [m.bank(f"small{tag}{j}") for j in range(2)]
        s_w = m.sem("s_w" + tag)
        s_load = [m.sem(f"s_load{tag}{j}") for j in range(2)]
        s_store = [m.sem(f"s_store{tag}{j}") for j in range(2)]
        s_chain = m.sem("s_chain" + tag)
        s_go = m.sem("s_go" + tag)
        pe_names, act_names, dve_names = [], [], []
        if first:
            pe_names += ["xT", "h1", "h1T"]
            act_names += ["xs", "xT", "root1", "h1T"] + ([] if both else ["hr"])
            dve_names += ["agg", "var1", "h1"]
        if second:
            pe_names += ["h2", "h2T", "cls", "yT", "x12"]
            act_names += ["root2", "h2T", "rooty", "yT", "x2"]
            dve_names += ([] if both else ["agg2"]) + ["var2", "h2", "vary", "y", "x12"]
        pe = Events(m.sem("s_pe" + tag), pe_names)
        act = Events(m.sem("s_act" + tag), act_names)
        dve = Events(m.sem("s_dve" + tag), dve_names)
        LINKS = 2 * ((2 + 6) * first + 2 * (second and not both) + (6 + 6 + 1) * second)
        loads = [(wrel1[:, :], a["Wrel1T"][:, :]), (wroot1[:, :], a["Wroot1T"][:, :]),
                 (wroot2[:, :, :], a["Wroot2T"].rearrange("(k p) o -> p k o", p=P)),
                 (wrel2[:, :, :], a["Wrel2T"].rearrange("(k p) o -> p k o", p=P)),
                 (wcls[:, :, :], a["WclsT"].rearrange("(k p) o -> p k o", p=P)),
                 (w12[:, 0, :], a["W1T"][:, :]), (w12[:, 1, :], a["W2T"][:, :])]
        loads += [(vec[n][:, :], a["L0_gnn_" + n].partition_broadcast(P)) for n in vec if n != "L1b1"]
        loads += [(vec["L1b1"][:, :], a["L1_gnn_b1"].partition_broadcast(P))]

        with nc.Block() as block:
            @block.sync
            def _(s):
                for to, of in loads:
                    s.dma_start(to, of).then_inc(s_w, 16)

                def body(it):
                    for j in range(2):
                        T = it * 2 + j
                        if first and not both:
                            act.wait(s, it, "h1T", j)
                            s.dma_start(g.hT[bass.ds(T * P, P), :], hT[0][:, j, :]).then_inc(s_store[j], 16)
                            act.wait(s, it, "hr", j)
                            for q in range(KD):
                                s.dma_start(g.hq[q][bass.ds(T * P, P), 0:F], hr[:, j, q * F:(q + 1) * F]
                                            ).then_inc(s_store[j], 16)
                        if second:
                            if not both:
                                if not isinstance(it, int):
                                    pe.wait(s, it - 1, "h2", j)
                                s.dma_start(hT[0][:, j, :], g.hT[bass.ds(T * P, P), :]).then_inc(s_load[j], 16)
                                s.dma_start(agg2[:, j, :].rearrange("p (q n) -> p q n", q=KD),
                                            g.agg2[:, :, bass.ds(T * P, P)].rearrange("q p n -> p q n")
                                            ).then_inc(s_load[j], 16)
                    if second:
                        for j in range(2):
                            act.wait(s, it, "x2", j)
                            s.dma_start(g.x2[bass.ds((it * 2 + j) * P, P), :], x2[:, j, :]).then_inc(s_store[j], 16)
                turns(s, body, HALF_TILES)
                per = 16 * HALF_TILES * (1 if second else 1 + KD)
                for j in range(2):
                    s.wait_ge(s_store[j], per)

            @block.scalar
            def _(s):
                def roots(it, name, i):
                    for j in range(2):
                        dve.wait(s, it, name, j)
                        s.activation(root[:, i, j:j + 1], mv[:, i, j, 1:2], ACT.Sqrt).then_inc(act.sem, 1)

                def body(it):
                    J = range(2)
                    if first:
                        for j in J:
                            s.activation(xs[:, j, :], g.xflat[:, bass.ds((it * 2 + j) * F, F)], ACT.Copy
                                         ).then_inc(act.sem, 1)
                        for j in J:
                            pe.wait(s, it, "xT", j)
                            s.activation(xT[:, j, :], tr[j][:, 0:P], ACT.Copy).then_inc(act.sem, 1)
                        roots(it, "var1", 0)
                        for j in J:
                            pe.wait(s, it, "h1T", j)
                            if not both and not isinstance(it, int):
                                s.wait_ge(s_store[j], it * (16 * (1 + KD)))
                            s.activation(hT[0][:, j, :], tr[j][:, :], ACT.Relu).then_inc(act.sem, 1)
                        if not both:
                            for j in J:
                                dve.wait(s, it, "h1", j)
                                s.activation(hr[:, j, :], h[0][:, j, :], ACT.Relu).then_inc(act.sem, 1)
                    if second:
                        roots(it, "var2", 1)
                        for j in J:
                            pe.wait(s, it, "h2T", j)
                            s.activation(hT[1][:, j, :], tr[j][:, :], ACT.Relu).then_inc(act.sem, 1)
                        roots(it, "vary", 2)
                        for j in J:
                            pe.wait(s, it, "yT", j)
                            s.activation(yT[:, j, :], tr[j][:, 0:P], ACT.Copy).then_inc(act.sem, 1)
                        for j in J:
                            dve.wait(s, it, "x12", j)
                            if not isinstance(it, int):
                                s.wait_ge(s_store[j], it * 16)
                            s.activation(x2[:, j, :], small[j][:, F:2 * F], ACT.Copy).then_inc(act.sem, 1)
                turns(s, body, HALF_TILES)

            @block.tensor
            def _(t):
                t.wait_ge(s_w, 16 * len(loads))

                def body(it):
                    J = range(2)
                    later = not isinstance(it, int)
                    if first:
                        for j in J:
                            act.wait(t, it, "xs", j)
                            if later and not both:
                                act.wait(t, it - 1, "h1T", j)
                            t.transpose(tr[j][:, 0:P], xs[:, j, :], g.ident[:, :]).then_inc(pe.sem, 1)
                        for j in J:
                            dve.wait(t, it, "agg", j)
                            act.wait(t, it, "xT", j)
                            t.matmul(big[j][:, :], agg[:, j, :], wrel1[:, :], start=True, stop=False)
                            t.matmul(big[j][:, :], xT[:, j, :], wroot1[:, :], start=False, stop=True
                                     ).then_inc(pe.sem, 1)
                        for j in J:
                            dve.wait(t, it, "h1", j)
                            for k in range(KD):
                                ins = t.transpose(tr[j][:, k * P:(k + 1) * P], h[0][:, j, k * P:(k + 1) * P], g.ident[:, :])
                            ins.then_inc(pe.sem, 1)
                    if second:
                        for j in J:
                            if both:
                                act.wait(t, it, "h1T", j)
                            else:
                                t.wait_ge(s_load[j], 32 * (it + 1))
                                dve.wait(t, it, "agg2", j)
                            for k in range(KD):
                                ins = t.matmul(big[j][:, :], hT[0][:, j, k * P:(k + 1) * P], wroot2[:, k, :],
                                               start=k == 0, stop=both and k == KD - 1)
                            if not both:
                                for k in range(KD):
                                    ins = t.matmul(big[j][:, :], agg2[:, j, k * P:(k + 1) * P], wrel2[:, k, :],
                                                   start=False, stop=k == KD - 1)
                            ins.then_inc(pe.sem, 1)
                        for j in J:
                            dve.wait(t, it, "h2", j)
                            for k in range(KD):
                                ins = t.transpose(tr[j][:, k * P:(k + 1) * P], h[1][:, j, k * P:(k + 1) * P], g.ident[:, :])
                            ins.then_inc(pe.sem, 1)
                        for j in J:
                            act.wait(t, it, "h2T", j)
                            if later:
                                act.wait(t, it - 1, "x2", j)
                            for k in range(KD):
                                ins = t.matmul(small[j][:, 0:F], hT[1][:, j, k * P:(k + 1) * P], wcls[:, k, :],
                                               start=k == 0, stop=k == KD - 1)
                            ins.then_inc(pe.sem, 1)
                        for j in J:
                            dve.wait(t, it, "y", j)
                            t.transpose(tr[j][:, 0:P], y[:, j, :], g.ident[:, :]).then_inc(pe.sem, 1)
                        for j in J:
                            act.wait(t, it, "yT", j)
                            t.matmul(small[j][:, 0:2 * F], yT[:, j, :], w12[:, :, :].rearrange("p c f -> p (c f)"),
                                     start=True, stop=True).then_inc(pe.sem, 1)
                turns(t, body, HALF_TILES)

            @block.vector
            def _(v):
                v.wait_ge(s_w, 16 * len(loads))

                def body(it):
                    ch = Chain(v, s_chain, it, LINKS)
                    J = range(2)

                    def stats(j, i, x):
                        ch.link(v.bn_stats(st[:, i, j, :], x))
                        v.sem_inc(s_go, 1)
                        ch.link(v.bn_aggr(mv[:, i, j, :], st[:, i, j, :]))
                        v.tensor_scalar(mv[:, i, j, 1:2], mv[:, i, j, 1:2], EPS, None, ALU.add).then_inc(dve.sem, 1)

                    def norm(j, i, x, root_of):
                        act.wait(v, it, root_of, j)
                        ch.link(v.reciprocal(mv[:, i, j, 1:2], root[:, i, j:j + 1]))
                        ch.link(v.tensor_scalar(x, x, mv[:, i, j, 0:1], mv[:, i, j, 1:2], ALU.subtract, ALU.mult))

                    def affine(i, source, names, root_of):
                        for j in J:
                            pe.wait(v, it, source, j)
                            ch.link(v.tensor_tensor(h[i][:, j, :], big[j][:, :], vec[names[0]][:, :], ALU.add))
                            stats(j, i, h[i][:, j, :])
                        for j in J:
                            norm(j, i, h[i][:, j, :], root_of)
                            ch.link(v.tensor_tensor(h[i][:, j, :], h[i][:, j, :], vec[names[1]][:, :], ALU.mult))
                            v.tensor_tensor(h[i][:, j, :], h[i][:, j, :], vec[names[2]][:, :], ALU.add
                                            ).then_inc(dve.sem, 1)

                    if first:
                        for j in J:
                            part = g.acc[:, bass.ds((it * 2 + j) * P, P)]
                            ch.link(v.tensor_scalar(low[:, j, :], part, HALFBIG, None, ALU.is_lt))
                            ch.link(v.scalar_tensor_tensor(out=finite[:, j, :], in0=part, scalar=-HALFBIG,
                                                           in1=low[:, j, :], op0=ALU.is_gt, op1=ALU.mult))
                            v.tensor_tensor(agg[:, j, :], finite[:, j, :], part, ALU.mult).then_inc(dve.sem, 1)
                        affine(0, "h1", ("brel1", "g1", "b1"), "root1")
                    if second:
                        if not both:
                            for j in J:
                                v.wait_ge(s_load[j], 32 * (it + 1))
                                ch.link(v.tensor_scalar(low2[:, j, :], agg2[:, j, :], HALFBIG, None, ALU.is_lt))
                                ch.link(v.scalar_tensor_tensor(out=low2[:, j, :], in0=agg2[:, j, :], scalar=-HALFBIG,
                                                               in1=low2[:, j, :], op0=ALU.is_gt, op1=ALU.mult))
                                v.tensor_tensor(agg2[:, j, :], low2[:, j, :], agg2[:, j, :], ALU.mult
                                                ).then_inc(dve.sem, 1)
                        affine(1, "h2", ("brel2", "g2", "b2"), "root2")
                        for j in J:
                            pe.wait(v, it, "cls", j)
                            ch.link(v.tensor_tensor(y[:, j, :], small[j][:, 0:F], vec["bcls"][:, :], ALU.add))
                            ch.link(v.tensor_tensor(y[:, j, :], y[:, j, :],
                                                    g.xflat[:, bass.ds((it * 2 + j) * F, F)], ALU.add))
                            stats(j, 2, y[:, j, :])
                        for j in J:
                            norm(j, 2, y[:, j, :], "rooty")
                            v.tensor_scalar(g.xflat[:, bass.ds((it * 2 + j) * F, F)], y[:, j, :], 1.0, None, ALU.mult
                                            ).then_inc(dve.sem, 1)
                        for j in J:
                            pe.wait(v, it, "x12", j)
                            to = g.yflat[:, bass.ds((it * 2 + j) * F, F)]
                            ch.link(v.tensor_tensor(to, small[j][:, 0:F], vec["L1b1"][:, :], ALU.add))
                            v.tensor_tensor(to, to, small[j][:, F:2 * F], ALU.subtract).then_inc(dve.sem, 1)
                    ch.end()
                turns(v, body, HALF_TILES)


def general_tables(nc, g, a):
    with ExitStack() as ctx:
        m = Memory(nc, ctx)
        half = m.sb("half", [P, NTP, F])
        s_half, s_out = m.sem("s_half"), m.sem("s_gout")
        with nc.Block() as block:
            @block.vector
            def _(v):
                v.memset(half[:, :, :], 0.5).then_inc(s_half, 1)

            @block.sync
            def _(s):
                s.wait_ge(s_half, 1)
                for q in range(DH // F):
                    s.dma_start(g.hq[q][:, F:2 * F].rearrange("(t p) f -> p t f", p=P), half[:, :, :]).then_inc(s_out, 16)
                    s.dma_start(g.hq[q][0:N, 2 * F:2 * F + 1], a["node_vec"].unsqueeze(1)).then_inc(s_out, 16)
                s.wait_ge(s_out, 32 * (DH // F))


def keep_agg2(nc, g, q):
    with ExitStack() as ctx:
        s_k = Memory(nc, ctx).sem(f"s_kept_agg{q}")
        with nc.Block() as block:
            @block.sync
            def _(s):
                s.dma_start(g.agg2[q, :, :], g.acc[:, :]).then_inc(s_k, 16)
                s.wait_ge(s_k, 16)


def all_have_equal(nc, g):
    with ExitStack() as ctx:
        m = Memory(nc, ctx)
        lack = m.sb("lack", [P, NT])
        col = m.sb("lackcol", [P, 1])
        tot = m.bank("lacktot")
        s_v, s_t = m.sem("s_lv"), m.sem("s_lt")
        with nc.Block() as block:
            @block.vector
            def _(v):
                cnt = g.deg[:, :].rearrange("p (t c) -> p t c", c=2)
                v.tensor_scalar(lack[:, :], cnt[:, 0:NT, 1], 0.0, None, ALU.is_equal).then_inc(s_v, 1)
                v.wait_ge(s_v, 1)
                v.tensor_tensor(lack[:, NT - 1:NT], lack[:, NT - 1:NT], g.valid[:, 0:1], ALU.mult).then_inc(s_v, 1)
                v.wait_ge(s_v, 2)
                v.tensor_reduce(col[:, :], lack[:, :], AX.X, ALU.add).then_inc(s_v, 1)
                v.wait_ge(s_t, 1)
                v.tensor_copy(g.lack[:, :], tot[:, 0:1]).then_inc(s_v, 1)

            @block.tensor
            def _(t):
                t.wait_ge(s_v, 3)
                t.matmul(tot[:, 0:1], g.ones[:, :], col[:, :], start=True, stop=True).then_inc(s_t, 1)


def sum_pass(nc, g, tag, table, acc):
    with ExitStack() as ctx:
        m = Memory(nc, ctx)
        ring = m.sb(f"ring{tag}", [P, U, F])
        idx = m.sb(f"idx{tag}", [P, U], I32)
        hot = m.sb(f"hot{tag}", [P, NG, GS, P])
        sel = [m.bank(f"sel{tag}{i}") for i in range(2)]
        s_idx, s_go = m.sem(f"s_idx{tag}"), m.sem(f"s_go{tag}")
        s_g = [m.sem(f"s_g{tag}{i}") for i in range(NG)]
        s_hot, s_sel, s_acc = m.sem(f"s_hot{tag}"), m.sem(f"s_sel{tag}"), m.sem(f"s_acc{tag}")
        s_ini = m.sem(f"s_ini{tag}")
        with nc.Block() as block:
            @block.gpsimd
            def _(p):
                def body(it):
                    for k in range(U):
                        q = k // GS
                        if k % GS == 0:
                            if not isinstance(it, int):
                                p.wait_ge(s_sel, it * NG - NG + q + 1)
                                p.sem_inc(s_go, 1)
                            p.tensor_copy(idx[:, k:k + GS], g.src_i[:, bass.ds(it * U + k, GS)]).then_inc(s_idx, 1)
                            p.wait_ge(s_idx, it * NG + q + 1)
                            p.sem_inc(s_go, 1)
                        p.indirect_dma_start(out=ring[:, k, :], out_offset=None, in_=table,
                                             in_offset=bass.IndirectOffsetOnAxis(ap=idx[:, k:k + 1], axis=0)
                                             ).then_inc(s_g[k // GS], 16)
                turns(p, body, TURNS)

            @block.tensor
            def _(t):
                def body(it):
                    for q in range(NG):
                        G = it * NG + q
                        wait(t, s_g[q], 64 * (it + 1))
                        wait(t, s_hot, G + 1)
                        wait(t, s_acc, (G - 1) * GS)
                        for k in range(GS):
                            ins = t.matmul(sel[q % 2][:, k * P:(k + 1) * P], hot[:, q, k, :], ring[:, q * GS + k, :],
                                           start=True, stop=True)
                        ins.then_inc(s_sel, 1)
                turns(t, body, TURNS)

            @block.vector
            def _(v):
                v.memset(acc[:, :], 0.0).then_inc(s_ini, 1)
                v.wait_ge(s_ini, 1)
                regs = [v.alloc_register(f"a{tag}{j}") for j in range(GS)]

                def add(G, q):
                    v.load(regs, g.T[0:1, bass.ds(G * GS, GS)])
                    T = [v.snap(r, min_val=0, max_val=NT - 1) for r in regs]
                    wait(v, s_sel, G + 1)
                    for k in range(GS):
                        wait(v, s_acc, G * GS + k)
                        to = acc[:, bass.ds(T[k] * P, P)]
                        v.tensor_tensor(to, to, sel[q % 2][:, k * P:(k + 1) * P], ALU.add).then_inc(s_acc, 1)

                def body(it):
                    for q in range(NG):
                        G = it * NG + q
                        wait(v, s_sel, G - NG + 1)
                        v.tensor_tensor(hot[:, q, :, :], bc_mid(g.iota_n[:, :], GS),
                                        bc_last(g.drel[:, bass.ds(G * GS, GS)], P), ALU.is_equal).then_inc(s_hot, 1)
                        if not (isinstance(it, int) and q < 1):
                            add(G - 1, (q - 1) % NG)
                turns(v, body, TURNS)
                add(TURNS * NG - 1, NG - 1)


def finish1(nc, g):
    with ExitStack() as ctx:
        m = Memory(nc, ctx)
        deg, mean, var = m.sb("deg1", [P, NTP]), m.sb("mean1", [P, NTP]), m.sb("var1", [P, NTP])
        s, s_root = m.sem("s_fin1"), m.sem("s_root1")
        ready = []
        with nc.Block() as block:
            @block.vector
            def _(v):
                ch = Chain(v, s, 0, 0)
                ch.link(v.tensor_copy(deg[:, :], g.deg[:, :].rearrange("p (t c) -> p t c", c=2)[:, :, 0]))
                ch.link(v.tensor_tensor(g.y[:, :, :], g.y[:, :, :], bc_last(deg[:, :], F), ALU.mult))
                ch.link(v.tensor_tensor(g.xflat, g.xflat, g.yflat, ALU.add))
                ch.link(v.tensor_tensor(g.xflat, g.xflat, g.acc[:, :], ALU.add))
                ready.append(nodes_layernorm(v, ch, g.x[:, :, :], g.y[:, :, :], mean[:, :], var[:, :], s_root))

            root_of_variance(block, ready[0], s, var, s_root)


CHAINS = 8


def scatter_pass(nc, g):
    HP = U * P // 2
    with ExitStack() as ctx:
        m = Memory(nc, ctx)
        zero = m.sb("zero2", [P, NTP + 1, F])
        dstb = m.sb("dstb2", [P, 2, HP])
        srcb = m.sb("srcb2", [P, 2, HP])
        hotT = m.sb("hotT2", [P, 2, GS * P])
        same = m.sb("same2", [P, 2, GS, P])
        junk = m.sb("junk2", [P, GS, P])
        lower = m.sb("lower2", [P, P])
        spare = m.sb("spare2", [P, 1])
        before = m.sb("before2", [P, GS])
        far = m.sb("far2", [P, GS])
        idx_f = m.sb("idx_f2", [P, GS])
        idx = m.sb("idx2", [P, U], I32)
        val = m.sb("val2", [P, 2, GS * F])
        rows = m.sb("rows2", [P, U, F])
        vps = [m.bank(f"vps2{i}") for i in range(2)]
        sps = [m.bank(f"sps2{i}") for i in range(2)]
        s_zero, s_z = m.sem("s_zero2"), m.sem("s_z2")
        s_ini = m.sem("s_ini2")
        s_b = [m.sem(f"s_b2{i}") for i in range(2)]
        s_hot = m.sem("s_hot2")
        s_same = m.sem("s_same2")
        s_c = m.sem("s_c2")
        s_idx = m.sem("s_idx2")
        s_v = m.sem("s_v2")
        s_vc = m.sem("s_vc2")
        s_s = m.sem("s_s2")
        s_sc = m.sem("s_sc2")
        s_add = [m.sem(f"s_add2{i}") for i in range(CHAINS)]
        s_go = m.sem("s_go2")
        LK = 4
        with nc.Block() as block:
            @block.gpsimd
            def _(p):
                p.memset(zero[:, :, :], 0.0).then_inc(s_zero, 1)
                p.memset(lower[:, :], 1.0).then_inc(s_ini, 1)
                p.wait_ge(s_ini, 1)
                p.affine_select(out=lower[:, :], in_=lower[:, :], compare_op=ALU.is_gt, fill=0.0,
                                base=0, pattern=[[-1, P]], channel_multiplier=1).then_inc(s_ini, 1)
                p.wait_ge(s_z, 16 * CHAINS)

                def body(it):
                    for k in range(U):
                        if k % GS == 0:
                            p.wait_ge(s_idx, it * NG + k // GS + 1)
                            p.sem_inc(s_go, 1)
                            p.wait_ge(s_sc, it * NG + k // GS + 1)
                            p.sem_inc(s_go, 1)
                        n = it * (U // CHAINS) + k // CHAINS
                        if not (isinstance(n, int) and n == 0):
                            p.wait_ge(s_add[k % CHAINS], n * 16)
                            p.sem_inc(s_go, 1)
                        p.indirect_dma_start(out=g.sums[k % CHAINS][:, :],
                                             out_offset=bass.IndirectOffsetOnAxis(ap=idx[:, k:k + 1], axis=0),
                                             in_=rows[:, k, :], in_offset=None, compute_op=ALU.add
                                             ).then_inc(s_add[k % CHAINS], 16)
                turns(p, body, TURNS)
                for c in range(CHAINS):
                    p.wait_ge(s_add[c], 16 * (SP_ // CHAINS))

            @block.sync
            def _(s):
                s.wait_ge(s_zero, 1)
                for c in range(CHAINS):
                    s.dma_start(g.sums[c].rearrange("(t p) f -> p t f", p=P), zero[:, :, :]).then_inc(s_z, 16)

                def body(it):
                    for h in range(2):
                        if not isinstance(it, int):
                            s.wait_ge(s_same, it * NG - NG + 2 * h + 2)
                        at = bass.ds(it * (U * P) + h * HP, HP)
                        s.dma_start(dstb[:, h, :], g.drelflat[at].partition_broadcast(P)).then_inc(s_b[h], 16)
                        s.dma_start(srcb[:, h, :], g.srcflat[at].partition_broadcast(P)).then_inc(s_b[h], 16)
                turns(s, body, TURNS)

            @block.scalar
            def _(s):
                def sums(G, q):
                    wait(s, s_s, G + 1)
                    s.activation(rows[:, q * GS:(q + 1) * GS, :].rearrange("p k f -> p (k f)"), sps[q % 2][:, :],
                                 ACT.Copy).then_inc(s_sc, 1)

                def body(it):
                    for q in range(NG):
                        G = it * NG + q
                        wait(s, s_v, G + 1)
                        wait(s, s_s, G - 1)
                        s.activation(val[:, q % 2, :], vps[q % 2][:, :], ACT.Copy).then_inc(s_vc, 1)
                        if not (isinstance(it, int) and q < 1):
                            sums(G - 1, (q - 1) % NG)
                turns(s, body, TURNS)
                sums(TURNS * NG - 1, NG - 1)

            @block.tensor
            def _(t):
                regs = [t.alloc_register(f"v2{j}") for j in range(GS)]

                def sums(G, q):
                    wait(t, s_vc, G + 1)
                    wait(t, s_same, G + 1)
                    wait(t, s_sc, G - 1)
                    for k in range(GS):
                        ins = t.matmul(sps[q % 2][:, k * F:(k + 1) * F], same[:, q % 2, k, :],
                                       val[:, q % 2, k * F:(k + 1) * F], start=True, stop=True)
                    ins.then_inc(s_s, 1)

                def body(it):
                    for q in range(NG):
                        G = it * NG + q
                        t.load(regs, g.T[0:1, bass.ds(G * GS, GS)])
                        T = [t.snap(r, min_val=0, max_val=NT - 1) for r in regs]
                        wait(t, s_hot, G + 1)
                        wait(t, s_vc, G - 1)
                        for k in range(GS):
                            ins = t.matmul(vps[q % 2][:, k * F:(k + 1) * F], hotT[:, q % 2, k * P:(k + 1) * P],
                                           g.xflat[:, bass.ds(T[k] * F, F)], start=True, stop=True)
                        ins.then_inc(s_v, 1)
                        if not (isinstance(it, int) and q < 1):
                            sums(G - 1, (q - 1) % NG)
                turns(t, body, TURNS)
                sums(TURNS * NG - 1, NG - 1)

            @block.vector
            def _(v):
                v.wait_ge(s_ini, 2)
                v.tensor_scalar(spare[:, :], g.iota_p[:, :], float(NP), None, ALU.add).then_inc(s_ini, 1)
                v.wait_ge(s_ini, 3)

                def body(it):
                    for q in range(NG):
                        G = it * NG + q
                        h, off = q // 2, (q % 2) * GS * P
                        srcs = g.src_f[:, bass.ds(G * GS, GS)]
                        if q % 2 == 0:
                            v.wait_ge(s_b[h], 32 * (it + 1))
                        wait(v, s_v, G - 1)
                        v.tensor_scalar(hotT[:, q % 2, :], dstb[:, h, off:off + GS * P], g.iota_p[:, :], None,
                                        ALU.is_equal).then_inc(s_hot, 1)
                        for k in range(GS):
                            ins = v.scalar_tensor_tensor(
                                out=junk[:, k, :], in0=srcb[:, h, off + k * P:off + (k + 1) * P],
                                scalar=g.src_f[:, bass.ds(G * GS + k, 1)], in1=lower[:, :],
                                op0=ALU.is_equal, op1=ALU.mult, accum_out=before[:, k:k + 1])
                        ins.then_inc(s_c, 1)
                        wait(v, s_s, G - 1)
                        if not isinstance(it, int):
                            for c in range(GS):
                                k = q * GS + c
                                v.wait_ge(s_add[k % CHAINS], (it - 1) * 32 + (k // CHAINS + 1) * 16)
                        v.tensor_tensor(same[:, q % 2, :, :],
                                        srcb[:, h, off:off + GS * P].rearrange("p (k e) -> p k e", k=GS),
                                        bc_last(srcs, P), ALU.is_equal).then_inc(s_same, 1)
                        v.tensor_scalar(far[:, :], srcs, spare[:, :], -1.0, ALU.subtract, ALU.mult).then_inc(s_c, 1)
                        v.wait_ge(s_c, G * LK + 2)
                        v.scalar_tensor_tensor(out=idx_f[:, :], in0=before[:, :], scalar=1.0, in1=far[:, :],
                                               op0=ALU.min, op1=ALU.mult).then_inc(s_c, 1)
                        v.wait_ge(s_c, G * LK + 3)
                        v.tensor_tensor(idx_f[:, :], idx_f[:, :], srcs, ALU.add).then_inc(s_c, 1)
                        v.wait_ge(s_c, G * LK + 4)
                        v.tensor_copy(idx[:, q * GS:(q + 1) * GS], idx_f[:, :]).then_inc(s_idx, 1)
                turns(v, body, TURNS)


def finish2(nc, g):
    with ExitStack() as ctx:
        m = Memory(nc, ctx)
        part = [m.sb(f"part{i}", [P, NTP, F]) for i in range(2)]
        mean, var = m.sb("mean2", [P, NTP]), m.sb("var2", [P, NTP])
        ready, s_root = [], m.sem("s_root2")
        s, s_ld = m.sem("s_fin2"), [m.sem(f"s_ld2{i}") for i in range(2)]
        with nc.Block() as block:
            @block.sync
            def _(y):
                for c in range(CHAINS):
                    wait(y, s, c - 1)
                    y.dma_start(part[c % 2][:, :, :], g.sums[c][0:NP, :].rearrange("(t p) f -> p t f", p=P)
                                ).then_inc(s_ld[c % 2], 16)

            @block.vector
            def _(v):
                ch = Chain(v, s, 0, 0)
                for c in range(CHAINS):
                    v.wait_ge(s_ld[c % 2], 16 * (c // 2 + 1))
                    ch.link(v.tensor_tensor(g.x[:, :, :], g.x[:, :, :], part[c % 2][:, :, :], ALU.add))
                ready.append(nodes_layernorm(v, ch, g.x[:, :, :], part[0][:, :, :], mean[:, :], var[:, :], s_root))

            root_of_variance(block, ready[0], s, var, s_root)


def layer3_nodes(nc, g, a):
    with ExitStack() as ctx:
        m = Memory(nc, ctx)
        wlr = m.sb("wlr", [P, 2, F])
        bias = m.sb("bias_lr", [P, 2, F])
        xs, xT = m.sb("xs3", [P, 2, F]), m.sb("xT3", [P, 2, P])
        xl = m.sb("xl3", [P, 2, F])
        tr = [m.bank(f"tr3{j}") for j in range(2)]
        lr = [m.bank(f"lr3{j}") for j in range(2)]
        s_w = m.sem("s_w3")
        s_store = [m.sem(f"s_store3{j}") for j in range(2)]
        pe = Events(m.sem("s_pe3"), ["xT", "lr"])
        act = Events(m.sem("s_act3"), ["xs", "xT"])
        dve = Events(m.sem("s_dve3"), ["xl", "xr"])
        with nc.Block() as block:
            @block.sync
            def _(s):
                for c, (w, b) in enumerate((("L3_gnn_Wl", "L3_gnn_bl"), ("L3_gnn_Wr", "L3_gnn_br"))):
                    s.dma_start(wlr[:, c, :], a[w][:, :]).then_inc(s_w, 16)
                    s.dma_start(bias[:, c, :], a[b].partition_broadcast(P)).then_inc(s_w, 16)

                def body(it):
                    for j in range(2):
                        dve.wait(s, it, "xl", j)
                        s.dma_start(g.xl_rows[bass.ds((it * 2 + j) * P, P), :], xl[:, j, :]).then_inc(s_store[j], 16)
                turns(s, body, HALF_TILES)
                for j in range(2):
                    s.wait_ge(s_store[j], 16 * HALF_TILES)

            @block.scalar
            def _(s):
                def body(it):
                    for j in range(2):
                        if not isinstance(it, int):
                            pe.wait(s, it - 1, "xT", j)
                        s.activation(xs[:, j, :], g.xflat[:, bass.ds((it * 2 + j) * F, F)], ACT.Copy).then_inc(act.sem, 1)
                    for j in range(2):
                        pe.wait(s, it, "xT", j)
                        s.activation(xT[:, j, :], tr[j][:, 0:P], ACT.Copy).then_inc(act.sem, 1)
                turns(s, body, HALF_TILES)

            @block.tensor
            def _(t):
                t.wait_ge(s_w, 64)

                def body(it):
                    for j in range(2):
                        act.wait(t, it, "xs", j)
                        t.transpose(tr[j][:, 0:P], xs[:, j, :], g.ident[:, :]).then_inc(pe.sem, 1)
                    for j in range(2):
                        act.wait(t, it, "xT", j)
                        if not isinstance(it, int):
                            dve.wait(t, it - 1, "xr", j)
                        t.matmul(lr[j][:, 0:2 * F], xT[:, j, :], wlr[:, :, :].rearrange("p c f -> p (c f)"),
                                 start=True, stop=True).then_inc(pe.sem, 1)
                turns(t, body, HALF_TILES)

            @block.vector
            def _(v):
                v.wait_ge(s_w, 64)

                def body(it):
                    for j in range(2):
                        pe.wait(v, it, "lr", j)
                        if not isinstance(it, int):
                            v.wait_ge(s_store[j], it * 16)
                        v.tensor_tensor(xl[:, j, :], lr[j][:, 0:F], bias[:, 0, :], ALU.add).then_inc(dve.sem, 1)
                    for j in range(2):
                        v.tensor_tensor(g.xrflat[:, bass.ds((it * 2 + j) * F, F)], lr[j][:, F:2 * F], bias[:, 1, :],
                                        ALU.add).then_inc(dve.sem, 1)
                turns(v, body, HALF_TILES)


def score_pass(nc, g, a):
    HP = U * P // 2
    GH = GS * HEADS
    with ExitStack() as ctx:
        m = Memory(nc, ctx)
        ring = m.sb("ring3", [P, U, F])
        idx = m.sb("idx3", [P, U], I32)
        dstb = m.sb("dstb3", [P, 2, HP])
        reset = m.sb("reset3", [HEADS, 2, HP])
        ea = m.sb("ea3", [P, NG, GS, DE])
        eaT = m.sb("eaT3", [DE, NG, GS, P])
        hot = m.sb("hot3", [P, 2, GS, P])
        hotT = m.sb("hotT3", [P, 2, GS * P])
        fifth = m.sb("fifth3", [P, 2, GS * F])
        leaky = m.sb("leaky3", [P, GS * F])
        weighted = m.sb("weighted3", [P, 2, GS * F])
        sc = m.sb("sc3", [P, 2, GH])
        run = m.sb("run3", [HEADS, 2, GS * P])
        ends = m.sb("ends3", [P, 2, GS, HEADS])
        zps = [m.bank(f"zps3{i}") for i in range(2)]
        eps = [m.bank(f"eps3{i}") for i in range(2)]
        scT, back, top = m.bank("scT3"), m.bank("back3"), [m.bank(f"top3{i}") for i in range(2)]
        s_ini = m.sem("s_ini3")
        s_idx, s_go = m.sem("s_idx3"), m.sem("s_go3")
        s_g = [m.sem(f"s_g3{i}") for i in range(NG)]
        s_b = [m.sem(f"s_b3{i}") for i in range(2)]
        s_ea = [m.sem(f"s_ea3{i}") for i in range(NG)]
        s_rows = [m.sem(f"s_rows3{i}") for i in range(NG)]
        s_hot = m.sem("s_hot3")
        s_z = m.sem("s_z3")
        s_lk = m.sem("s_lk3")
        s_lz = m.sem("s_lz3")
        s_w = m.sem("s_wt3")
        s_sc = m.sem("s_sc3")
        s_keep = m.sem("s_keep3")
        s_scT = m.sem("s_scT3")
        s_run = m.sem("s_run3")
        s_back = m.sem("s_back3")
        s_end = m.sem("s_end3")
        s_top = m.sem("s_top3")
        s_esum = m.sem("s_esum3")
        s_max = m.sem("s_max3")

        with nc.Block() as block:
            @block.gpsimd
            def _(p):
                def body(it):
                    for k in range(U):
                        q = k // GS
                        if k % GS == 0:
                            if not isinstance(it, int):
                                p.wait_ge(s_z, it * NG - NG + q + 1)
                                p.sem_inc(s_go, 1)
                                p.wait_ge(s_rows[q], it * 16)
                                p.sem_inc(s_go, 1)
                            p.tensor_copy(idx[:, k:k + GS], g.src_i[:, bass.ds(it * U + k, GS)]).then_inc(s_idx, 1)
                            p.wait_ge(s_idx, it * NG + q + 1)
                            p.sem_inc(s_go, 1)
                        p.indirect_dma_start(out=ring[:, k, :], out_offset=None, in_=g.xl_rows[0:N, :],
                                             in_offset=bass.IndirectOffsetOnAxis(ap=idx[:, k:k + 1], axis=0)
                                             ).then_inc(s_g[q], 16)
                turns(p, body, TURNS)

            @block.sync
            def _(s):
                regs = [s.alloc_register(f"t3{j}") for j in range(GS)]

                def keep(it, q):
                    s.wait_ge(s_g[q], 64 * (it + 1))
                    s.dma_start(g.rows[bass.ds((it * NG + q) * GS, GS), :, :].rearrange("k e f -> e k f"),
                                ring[:, q * GS:(q + 1) * GS, :]).then_inc(s_rows[q], 16)

                def body(it):
                    first = isinstance(it, int)
                    for q in range(NG):
                        G = it * NG + q
                        h = q // 2
                        if q % 2 == 0:
                            if not first:
                                s.wait_ge(s_hot, it * NG - NG + 2 * h + 2)
                                s.wait_ge(s_run, it * NG - NG + 2 * h + 2)
                            at = bass.ds(it * (U * P) + h * HP, HP)
                            s.dma_start(dstb[:, h, :], g.drelflat[at].partition_broadcast(P)).then_inc(s_b[h], 16)
                            s.dma_start(reset[:, h, :], g.d0flat[at].partition_broadcast(HEADS)).then_inc(s_b[h], 16)
                        s.load(regs, g.t[0:1, bass.ds(G * GS, GS)])
                        t = [s.snap(r, min_val=0, max_val=ET - 1) for r in regs]
                        if not first:
                            s.wait_ge(s_z, it * NG - NG + q + 1)
                        for k in range(GS):
                            s.dma_start(ea[:, q, k, :], a["ea"][bass.ds(t[k] * P, P), :]).then_inc(s_ea[q], 16)
                            s.dma_start(eaT[:, q, k, :], a["eaT"][:, bass.ds(t[k] * P, P)]).then_inc(s_ea[q], 16)
                        if not (first and q < 1):
                            keep(it if q else it - 1, (q - 1) % NG)
                turns(s, body, TURNS)
                keep(TURNS - 1, NG - 1)
                for q in range(NG):
                    s.wait_ge(s_rows[q], 16 * TURNS)

            @block.scalar
            def _(s):
                def body(it):
                    for q in range(NG):
                        G = it * NG + q
                        wait(s, s_z, G + 1)
                        wait(s, s_w, G - 1)
                        s.activation(fifth[:, q % 2, :], zps[q % 2][:, :], ACT.Copy, scale=0.2).then_inc(s_lk, 1)
                        wait(s, s_sc, G + 1)
                        s.activation(g.score[:, bass.ds(G * GH, GH)], sc[:, q % 2, :], ACT.Copy).then_inc(s_keep, 1)
                turns(s, body, TURNS)

            @block.tensor
            def _(t):
                regs = [t.alloc_register(f"v3{j}") for j in range(GS)]

                def transposed(G, q):
                    wait(t, s_sc, G + 1)
                    wait(t, s_run, G)
                    for k in range(GS):
                        ins = t.transpose(scT[0:HEADS, k * P:(k + 1) * P], sc[:, q % 2, k * HEADS:(k + 1) * HEADS],
                                          g.ident[:, :])
                    ins.then_inc(s_scT, 1)

                def backward(G, q):
                    wait(t, s_run, G + 1)
                    wait(t, s_end, G)
                    t.sem_inc(s_go, 1)
                    for k in range(GS):
                        ins = t.transpose(back[:, k * HEADS:(k + 1) * HEADS], run[:, q % 2, k * P:(k + 1) * P],
                                          g.ident[0:HEADS, 0:HEADS])
                    ins.then_inc(s_back, 1)

                def place(G, q):
                    wait(t, s_end, G + 1)
                    wait(t, s_max, (G - 1) * GS)
                    for k in range(GS):
                        ins = t.matmul(top[q % 2][:, k * HEADS:(k + 1) * HEADS], g.hot3[:, q, k, :], ends[:, q % 2, k, :],
                                       start=True, stop=True)
                    ins.then_inc(s_top, 1)

                def body(it):
                    first = isinstance(it, int)
                    for q in range(NG):
                        G = it * NG + q
                        t.load(regs, g.T[0:1, bass.ds(G * GS, GS)])
                        T = [t.snap(r, min_val=0, max_val=NT - 1) for r in regs]
                        wait(t, s_hot, G + 1)
                        t.wait_ge(s_g[q], 64 * (it + 1))
                        t.wait_ge(s_ea[q], 128 * (it + 1))
                        wait(t, s_lz, G - 1)
                        wait(t, s_esum, (G - 1) * GS)
                        for k in range(GS):
                            z = zps[q % 2][:, k * F:(k + 1) * F]
                            t.matmul(z, hotT[:, q % 2, k * P:(k + 1) * P], g.xrflat[:, bass.ds(T[k] * F, F)],
                                     start=True, stop=False)
                            t.matmul(z, eaT[:, q, k, :], g.We[:, :], start=False, stop=False)
                            t.matmul(z, g.ident[:, :], ring[:, q * GS + k, :], start=False, stop=True)
                            ins = t.matmul(eps[q % 2][:, k * DE:(k + 1) * DE], g.hot3[:, q, k, :], ea[:, q, k, :],
                                           start=True, stop=True)
                        ins.then_inc(s_z, 1)
                        if not (first and q < 1):
                            transposed(G - 1, (q - 1) % NG)
                        if not (first and q < 2):
                            backward(G - 2, (q - 2) % NG)
                        if not (first and q < 3):
                            place(G - 3, (q - 3) % NG)
                turns(t, body, TURNS)
                GL = TURNS * NG
                transposed(GL - 1, NG - 1)
                backward(GL - 2, NG - 2)
                backward(GL - 1, NG - 1)
                for b in (3, 2, 1):
                    place(GL - b, NG - b)

            @block.vector
            def _(v):
                v.memset(g.easum[:, :], 0.0).then_inc(s_ini, 1)
                v.memset(g.smax[:, :], 0.0).then_inc(s_ini, 1)
                v.memset(run[:, :, :], -BIG).then_inc(s_ini, 1)
                v.wait_ge(s_ini, 3)
                regs = [v.alloc_register(f"a3{j}") for j in range(GS)]

                def tiles_of(G):
                    v.load(regs, g.T[0:1, bass.ds(G * GS, GS)])
                    return [v.snap(r, min_val=0, max_val=NT - 1) for r in regs]

                def scores(G, q):
                    wait(v, s_lk, G + 1)
                    v.tensor_tensor(leaky[:, :], zps[q % 2][:, :], fifth[:, q % 2, :], ALU.max).then_inc(s_lz, 1)
                    wait(v, s_lz, G + 1)
                    v.tensor_tensor(weighted[:, q % 2, :].rearrange("p (k f) -> p k f", k=GS),
                                    leaky[:, :].rearrange("p (k f) -> p k f", k=GS), bc_mid(g.att[:, :], GS),
                                    ALU.mult).then_inc(s_w, 1)
                    wait(v, s_w, G + 1)
                    wait(v, s_keep, G - 1)
                    wait(v, s_scT, G - 1)
                    v.tensor_reduce(sc[:, q % 2, :], weighted[:, q % 2, :].rearrange("p (k c) -> p k c", c=C), AX.X,
                                    ALU.add).then_inc(s_sc, 1)
                    T = tiles_of(G)
                    for k in range(GS):
                        wait(v, s_esum, G * GS + k)
                        to = g.easum[:, bass.ds(T[k] * DE, DE)]
                        v.tensor_tensor(to, to, eps[q % 2][:, k * DE:(k + 1) * DE], ALU.add).then_inc(s_esum, 1)

                def scan(G, q):
                    wait(v, s_scT, G + 1)
                    wait(v, s_run, G)
                    wait(v, s_back, G - 1)
                    v.tensor_tensor_scan(run[:, q % 2, :], reset[:, q // 2, (q % 2) * GS * P:(q % 2 + 1) * GS * P],
                                         scT[0:HEADS, :], run[:, (q + 1) % 2, GS * P - 1:GS * P],
                                         ALU.min, ALU.max).then_inc(s_run, 1)

                def ends_of(G, q):
                    wait(v, s_back, G + 1)
                    wait(v, s_top, G - 1)
                    v.tensor_tensor(ends[:, q % 2, :, :], back[:, 0:GH].rearrange("p (k h) -> p k h", k=GS),
                                    bc_last(g.endf[:, bass.ds(G * GS, GS)], HEADS), ALU.mult).then_inc(s_end, 1)

                def add(G, q):
                    T = tiles_of(G)
                    wait(v, s_top, G + 1)
                    for k in range(GS):
                        wait(v, s_max, G * GS + k)
                        to = g.smax[:, bass.ds(T[k] * HEADS, HEADS)]
                        v.tensor_tensor(to, to, top[q % 2][:, k * HEADS:(k + 1) * HEADS], ALU.add).then_inc(s_max, 1)

                def body(it):
                    first = isinstance(it, int)
                    for q in range(NG):
                        G = it * NG + q
                        h, off = q // 2, (q % 2) * GS * P
                        if not first:
                            v.wait_ge(s_top, it * NG - NG + q + 1)
                        v.tensor_tensor(g.hot3[:, q, :, :], bc_mid(g.iota_n[:, :], GS),
                                        bc_last(g.drel[:, bass.ds(G * GS, GS)], P), ALU.is_equal)
                        if q % 2 == 0:
                            v.wait_ge(s_b[h], 32 * (it + 1))
                        wait(v, s_z, G - 1)
                        v.tensor_scalar(hotT[:, q % 2, :], dstb[:, h, off:off + GS * P], g.iota_p[:, :], None,
                                        ALU.is_equal).then_inc(s_hot, 1)
                        if not (first and q < 1):
                            scores(G - 1, (q - 1) % NG)
                        if not (first and q < 2):
                            scan(G - 2, (q - 2) % NG)
                        if not (first and q < 3):
                            ends_of(G - 3, (q - 3) % NG)
                        if not (first and q < 4):
                            add(G - 4, q)
                turns(v, body, TURNS)
                GL = TURNS * NG
                scores(GL - 1, NG - 1)
                scan(GL - 2, NG - 2)
                scan(GL - 1, NG - 1)
                for b in (3, 2, 1):
                    ends_of(GL - b, NG - b)
                for b in (4, 3, 2, 1):
                    add(GL - b, NG - b)


def self_loops(nc, g, a):
    with ExitStack() as ctx:
        m = Memory(nc, ctx)
        rdeg, none = m.sb("rdeg", [P, NTP]), m.sb("none", [P, NTP])
        ls, lT = m.sb("ls", [P, 2, DE]), m.sb("lT", [DE, 2, P])
        xl = m.sb("xln", [P, NTP, F])
        z, z2 = m.sb("zn", [P, NTP, F]), m.sb("zn2", [P, NTP, F])
        zf = z[:, :, :].rearrange("p t f -> p (t f)")
        sl = m.sb("sl", [P, NTP * HEADS])
        tr = [m.bank(f"trl{j}") for j in range(2)]
        zp = [m.bank(f"zl{j}") for j in range(2)]
        s_c, s_x, s_e = m.sem("s_cl"), m.sem("s_xln"), m.sem("s_el")
        pe = Events(m.sem("s_pel"), ["lT", "z"])
        act = Events(m.sem("s_actl"), ["ls", "lT", "z"])
        LINKS = 12
        s_go = m.sem("s_gol")
        with nc.Block() as block:
            @block.sync
            def _(s):
                s.dma_start(xl[:, :, :], g.xl_rows.rearrange("(t p) f -> p t f", p=P)).then_inc(s_x, 16)

            @block.scalar
            def _(s):
                s.wait_ge(s_c, 4)

                def body(it):
                    J = range(2)
                    for j in J:
                        s.activation(ls[:, j, :], g.easum[:, bass.ds((it * 2 + j) * DE, DE)], ACT.Copy).then_inc(act.sem, 1)
                    for j in J:
                        pe.wait(s, it, "lT", j)
                        s.activation(lT[:, j, :], tr[j][0:DE, 0:P], ACT.Copy).then_inc(act.sem, 1)
                    for j in J:
                        pe.wait(s, it, "z", j)
                        s.activation(zf[:, bass.ds((it * 2 + j) * F, F)], zp[j][:, 0:F], ACT.Copy).then_inc(act.sem, 1)
                turns(s, body, HALF_TILES)
                s.wait_ge(s_c, LINKS)
                s.activation(g.eloop[:, :], sl[:, :], ACT.Exp).then_inc(s_e, 1)

            @block.tensor
            def _(t):
                def body(it):
                    J = range(2)
                    for j in J:
                        act.wait(t, it, "ls", j)
                        t.sem_inc(s_go, 1)
                        t.transpose(tr[j][0:DE, 0:P], ls[:, j, :], g.ident[:, :]).then_inc(pe.sem, 1)
                    for j in J:
                        act.wait(t, it, "lT", j)
                        t.matmul(zp[j][:, 0:F], lT[:, j, :], g.We[:, :], start=True, stop=True).then_inc(pe.sem, 1)
                turns(t, body, HALF_TILES)

            @block.vector
            def _(v):
                ch = Chain(v, s_c, 0, 0)
                deg = g.deg[:, :].rearrange("p (t c) -> p t c", c=2)[:, :, 0]
                ch.link(v.tensor_scalar(rdeg[:, :], deg, 1.0, None, ALU.max))
                ch.link(v.reciprocal(rdeg[:, :], rdeg[:, :]))
                ch.link(v.tensor_scalar(none[:, :], deg, 0.0, -BIG, ALU.is_equal, ALU.mult))
                es = g.easum[:, :].rearrange("p (t d) -> p t d", d=DE)
                ch.link(v.tensor_tensor(es, es, bc_last(rdeg[:, :], DE), ALU.mult))
                sm = g.smax[:, :].rearrange("p (t h) -> p t h", h=HEADS)
                ch.link(v.tensor_tensor(sm, sm, bc_last(none[:, :], HEADS), ALU.add))
                act.wait(v, HALF_TILES - 1, "z", 1)
                v.wait_ge(s_x, 16)
                ch.link(v.tensor_tensor(z[:, :, :], z[:, :, :], xl[:, :, :], ALU.add))
                ch.link(v.tensor_tensor(zf, zf, g.xrflat, ALU.add))
                ch.link(v.scalar_tensor_tensor(out=z2[:, :, :], in0=z[:, :, :], scalar=0.2, in1=z[:, :, :],
                                               op0=ALU.mult, op1=ALU.max))
                ch.link(v.tensor_tensor(z2[:, :, :], z2[:, :, :], bc_mid(g.att[:, :], NTP), ALU.mult))
                ch.link(v.tensor_reduce(sl[:, :], z2[:, :, :].rearrange("p t (h c) -> p (t h) c", c=C), AX.X, ALU.add))
                ch.link(v.tensor_tensor(g.smax[:, :], g.smax[:, :], sl[:, :], ALU.max))
                ch.link(v.tensor_tensor(sl[:, :], sl[:, :], g.smax[:, :], ALU.subtract))
                assert ch.n == LINKS
                v.wait_ge(s_e, 1)


def weighted_pass(nc, g):
    HP = U * P // 2
    GH = GS * HEADS
    with ExitStack() as ctx:
        m = Memory(nc, ctx)
        rows = m.sb("rows4", [P, NG, GS * F])
        dstb = m.sb("dstb4", [P, 2, HP])
        hot = m.sb("hot4", [P, NG, GS, P])
        hotT = m.sb("hotT4", [P, 2, GS * P])
        under = m.sb("under4", [P, 2, GH])
        ex = m.sb("ex4", [P, 2, GH])
        val = m.sb("val4", [P, 2, GS * F])
        mps = [m.bank(f"mps4{i}") for i in range(2)]
        ops = [m.bank(f"ops4{i}") for i in range(2)]
        dps = [m.bank(f"dps4{i}") for i in range(2)]
        s_ini = m.sem("s_ini4")
        s_b = [m.sem(f"s_b4{i}") for i in range(2)]
        s_r = [m.sem(f"s_r4{i}") for i in range(NG)]
        s_hot = m.sem("s_hot4")
        s_m = m.sem("s_m4")
        s_u = m.sem("s_u4")
        s_ex = m.sem("s_ex4")
        s_val = m.sem("s_val4")
        s_o = m.sem("s_o4")
        s_out = m.sem("s_out4")
        s_den = m.sem("s_den4")
        with nc.Block() as block:
            @block.sync
            def _(s):
                def body(it):
                    for q in range(NG):
                        if q % 2 == 0:
                            h = q // 2
                            if not isinstance(it, int):
                                s.wait_ge(s_hot, it * NG - NG + 2 * h + 2)
                            s.dma_start(dstb[:, h, :], g.drelflat[bass.ds(it * (U * P) + h * HP, HP)].partition_broadcast(P)
                                        ).then_inc(s_b[h], 16)
                        if not isinstance(it, int):
                            s.wait_ge(s_val, it * NG - NG + q + 1)
                        s.dma_start(rows[:, q, :].rearrange("p (k f) -> p k f", k=GS),
                                    g.rows[bass.ds((it * NG + q) * GS, GS), :, :].rearrange("k e f -> e k f")
                                    ).then_inc(s_r[q], 16)
                turns(s, body, TURNS)

            @block.scalar
            def _(s):
                def body(it):
                    for q in range(NG):
                        G = it * NG + q
                        wait(s, s_u, 2 * (G + 1))
                        wait(s, s_o, G - 1)
                        s.activation(ex[:, q % 2, :], under[:, q % 2, :], ACT.Exp).then_inc(s_ex, 1)
                turns(s, body, TURNS)

            @block.tensor
            def _(t):
                regs = [t.alloc_register(f"v4{j}") for j in range(GS)]

                def sums(G, q):
                    wait(t, s_val, G + 1)
                    wait(t, s_den, (G - 1) * GS)
                    for k in range(GS):
                        t.matmul(ops[q % 2][:, k * F:(k + 1) * F], hot[:, q, k, :], val[:, q % 2, k * F:(k + 1) * F],
                                 start=True, stop=True)
                        ins = t.matmul(dps[q % 2][:, k * HEADS:(k + 1) * HEADS], hot[:, q, k, :],
                                       ex[:, q % 2, k * HEADS:(k + 1) * HEADS], start=True, stop=True)
                    ins.then_inc(s_o, 1)

                def body(it):
                    for q in range(NG):
                        G = it * NG + q
                        t.load(regs, g.T[0:1, bass.ds(G * GS, GS)])
                        T = [t.snap(r, min_val=0, max_val=NT - 1) for r in regs]
                        wait(t, s_hot, G + 1)
                        wait(t, s_u, 2 * (G - 1))
                        for k in range(GS):
                            ins = t.matmul(mps[q % 2][:, k * HEADS:(k + 1) * HEADS], hotT[:, q % 2, k * P:(k + 1) * P],
                                           g.smax[:, bass.ds(T[k] * HEADS, HEADS)], start=True, stop=True)
                        ins.then_inc(s_m, 1)
                        if not (isinstance(it, int) and q < 1):
                            sums(G - 1, (q - 1) % NG)
                turns(t, body, TURNS)
                sums(TURNS * NG - 1, NG - 1)

            @block.vector
            def _(v):
                v.memset(g.out[:, :], 0.0).then_inc(s_ini, 1)
                v.memset(g.den[:, :], 0.0).then_inc(s_ini, 1)
                v.wait_ge(s_ini, 2)
                regs = [v.alloc_register(f"a4{j}") for j in range(GS)]

                def values(G, q, it_q):
                    wait(v, s_ex, G + 1)
                    v.wait_ge(s_r[q], 16 * (it_q + 1))
                    wait(v, s_o, G - 1)
                    v.tensor_tensor(val[:, q % 2, :].rearrange("p (h c) -> p h c", c=C),
                                    rows[:, q, :].rearrange("p (h c) -> p h c", c=C), bc_last(ex[:, q % 2, :], C),
                                    ALU.mult).then_inc(s_val, 1)

                def add(G, q):
                    v.load(regs, g.T[0:1, bass.ds(G * GS, GS)])
                    T = [v.snap(r, min_val=0, max_val=NT - 1) for r in regs]
                    wait(v, s_o, G + 1)
                    for k in range(GS):
                        wait(v, s_out, G * GS + k)
                        to = g.out[:, bass.ds(T[k] * F, F)]
                        v.tensor_tensor(to, to, ops[q % 2][:, k * F:(k + 1) * F], ALU.add).then_inc(s_out, 1)
                    for k in range(GS):
                        wait(v, s_den, G * GS + k)
                        to = g.den[:, bass.ds(T[k] * HEADS, HEADS)]
                        v.tensor_tensor(to, to, dps[q % 2][:, k * HEADS:(k + 1) * HEADS], ALU.add).then_inc(s_den, 1)

                def body(it):
                    first = isinstance(it, int)
                    for q in range(NG):
                        G = it * NG + q
                        h, off = q // 2, (q % 2) * GS * P
                        if not first:
                            v.wait_ge(s_o, it * NG - NG + q + 1)
                        v.tensor_tensor(hot[:, q, :, :], bc_mid(g.iota_n[:, :], GS),
                                        bc_last(g.drel[:, bass.ds(G * GS, GS)], P), ALU.is_equal)
                        if q % 2 == 0:
                            v.wait_ge(s_b[h], 16 * (it + 1))
                        wait(v, s_m, G - 1)
                        v.tensor_scalar(hotT[:, q % 2, :], dstb[:, h, off:off + GS * P], g.iota_p[:, :], None,
                                        ALU.is_equal).then_inc(s_hot, 1)
                        if not (first and q < 1):
                            values(G - 1, (q - 1) % NG, it if q else it - 1)
                        wait(v, s_m, G + 1)
                        wait(v, s_ex, G - 1)
                        v.tensor_tensor(under[:, q % 2, :], g.score[:, bass.ds(G * GH, GH)], mps[q % 2][:, 0:GH],
                                        ALU.subtract).then_inc(s_u, 1)
                        v.wait_ge(s_u, 2 * G + 1)
                        v.tensor_scalar(under[:, q % 2, :], under[:, q % 2, :], 0.0, None, ALU.min).then_inc(s_u, 1)
                        if not (first and q < 2):
                            add(G - 2, (q - 2) % NG)
                turns(v, body, TURNS)
                GL = TURNS * NG
                values(GL - 1, NG - 1, TURNS - 1)
                add(GL - 2, NG - 2)
                add(GL - 1, NG - 1)


def finish3(nc, g, a):
    with ExitStack() as ctx:
        m = Memory(nc, ctx)
        names = ("bias_out", "gn_weight", "gn_bias", "gn_mean_scale")
        vec = {n: m.sb("v" + n, [P, F]) for n in names}
        xl = m.sb("xl5", [P, NTP, F])
        sq = m.sb("sq5", [P, NTP, F])
        sqf = sq[:, :, :].rearrange("p t f -> p (t f)")
        mean, scale = m.sb("gmean", [P, F]), m.sb("gscale", [P, F])
        rmean, var = m.sb("rmean", [P, NTP]), m.sb("rvar", [P, NTP])
        mp, vp = m.bank("mp5"), m.bank("vp5")
        s, s_w, s_root, s_sum, s_groot = m.sem("s5"), m.sem("s_w5"), m.sem("s_root5"), m.sem("s_sum5"), m.sem("s_gr5")
        ready = []
        with nc.Block() as block:
            @block.sync
            def _(e):
                e.dma_start(xl[:, :, :], g.xl_rows.rearrange("(t p) f -> p t f", p=P)).then_inc(s_w, 16)
                for n in names:
                    e.dma_start(vec[n][:, :], a["L3_gnn_" + n].partition_broadcast(P)).then_inc(s_w, 16)

            @block.vector
            def _(v):
                ch = Chain(v, s, 0, 0)
                out3 = g.out[:, :].rearrange("p (t f) -> p t f", f=F)
                outh = g.out[:, :].rearrange("p (h c) -> p h c", c=C)
                v.wait_ge(s_w, 16 * 5)
                ch.link(v.tensor_tensor(sqf.rearrange("p (h c) -> p h c", c=C),
                                        xl[:, :, :].rearrange("p t (h c) -> p (t h) c", c=C),
                                        bc_last(g.eloop[:, :], C), ALU.mult))
                ch.link(v.tensor_tensor(g.out[:, :], g.out[:, :], sqf, ALU.add))
                ch.link(v.tensor_tensor(g.den[:, :], g.den[:, :], g.eloop[:, :], ALU.add))
                ch.link(v.tensor_scalar(g.den[:, :], g.den[:, :], 1e-16, None, ALU.add))
                ch.link(v.reciprocal(g.den[:, :], g.den[:, :]))
                ch.link(v.tensor_tensor(outh, outh, bc_last(g.den[:, :], C), ALU.mult))
                ch.link(v.tensor_tensor(out3, out3, bc_mid(vec["bias_out"][:, :], NTP), ALU.add))
                ready.append(ch.n)
                v.wait_ge(s_sum, 1)
                ch.link(v.scalar_tensor_tensor(out=mean[:, :], in0=mp[:, 0:F], scalar=1.0 / N,
                                               in1=vec["gn_mean_scale"][:, :], op0=ALU.mult, op1=ALU.mult))
                ch.link(v.tensor_tensor(out3, out3, bc_mid(mean[:, :], NTP), ALU.subtract))
                ch.link(v.tensor_tensor(sqf, g.out[:, :], g.out[:, :], ALU.mult))
                ready.append(ch.n)
                v.wait_ge(s_sum, 2)
                ch.link(v.tensor_scalar(scale[:, :], vp[:, 0:F], 1.0 / N, EPS, ALU.mult, ALU.add))
                ready.append(ch.n)
                v.wait_ge(s_groot, 1)
                ch.link(v.reciprocal(scale[:, :], scale[:, :]))
                ch.link(v.tensor_tensor(scale[:, :], scale[:, :], vec["gn_weight"][:, :], ALU.mult))
                ch.link(v.tensor_tensor(out3, out3, bc_mid(scale[:, :], NTP), ALU.mult))
                ch.link(v.tensor_tensor(out3, out3, bc_mid(vec["gn_bias"][:, :], NTP), ALU.add))
                ch.link(v.scalar_tensor_tensor(out=g.xflat, in0=g.out[:, :], scalar=0.0, in1=g.xflat,
                                               op0=ALU.max, op1=ALU.add))
                ready.append(nodes_layernorm(v, ch, g.x[:, :, :], sq[:, :, :], rmean[:, :], var[:, :], s_root))

            @block.tensor
            def _(t):
                for i, (bank, rows) in enumerate(((mp, g.out[:, :]), (vp, sqf))):
                    t.wait_ge(s, ready[i])
                    for T in range(NT):
                        w = g.valid if T == NT - 1 else g.ones
                        ins = t.matmul(bank[:, 0:F], w[:, :], rows[:, T * F:(T + 1) * F], start=T == 0, stop=T == NT - 1)
                    ins.then_inc(s_sum, 1)

            @block.scalar
            def _(e):
                e.wait_ge(s, ready[2])
                e.activation(scale[:, :], scale[:, :], ACT.Sqrt).then_inc(s_groot, 1)
                e.wait_ge(s, ready[3])
                e.activation(var[:, :], var[:, :], ACT.Sqrt).then_inc(s_root, 1)


def layer3(nc, g, a):
    with ExitStack() as ctx:
        m = Memory(nc, ctx)
        g.out, g.den = m.sb("out3", [P, NP]), m.sb("den3", [P, NTP * HEADS])
        g.score = m.sb("score", [P, SP_ * HEADS])
        g.smax, g.eloop = m.sb("smax", [P, NTP * HEADS]), m.sb("eloop", [P, NTP * HEADS])
        with ExitStack() as c3:
            m3 = Memory(nc, c3)
            g.xr = m3.sb("xr", [P, NTP * F])
            g.xrflat = g.xr[:, :]
            g.easum = m3.sb("easum", [P, NTP * DE])
            g.We, g.att = m3.sb("We", [DE, F]), m3.sb("att", [P, F])
            s_w = m3.sem("s_we")
            with nc.Block() as block:
                @block.sync
                def _(s):
                    s.dma_start(g.We[:, :], a["L3_gnn_We"][:, :]).then_inc(s_w, 16)
                    s.dma_start(g.att[:, :], a["L3_gnn_att"].rearrange("h c -> (h c)").partition_broadcast(P)).then_inc(s_w, 16)
                    s.wait_ge(s_w, 32)
            layer3_nodes(nc, g, a)
            with ExitStack() as ch:
                g.hot3 = Memory(nc, ch).sb("hot_ring3", [P, NG, GS, P])
                score_pass(nc, g, a)
            self_loops(nc, g, a)
        weighted_pass(nc, g)
        finish3(nc, g, a)


class Shared:
    pass


def build(nc, a, out, stop=None):
    g = Shared()
    dram = lambda name, shape, dt=F32: nc.dram_tensor(name, shape, dt).ap()
    g.ct = dram("edge_rows", (ET, 4 * P), I32)
    g.d0row = dram("resets", (SP_, P))
    g.drelrow = dram("dst_in_tile", (SP_, P))
    g.srcrow = dram("src_rows", (SP_, P))
    g.d0flat, g.drelflat, g.srcflat = (r.rearrange("k e -> (k e)") for r in (g.d0row, g.drelrow, g.srcrow))
    g.trow = dram("node_tile_of_step", (KB * P,), I32)
    g.erow = dram("edge_tile_of_step", (KB * P,), I32)
    g.xp = dram("x_sign_pos", (NP, W))
    g.hq = [dram(f"h_sign_pos{q}", (NP, W)) for q in range(DH // F)]
    g.hT = dram("h_transposed", (NP, DH))
    g.agg2 = dram("agg2", (DH // F, P, NP))
    g.x2 = dram("x2", (NP, F))
    g.sums = [dram(f"sums{c}", (NP + P, F)) for c in range(CHAINS)]
    g.xl_rows = dram("xl_rows", (NP, F))
    g.rows = dram("xl_of_steps", (SP_, P, F))
    with ExitStack() as ctx:
        ctx.enter_context(nc.allow_non_contiguous_dma(reason="columns of positions and node tiles, a few thousand words"))
        m = Memory(nc, ctx)
        g.src_i = m.sb("src_i", [P, KB * P], I32)
        g.src_f = m.sb("src_f", [P, KB * P])
        g.drel = m.sb("drel", [P, KB * P])
        g.endf = m.sb("endf", [P, KB * P])
        g.T = m.sb("T", [1, SP_], I32)
        g.t = m.sb("t", [1, SP_], I32)
        g.iota_n = m.sb("iota_n", [P, P])
        g.iota_p = m.sb("iota_p", [P, 1])
        g.valid = m.sb("valid", [P, P])
        g.ones = m.sb("ones", [P, P])
        g.ident = m.sb("ident", [P, P])
        g.lack = m.sb("lack_i", [P, 1], I32)
        g.deg = m.sb("deg", [P, NTP * 2])
        g.x = m.sb("x_nodes", [P, NTP, F])
        g.xflat = g.x[:, :, :].rearrange("p t f -> p (t f)")
        with ExitStack() as c12:
            m12 = Memory(nc, c12)
            g.acc = m12.sb("acc", [P, NP])
            g.y = m12.sb("y_nodes", [P, NTP, F])
            g.yflat = g.y[:, :, :].rearrange("p t f -> p (t f)")
            with ExitStack() as c0:
                g.posb = Memory(nc, c0).sb("posb", [P, NP])
                prepare(nc, g, a)
                max_pass(nc, g, "a", g.xp[0:N, :], g.acc, g.deg)
                all_have_equal(nc, g)
                lack = nc.values_load(g.lack[0:1, 0:1], min_val=0, max_val=N)
                with nc.If(lack > 0):
                    nc.all_engine_barrier()
                    layer0(nc, g, a, "f", True, False)
                    general_tables(nc, g, a)
                    for q in range(DH // F):
                        max_pass(nc, g, f"q{q}", g.hq[q][0:N, :], g.acc, g.deg)
                        keep_agg2(nc, g, q)
                    layer0(nc, g, a, "s", False, True)
                with nc.Else():
                    nc.all_engine_barrier()
                    layer0(nc, g, a, "b", True, True)
            if stop != "L0":
                sum_pass(nc, g, "1", g.x2[0:N, :], g.acc)
                finish1(nc, g)
        if stop is None or stop == "L2":
            scatter_pass(nc, g)
            finish2(nc, g)
        if stop is None:
            layer3(nc, g, a)
        store(nc, g, out)


def store(nc, g, out):
    with ExitStack() as ctx:
        s_o = Memory(nc, ctx).sem("s_stored")
        with nc.Block() as block:
            @block.sync
            def _(s):
                s.dma_start(out[0:(NT - 1) * P, :].rearrange("(t p) f -> p t f", p=P), g.x[:, 0:NT - 1, :]).then_inc(s_o, 16)
                s.dma_start(out[(NT - 1) * P:N, :], g.x[0:N - (NT - 1) * P, NT - 1, :]).then_inc(s_o, 16)
                s.wait_ge(s_o, 32)


def kernel(**inputs):
    import numpy as np
    import concourse.bacc as bacc
    from concourse.bass_utils import run_bass_kernel_spmd as run
    nc = bacc.Bacc("TRN2", target_bir_lowering=False, num_devices=1)
    arrays, aps = {}, {}
    transposed = {"L0_gnn_Wrel1": "Wrel1T", "L0_gnn_Wroot1": "Wroot1T", "L0_gnn_Wrel2": "Wrel2T",
                  "L0_gnn_Wroot2": "Wroot2T", "L0_gnn_Wcls": "WclsT", "L1_gnn_W1": "W1T", "L1_gnn_W2": "W2T"}
    for name, v in inputs.items():
        v = np.asarray(v)
        if name in transposed:
            v, name = v.T, transposed[name]
        if name == "edge_attr_64":
            rows = np.zeros((ET * P, DE), v.dtype)
            rows[:E] = v
            layouts = {"ea": rows, "eaT": rows.T}
        else:
            layouts = {name: v}
        for name, v in layouts.items():
            v = np.ascontiguousarray(v)
            arrays["in_" + name] = v
            aps[name] = nc.dram_tensor("in_" + name, v.shape, mybir.dt.from_np(v.dtype), kind="ExternalInput").ap()
    out = nc.dram_tensor("out", (N, F), F32, kind="ExternalOutput").ap()
    build(nc, aps, out, None)
    r = run(nc, [arrays], core_ids=[0])
    return r.results[0]["out"]
```

```python
import concourse.bass as bass
from concourse import mybir
from contextlib import ExitStack

F32 = mybir.dt.float32
I32 = mybir.dt.int32
ALU = mybir.AluOpType
ACT = mybir.ActivationFunctionType
AX = mybir.AxisListType

N = 6250
E = 106250
F = 128
DH = 512
DE = 64
HEADS = 4
C = F // HEADS
FN = F + 1
FH = F + HEADS
P = 128
NT = -(-N // P)
NTP = NT + NT % 2
NP = NTP * P
EF = E // P
EREM = E - EF * P
ET = EF + 2
U = 16
GS = 4
NG = U // GS
STEPS = EF + 1 + NT - 1
TURNS = -(-STEPS // U)
SP_ = TURNS * U
KB = -(-SP_ // P)
U3 = 32
NG3 = U3 // GS
TURNS3 = -(-STEPS // U3)
SPX = TURNS3 * U3
PAD = 1 << 20
BIG = 3e38
HALFBIG = 1e38
EPS = 1e-5
W = 2 * F + 1


def wait(eng, sem, value):
    if isinstance(value, int) and value <= 0:
        return
    eng.wait_ge(sem, value)


def turns(eng, body, n, last=0):
    body(0)
    with eng.Fori(1, n) as it:
        body(it)


class Memory:

    def __init__(self, nc, ctx):
        self.nc, self.ctx, self.sems = nc, ctx, []
        ctx.callback(self.end)

    def end(self):
        if self.sems:
            self.nc.clear_and_free_semaphores(self.sems)
            self.nc.all_engine_barrier()

    def sb(self, name, shape, dt=F32):
        return self.ctx.enter_context(self.nc.sbuf_tensor(name, shape, dt))

    def bank(self, name):
        return self.ctx.enter_context(self.nc.psum_tensor(name, [P, 512], F32))

    def sem(self, name):
        self.sems.append(self.nc.alloc_semaphore(name))
        return self.sems[-1]


def bc_last(ap, n):
    return ap.unsqueeze(2).broadcast_to([ap.shape[0], ap.shape[1], n])


def bc_mid(ap, n):
    return ap.unsqueeze(1).broadcast_to([ap.shape[0], n, ap.shape[1]])


def prepare(nc, g, a):
    with ExitStack() as ctx:
        m = Memory(nc, ctx)
        padc = m.sb("padc", [2, 4 * P], I32)
        dst_i = m.sb("dst_i", [P, KB, P], I32)
        dst_f = m.sb("dst_f", [P, KB * P])
        less = m.sb("less", [P, KB * P])
        cnt = m.sb("cnt", [P, NT - 1])
        start_i = m.sb("start_i", [P, NT - 1], I32)
        first_i = m.sb("first_i", [P, NT - 1], I32)
        first_f = m.sb("first_f", [P, NT - 1])
        tile_no = m.sb("tile_no", [P, NT - 1])
        stepno = m.sb("stepno", [P, KB])
        le = m.sb("le", [P, NT - 1])
        T_f = m.sb("T_f", [P, KB])
        T_i = m.sb("T_i", [P, KB], I32)
        T128 = m.sb("T128", [P, KB])
        t_f = m.sb("t_f", [P, KB])
        t_i = m.sb("t_i", [P, KB], I32)
        rows = m.sb("rows", [P, KB, 4 * P], I32)
        rows_f = m.sb("rows_f", [P, KB, 4, P])
        flag = m.sb("flag", [P, KB, P])
        endf_r = m.sb("endf_r", [P, KB, P])
        drel_r = m.sb("drel_r", [P, KB, P])
        sgn = m.sb("sgn", [P, NTP, F])
        start_ps = m.bank("start_ps")
        tr_ps = [m.bank(f"tr_ps{i}") for i in range(2)]
        s_init = m.sem("s_init")
        s_x = m.sem("s_x")
        s_pos = m.sem("s_pos")
        s_padded = m.sem("s_padded")
        s_built = m.sem("s_built")
        s_dst = m.sem("s_dst")
        s_v = m.sem("s_v")
        s_start = m.sem("s_start")
        s_rows = m.sem("s_rows")
        s_tr = m.sem("s_tr")
        s_cp = m.sem("s_cp")
        s_out = m.sem("s_out")
        s_T = m.sem("s_T")
        s_Tl = m.sem("s_Tl")
        ct = g.ct
        V_X = 5
        V_CNT = V_X + NT - 1
        V_T = V_CNT + 4 + 5 * KB

        with nc.Block() as block:
            @block.gpsimd
            def _(p):
                p.iota(g.iota_n[:, :], [[1, P]], base=0, channel_multiplier=0,
                       allow_small_or_imprecise_dtypes=True).then_inc(s_init, 1)
                p.iota(g.iota_p[:, :], [[0, 1]], base=0, channel_multiplier=1,
                       allow_small_or_imprecise_dtypes=True).then_inc(s_init, 1)
                p.iota(tile_no[:, :], [[1, NT - 1]], base=1, channel_multiplier=0,
                       allow_small_or_imprecise_dtypes=True).then_inc(s_init, 1)
                p.iota(stepno[:, :], [[P, KB]], base=0, channel_multiplier=1,
                       allow_small_or_imprecise_dtypes=True).then_inc(s_init, 1)
                p.memset(g.ones[:, :], 1.0).then_inc(s_init, 1)
                p.memset(padc[:, 0:P], 0).then_inc(s_init, 1)
                p.memset(padc[:, P:4 * P], PAD).then_inc(s_init, 1)
                p.memset(dst_i[:, :, :], PAD).then_inc(s_init, 1)
                p.memset(g.x[:, :, :], 0.0).then_inc(s_init, 1)
                p.memset(g.posb[:, N:NP], 0.0).then_inc(s_init, 1)
                p.memset(g.ident[:, :], 0.0).then_inc(s_init, 1)
                p.wait_ge(s_init, 11)
                p.affine_select(out=g.ident[:, :], in_=g.ident[:, :], compare_op=ALU.not_equal, fill=1.0,
                                base=0, pattern=[[-1, P]], channel_multiplier=1).then_inc(s_init, 1)
                p.wait_ge(s_v, V_T)
                p.wait_ge(s_built, 16 * 7)
                for b in range(KB):
                    p.indirect_dma_start(out=rows[:, b, :], out_offset=None, in_=ct[:, :],
                                         in_offset=bass.IndirectOffsetOnAxis(ap=t_i[:, b:b + 1], axis=0)
                                         ).then_inc(s_rows, 16)

            @block.sync
            def _(s):
                s.wait_ge(s_init, 11)
                s.dma_start(ct[EF:EF + 2, :], padc[:, :]).then_inc(s_padded, 16)
                s.dma_start(ct[0:1, 2 * P:2 * P + 1], padc[0:1, P:P + 1]).then_inc(s_padded, 16)
                full = (ET // P) * P
                s.dma_start(dst_i[:, 0:ET // P, :],
                            a["dst"][0:full * P].rearrange("(b p e) -> p b e", p=P, e=P)).then_inc(s_dst, 16)
                s.dma_start(dst_i[0:EF - full, ET // P, :],
                            a["dst"][full * P:EF * P].rearrange("(p e) -> p e", e=P)).then_inc(s_dst, 16)
                s.dma_start(dst_i[EF - full:EF - full + 1, ET // P, 0:EREM],
                            a["dst"][EF * P:E].unsqueeze(0)).then_inc(s_dst, 16)
                s.wait_ge(s_padded, 32)
                s.dma_start(ct[0:EF, 0:P], a["src"][0:EF * P].rearrange("(t e) -> t e", e=P)).then_inc(s_built, 16)
                s.dma_start(ct[0:EF, P:2 * P], a["dst"][0:EF * P].rearrange("(t e) -> t e", e=P)).then_inc(s_built, 16)
                s.dma_start(ct[1:EF, 2 * P:3 * P],
                            a["dst"][P - 1:EF * P - 1].rearrange("(t e) -> t e", e=P)).then_inc(s_built, 16)
                s.dma_start(ct[0:EF, 3 * P:4 * P],
                            a["dst"][1:EF * P + 1].rearrange("(t e) -> t e", e=P)).then_inc(s_built, 16)
                s.dma_start(ct[0:1, 2 * P + 1:3 * P], a["dst"][0:P - 1].unsqueeze(0)).then_inc(s_built, 16)
                s.dma_start(ct[EF:EF + 1, 0:2 * P].rearrange("o (c e) -> o c e", c=2)[:, 0, 0:EREM],
                            a["src"][EF * P:E].unsqueeze(0)).then_inc(s_built, 16)
                for off, lo, n in ((P, 0, EREM), (2 * P, -1, EREM), (3 * P, 1, EREM - 1)):
                    s.dma_start(ct[EF:EF + 1, off:off + n],
                                a["dst"][EF * P + lo:EF * P + lo + n].unsqueeze(0)).then_inc(s_padded, 16)
                s.wait_ge(s_padded, 32 + 48)
                s.sem_inc(s_built, 16)
                s.wait_ge(s_v, V_T + 8)
                nb = SPX // P
                for dst, srct in ((g.d0row, flag[:, :, :]), (g.drelrow, drel_r[:, :, :]), (g.srcrow, rows_f[:, :, 0, :])):
                    s.dma_start(dst[0:nb * P, :].rearrange("(b p) e -> p b e", p=P), srct[:, 0:nb, :]).then_inc(s_out, 16)
                    assert nb * P == SPX
                s.wait_ge(s_out, 48)

            @block.scalar
            def _(s):
                s.wait_ge(s_init, 10)
                s.dma_start(g.x[:, 0:NT - 1, :], a["x"][0:(NT - 1) * P, :].rearrange("(t p) f -> p t f", p=P)
                            ).then_inc(s_x, 16)
                s.dma_start(g.x[0:N - (NT - 1) * P, NT - 1, :], a["x"][(NT - 1) * P:N, :]).then_inc(s_x, 16)
                s.dma_start(g.posb[:, 0:N], a["node_vec"].partition_broadcast(P)).then_inc(s_pos, 16)
                s.dma_start(g.xp[0:N, 2 * F:2 * F + 1], a["node_vec"].unsqueeze(1)).then_inc(s_pos, 16)
                s.dma_start(g.xp[0:N, 0:F], a["x"][:, :]).then_inc(s_pos, 16)
                s.wait_ge(s_v, V_T)
                s.dma_start(g.trow[0:KB * P].rearrange("(b p) -> p b", p=P), T_i[:, :]).then_inc(s_T, 16)
                s.dma_start(g.erow[0:KB * P].rearrange("(b p) -> p b", p=P), t_i[:, :]).then_inc(s_T, 16)
                s.wait_ge(s_T, 32)
                s.dma_start(g.T[:, :], g.trow[0:SPX].unsqueeze(0)).then_inc(s_Tl, 16)
                s.dma_start(g.t[:, :], g.erow[0:SPX].unsqueeze(0)).then_inc(s_Tl, 16)
                s.dma_start(g.xp[:, F:2 * F].rearrange("(t p) f -> p t f", p=P), sgn[:, :, :]).then_inc(s_pos, 16)
                s.wait_ge(s_Tl, 32)
                s.wait_ge(s_pos, 64)

            @block.tensor
            def _(t):
                t.wait_ge(s_init, 12)
                t.wait_ge(s_v, V_CNT)
                t.matmul(start_ps[:, 0:NT - 1], g.ones[:, :], cnt[:, :], start=True, stop=True).then_inc(s_start, 1)
                t.wait_ge(s_v, V_T + 8)
                i = 0
                for b in range(KB):
                    for src in (rows_f[:, b, 0, :], drel_r[:, b, :], endf_r[:, b, :]):
                        wait(t, s_cp, i - 1)
                        t.transpose(tr_ps[i % 2][:, 0:P], src, g.ident[:, :]).then_inc(s_tr, 1)
                        i += 1

            @block.vector
            def _(v):
                done = 0

                def step(ins):
                    nonlocal done
                    ins.then_inc(s_v, 1)
                    done += 1

                def link(ins):
                    step(ins)
                    v.wait_ge(s_v, done)

                v.wait_ge(s_dst, 48)
                v.wait_ge(s_init, 12)
                v.wait_ge(s_x, 32)
                link(v.tensor_scalar(g.valid[:, :], g.ones[:, :], g.iota_p[:, :], None, ALU.mult))
                link(v.tensor_scalar(g.valid[:, :], g.valid[:, :], float(N - (NT - 1) * P), None, ALU.is_lt))
                link(v.tensor_copy(dst_f[:, :], dst_i[:, :, :].rearrange("p b e -> p (b e)")))
                link(v.tensor_scalar(sgn[:, :, :], g.x[:, :, :], 0.0, 0.5, ALU.is_ge, ALU.subtract))
                link(v.memset(less[:, :], 0.0))
                assert done == V_X
                for T in range(1, NT):
                    link(v.tensor_scalar(less[:, :], dst_f[:, :], float(T * P), 0.0, ALU.is_lt, ALU.add,
                                         accum_out=cnt[:, T - 1:T]))
                assert done == V_CNT
                v.wait_ge(s_start, 1)
                link(v.tensor_copy(start_i[:, :], start_ps[:, 0:NT - 1]))
                link(v.tensor_scalar(first_i[:, :], start_i[:, :], 7, None, ALU.arith_shift_right))
                link(v.tensor_copy(first_f[:, :], first_i[:, :]))
                link(v.tensor_tensor(first_f[:, :], first_f[:, :], tile_no[:, :], ALU.add))
                for b in range(KB):
                    col = slice(b, b + 1)
                    link(v.tensor_scalar(le[:, :], first_f[:, :], stepno[:, col], 0.0, ALU.is_le, ALU.add,
                                         accum_out=T_f[:, col]))
                    link(v.tensor_copy(T_i[:, col], T_f[:, col]))
                    link(v.tensor_tensor(t_f[:, col], stepno[:, col], T_f[:, col], ALU.subtract))
                    link(v.tensor_scalar(t_f[:, col], t_f[:, col], float(ET - 1), None, ALU.min))
                    link(v.tensor_copy(t_i[:, col], t_f[:, col]))
                assert done == V_T
                v.wait_ge(s_rows, 16 * KB)
                link(v.tensor_copy(rows_f[:, :, :, :], rows[:, :, :].rearrange("p b (c e) -> p b c e", c=4)))
                link(v.tensor_scalar(T128[:, :], T_f[:, :], float(P), None, ALU.mult))
                link(v.tensor_tensor(drel_r[:, :, :], rows_f[:, :, 1, :], bc_last(T128[:, :], P), ALU.subtract))
                link(v.tensor_tensor(endf_r[:, :, :], rows_f[:, :, 1, :], rows_f[:, :, 3, :], ALU.not_equal))
                link(v.tensor_tensor(flag[:, :, :], rows_f[:, :, 1, :], rows_f[:, :, 2, :], ALU.not_equal))
                link(v.tensor_scalar(flag[:, :, :], flag[:, :, :], -2.0, 1.0, ALU.mult, ALU.add))
                link(v.tensor_scalar(flag[:, :, :], flag[:, :, :], BIG, None, ALU.mult))
                link(v.tensor_scalar(T128[:, :], T_f[:, :], float(P), None, ALU.mult))
                assert done == V_T + 8
                i = 0
                for b in range(KB):
                    for to in (g.src_f, g.drel, g.endf):
                        v.wait_ge(s_tr, i + 1)
                        v.tensor_copy(to[:, b * P:(b + 1) * P], tr_ps[i % 2][:, 0:P]).then_inc(s_cp, 1)
                        i += 1
                v.wait_ge(s_cp, i)
                v.tensor_copy(g.src_i[:, :], g.src_f[:, :]).then_inc(s_cp, 1)


def max_pass(nc, g, tag, table, acc):
    with ExitStack() as ctx:
        m = Memory(nc, ctx)
        ring = m.sb(f"ring{tag}", [P, U, W])
        idx = m.sb(f"idx{tag}", [P, U], I32)
        hot = m.sb(f"hot{tag}", [P, NG, GS, P])
        msg = m.sb(f"msg{tag}", [P, 2, GS, F])
        sgn = m.sb(f"sg{tag}", [P, 2, GS, F])
        run = m.sb(f"run{tag}", [P, 2, GS * P])
        ends = m.sb(f"ends{tag}", [P, 2, GS, F])
        reset = m.sb(f"reset{tag}", [P, 2, 2 * GS * P])
        posd = m.sb(f"posd{tag}", [P, GS])
        junk = m.sb(f"junk{tag}", [P, GS, P])
        nd = m.sb(f"nd{tag}", [P, GS])
        dz = m.sb(f"dz{tag}", [P, GS])
        wn = m.sb(f"wn{tag}", [P, GS])
        w2 = m.sb(f"w2{tag}", [P, 2, GS])
        zs = m.sb(f"zs{tag}", [P, 2, GS])
        msgT = [m.bank(f"msgT{tag}{i}") for i in range(2)]
        runT = [m.bank(f"runT{tag}{i}") for i in range(2)]
        sel = [m.bank(f"sel{tag}{i}") for i in range(2)]
        s_idx = m.sem(f"s_idx{tag}")
        s_go = m.sem(f"s_go{tag}")
        s_g = [m.sem(f"s_g{tag}{i}") for i in range(NG)]
        s_rst = [m.sem(f"s_rst{tag}{i}") for i in range(2)]
        s_hot = m.sem(f"s_hot{tag}")
        s_c = m.sem(f"s_c{tag}")
        s_z = m.sem(f"s_z{tag}")
        s_sg = m.sem(f"s_sg{tag}")
        s_m = m.sem(f"s_m{tag}")
        s_mT = m.sem(f"s_mT{tag}")
        s_run = m.sem(f"s_run{tag}")
        s_rT = m.sem(f"s_rT{tag}")
        s_e = m.sem(f"s_e{tag}")
        s_sel = m.sem(f"s_sel{tag}")
        s_acc = m.sem(f"s_acc{tag}")
        s_ini = m.sem(f"s_ini{tag}")
        NCH = 5

        with nc.Block() as block:
            @block.gpsimd
            def _(p):
                def body(it):
                    for k in range(U):
                        q = k // GS
                        if k % GS == 0:
                            if not isinstance(it, int):
                                p.wait_ge(s_m, it * NG - NG + q + 1)
                                p.sem_inc(s_go, 1)
                            p.tensor_copy(idx[:, k:k + GS], g.src_i[:, bass.ds(it * U + k, GS)]).then_inc(s_idx, 1)
                            p.wait_ge(s_idx, it * NG + q + 1)
                            p.sem_inc(s_go, 1)
                        p.indirect_dma_start(out=ring[:, k, :], out_offset=None, in_=table,
                                             in_offset=bass.IndirectOffsetOnAxis(ap=idx[:, k:k + 1], axis=0)
                                             ).then_inc(s_g[k // GS], 16)
                turns(p, body, TURNS)

            @block.sync
            def _(s):
                def body(it):
                    for h in range(2):
                        if not isinstance(it, int):
                            s.wait_ge(s_run, it * NG - NG + 2 * h + 2)
                        rows = g.d0flat[bass.ds(it * (U * P) + h * (U * P // 2), U * P // 2)]
                        s.dma_start(reset[:, h, :], rows.partition_broadcast(P)).then_inc(s_rst[h], 16)
                turns(s, body, TURNS)

            @block.scalar
            def _(s):
                def ends_of(G, q):
                    wait(s, s_rT, G + 1)
                    wait(s, s_sel, G - 1)
                    for k in range(GS):
                        ins = s.activation(ends[:, q % 2, k, :], runT[q % 2][:, k * P:(k + 1) * P], ACT.Copy,
                                           scale=g.endf[:, bass.ds(G * GS + k, 1)])
                    ins.then_inc(s_e, 1)

                def body(it):
                    for q in range(NG):
                        G = it * NG + q
                        wait(s, s_g[q], 64 * (it + 1))
                        wait(s, s_z, G + 1)
                        wait(s, s_m, G - 1)
                        for k in range(GS):
                            ins = s.activation(sgn[:, q % 2, k, :], ring[:, q * GS + k, F:2 * F], ACT.Copy,
                                               scale=zs[:, q % 2, k:k + 1])
                        ins.then_inc(s_sg, 1)
                        if not (isinstance(it, int) and q < 2):
                            ends_of(G - 2, (q - 2) % NG)
                turns(s, body, TURNS)
                for b in (2, 1):
                    ends_of(TURNS * NG - b, NG - b)

            @block.tensor
            def _(t):
                def back(G, q):
                    wait(t, s_run, G + 1)
                    wait(t, s_e, G - 1)
                    for k in range(GS):
                        ins = t.transpose(runT[q % 2][:, k * P:(k + 1) * P], run[:, q % 2, k * P:(k + 1) * P],
                                          g.ident[:, :])
                    ins.then_inc(s_rT, 1)

                def select(G, q):
                    wait(t, s_hot, G + 1)
                    wait(t, s_e, G + 1)
                    wait(t, s_acc, (G - 1) * GS)
                    for k in range(GS):
                        ins = t.matmul(sel[q % 2][:, k * P:(k + 1) * P], ends[:, q % 2, k, :], hot[:, q, k, :],
                                       start=True, stop=True)
                    ins.then_inc(s_sel, 1)

                def transposed(G, q):
                    wait(t, s_m, G + 1)
                    wait(t, s_run, G - 1)
                    for k in range(GS):
                        ins = t.transpose(msgT[q % 2][:, k * P:(k + 1) * P], msg[:, q % 2, k, :], g.ident[:, :])
                    ins.then_inc(s_mT, 1)

                def body(it):
                    for q in range(NG):
                        G = it * NG + q
                        for lag, stage in ((3, select), (1, transposed), (2, back)):
                            if not (isinstance(it, int) and q < lag):
                                stage(G - lag, (q - lag) % NG)
                turns(t, body, TURNS)
                GL = TURNS * NG
                select(GL - 3, NG - 3)
                transposed(GL - 1, NG - 1)
                back(GL - 2, NG - 2)
                back(GL - 1, NG - 1)
                select(GL - 2, NG - 2)
                select(GL - 1, NG - 1)

            @block.vector
            def _(v):
                v.memset(acc, 0.0).then_inc(s_ini, 1)
                v.memset(run[:, :, :], -BIG).then_inc(s_ini, 1)
                v.wait_ge(s_ini, 2)
                tregs = [v.alloc_register(f"t{tag}{j}") for j in range(GS)]
                aregs = [v.alloc_register(f"a{tag}{j}") for j in range(GS)]

                def tiles_of(G, regs):
                    v.load(regs, g.T[0:1, bass.ds(G * GS, GS)])
                    return [v.snap(r, min_val=0, max_val=NT - 1) for r in regs]

                def scan(G, q, it_half, h):
                    wait(v, s_mT, G + 1)
                    if q % 2 == 0:
                        wait(v, s_rst[h], 16 * (it_half + 1))
                    wait(v, s_run, G)
                    wait(v, s_rT, G - 1)
                    v.tensor_tensor_scan(run[:, q % 2, :], reset[:, h, (q % 2) * GS * P:(q % 2 + 1) * GS * P],
                                         msgT[q % 2][:, :], run[:, (q + 1) % 2, GS * P - 1:GS * P],
                                         ALU.min, ALU.max).then_inc(s_run, 1)

                def add(G, q, k, T):
                    if k == 0:
                        wait(v, s_sel, G + 1)
                    wait(v, s_acc, G * GS + k)
                    to = acc[:, bass.ds(T[k] * P, P)]
                    v.tensor_tensor(to, to, sel[q % 2][:, k * P:(k + 1) * P], ALU.add).then_inc(s_acc, 1)

                def message(G, q, k):
                    if k == 0:
                        v.wait_ge(s_c, G * NCH + 5)
                        v.wait_ge(s_sg, G + 1)
                        wait(v, s_mT, G - 1)
                    ins = v.scalar_tensor_tensor(
                        out=msg[:, q % 2, k, :], in0=ring[:, q * GS + k, 0:F], scalar=w2[:, q % 2, k:k + 1],
                        in1=sgn[:, q % 2, k, :], op0=ALU.mult, op1=ALU.add)
                    if k == GS - 1:
                        ins.then_inc(s_m, 1)

                def dst_position(G, k, T):
                    ins = v.scalar_tensor_tensor(
                        out=junk[:, k, :], in0=g.iota_n[:, :], scalar=g.drel[:, bass.ds(G * GS + k, 1)],
                        in1=g.posb[:, bass.ds(T[k] * P, P)], op0=ALU.is_equal, op1=ALU.mult,
                        accum_out=posd[:, k:k + 1])
                    if k == GS - 1:
                        ins.then_inc(s_c, 1)

                def step(it, q, last=0):
                    G = it * NG + q
                    first = isinstance(it, int) and it == 0
                    on = lambda lag: lag >= last and not (first and q < lag)
                    at = lambda lag: (G - lag, (q - lag) % NG)
                    new, adds, msgs = on(0), on(4), on(1)
                    if adds:
                        A = tiles_of(G - 4, aregs)
                        add(*at(4), 0, A)
                    if new:
                        wait(v, s_sel, G - NG + 1)
                        v.tensor_tensor(hot[:, q, :, :], bc_mid(g.iota_n[:, :], GS),
                                        bc_last(g.drel[:, bass.ds(G * GS, GS)], P), ALU.is_equal).then_inc(s_hot, 1)
                        T = tiles_of(G, tregs)
                        dst_position(G, 0, T)
                    if adds:
                        add(*at(4), 1, A)
                    if new:
                        dst_position(G, 1, T)
                        dst_position(G, 2, T)
                    if adds:
                        add(*at(4), 2, A)
                    if new:
                        dst_position(G, 3, T)
                    if on(2):
                        scan(*at(2), it if q >= 2 else it - 1, ((q - 2) % NG) // 2)
                    if new:
                        v.wait_ge(s_c, G * NCH + 1)
                        v.wait_ge(s_g[q], 64 * (it + 1))
                        wait(v, s_sg, G - 1)
                        poss = ring[:, q * GS:(q + 1) * GS, 2 * F]
                        v.tensor_tensor(nd[:, :], posd[:, :], poss, ALU.subtract).then_inc(s_c, 1)
                    if adds:
                        add(*at(4), 3, A)
                    if new:
                        v.wait_ge(s_c, G * NCH + 2)
                        v.tensor_scalar(zs[:, q % 2, :], nd[:, :], 0.0, BIG, ALU.is_equal, ALU.mult).then_inc(s_z, 1)
                        v.scalar_tensor_tensor(out=dz[:, :], in0=nd[:, :], scalar=0.0, in1=nd[:, :],
                                               op0=ALU.is_equal, op1=ALU.add).then_inc(s_c, 1)
                    if msgs:
                        message(*at(1), 0)
                        message(*at(1), 1)
                    if new:
                        v.wait_ge(s_c, G * NCH + 3)
                        v.reciprocal(wn[:, :], dz[:, :]).then_inc(s_c, 1)
                    if msgs:
                        message(*at(1), 2)
                        message(*at(1), 3)
                    if new:
                        v.wait_ge(s_c, G * NCH + 4)
                        v.scalar_tensor_tensor(out=w2[:, q % 2, :], in0=nd[:, :], scalar=0.0, in1=wn[:, :],
                                               op0=ALU.is_equal, op1=ALU.subtract).then_inc(s_c, 1)

                def body(it):
                    for q in range(NG):
                        step(it, q)
                turns(v, body, TURNS)
                for q in range(4):
                    step(TURNS, q, q + 1)


class Events:

    def __init__(self, sem, names):
        self.sem, self.names = sem, names

    def value(self, it, name, j):
        return it * (2 * len(self.names)) + 2 * self.names.index(name) + j + 1

    def wait(self, eng, it, name, j):
        eng.wait_ge(self.sem, self.value(it, name, j))


class Chain:

    def __init__(self, eng, sem, it, per):
        self.eng, self.sem, self.base, self.per, self.n = eng, sem, it * per, per, 0

    def link(self, ins):
        self.n += 1
        ins.then_inc(self.sem, 1)
        self.eng.wait_ge(self.sem, self.base + self.n)

    def end(self):
        assert self.n == self.per, (self.n, self.per)


def nodes_layernorm(v, ch, x, tmp, mean, var, s_root):
    ch.link(v.tensor_reduce(mean, x, AX.X, ALU.add))
    ch.link(v.tensor_scalar(mean, mean, 1.0 / F, None, ALU.mult))
    ch.link(v.tensor_tensor(x, x, bc_last(mean, F), ALU.subtract))
    ch.link(v.tensor_tensor(tmp, x, x, ALU.mult))
    ch.link(v.tensor_reduce(var, tmp, AX.X, ALU.add))
    ch.link(v.tensor_scalar(var, var, 1.0 / F, EPS, ALU.mult, ALU.add))
    ready = ch.n
    v.wait_ge(s_root, 1)
    ch.link(v.reciprocal(var, var))
    ch.link(v.tensor_tensor(x, x, bc_last(var, F), ALU.mult))
    return ready


def root_of_variance(block, ready, s, var, s_root):
    @block.scalar
    def _(e):
        e.wait_ge(s, ready)
        e.activation(var[:, :], var[:, :], ACT.Sqrt).then_inc(s_root, 1)


HALF_TILES = NTP // 2


def layer0(nc, g, a, tag, first, second):
    both = first and second
    with ExitStack() as ctx:
        m = Memory(nc, ctx)
        KD = DH // P
        sb = lambda name, shape: m.sb(name + tag, shape)
        wrel1, wroot1 = sb("wrel1", [P, DH]), sb("wroot1", [P, DH])
        wroot2 = sb("wroot2", [P, KD, DH])
        wrel2 = sb("wrel2", [P, KD, DH])
        wcls = sb("wcls", [P, KD, F])
        w12 = sb("w12", [P, 2, F])
        vec = {n: sb(n, [P, DH]) for n in ("brel1", "g1", "b1", "brel2", "g2", "b2")}
        vec.update({n: sb(n, [P, F]) for n in ("bcls", "L1b1")})
        xs, xT = sb("xs", [P, 2, F]), sb("xT", [P, 2, P])
        low, finite = sb("low", [P, 2, P]), sb("finite", [P, 2, P])
        agg = sb("agg", [P, 2, P])
        h = [sb(f"h{i}", [P, 2, DH]) for i in range(2)]
        hT = [sb(f"hT{i}", [P, 2, DH]) for i in range(2)]
        hr = sb("hr", [P, 2, DH])
        agg2, low2 = sb("agg2", [P, 2, DH]), sb("low2", [P, 2, DH])
        y, yT = sb("y", [P, 2, F]), sb("yT", [P, 2, P])
        x2 = sb("x2", [P, 2, F])
        st, mv = sb("st", [P, 3, 2, 6]), sb("mv", [P, 3, 2, 2])
        root = sb("root", [P, 3, 2])
        tr = [m.bank(f"tr{tag}{j}") for j in range(2)]
        big = [m.bank(f"big{tag}{j}") for j in range(2)]
        small = [m.bank(f"small{tag}{j}") for j in range(2)]
        s_w = m.sem("s_w" + tag)
        s_load = [m.sem(f"s_load{tag}{j}") for j in range(2)]
        s_store = [m.sem(f"s_store{tag}{j}") for j in range(2)]
        s_chain = m.sem("s_chain" + tag)
        s_go = m.sem("s_go" + tag)
        pe_names, act_names, dve_names = [], [], []
        if first:
            pe_names += ["xT", "h1", "h1T"]
            act_names += ["xs", "xT", "root1", "h1T"] + ([] if both else ["hr"])
            dve_names += ["agg", "var1", "h1"]
        if second:
            pe_names += ["h2", "h2T", "cls", "yT", "x12"]
            act_names += ["root2", "h2T", "rooty", "yT", "x2"]
            dve_names += ([] if both else ["agg2"]) + ["var2", "h2", "vary", "y", "x12"]
        pe = Events(m.sem("s_pe" + tag), pe_names)
        act = Events(m.sem("s_act" + tag), act_names)
        dve = Events(m.sem("s_dve" + tag), dve_names)
        LINKS = 2 * ((2 + 6) * first + 2 * (second and not both) + (6 + 6 + 1) * second)
        loads = [(wrel1[:, :], a["Wrel1T"][:, :]), (wroot1[:, :], a["Wroot1T"][:, :]),
                 (wroot2[:, :, :], a["Wroot2T"].rearrange("(k p) o -> p k o", p=P)),
                 (wrel2[:, :, :], a["Wrel2T"].rearrange("(k p) o -> p k o", p=P)),
                 (wcls[:, :, :], a["WclsT"].rearrange("(k p) o -> p k o", p=P)),
                 (w12[:, 0, :], a["W1T"][:, :]), (w12[:, 1, :], a["W2T"][:, :])]
        loads += [(vec[n][:, :], a["L0_gnn_" + n].partition_broadcast(P)) for n in vec if n != "L1b1"]
        loads += [(vec["L1b1"][:, :], a["L1_gnn_b1"].partition_broadcast(P))]

        with nc.Block() as block:
            @block.sync
            def _(s):
                for to, of in loads:
                    s.dma_start(to, of).then_inc(s_w, 16)

                def body(it):
                    for j in range(2):
                        T = it * 2 + j
                        if first and not both:
                            act.wait(s, it, "h1T", j)
                            s.dma_start(g.hT[bass.ds(T * P, P), :], hT[0][:, j, :]).then_inc(s_store[j], 16)
                            act.wait(s, it, "hr", j)
                            for q in range(KD):
                                s.dma_start(g.hq[q][bass.ds(T * P, P), 0:F], hr[:, j, q * F:(q + 1) * F]
                                            ).then_inc(s_store[j], 16)
                        if second:
                            if not both:
                                if not isinstance(it, int):
                                    pe.wait(s, it - 1, "h2", j)
                                s.dma_start(hT[0][:, j, :], g.hT[bass.ds(T * P, P), :]).then_inc(s_load[j], 16)
                                s.dma_start(agg2[:, j, :].rearrange("p (q n) -> p q n", q=KD),
                                            g.agg2[:, :, bass.ds(T * P, P)].rearrange("q p n -> p q n")
                                            ).then_inc(s_load[j], 16)
                    if second:
                        for j in range(2):
                            act.wait(s, it, "x2", j)
                            s.dma_start(g.x2[bass.ds((it * 2 + j) * P, P), :], x2[:, j, :]).then_inc(s_store[j], 16)
                turns(s, body, HALF_TILES)
                per = 16 * HALF_TILES * (1 if second else 1 + KD)
                for j in range(2):
                    s.wait_ge(s_store[j], per)

            @block.scalar
            def _(s):
                def roots(it, name, i):
                    for j in range(2):
                        dve.wait(s, it, name, j)
                        s.activation(root[:, i, j:j + 1], mv[:, i, j, 1:2], ACT.Sqrt).then_inc(act.sem, 1)

                def body(it):
                    J = range(2)
                    if first:
                        for j in J:
                            s.activation(xs[:, j, :], g.xflat[:, bass.ds((it * 2 + j) * F, F)], ACT.Copy
                                         ).then_inc(act.sem, 1)
                        for j in J:
                            pe.wait(s, it, "xT", j)
                            s.activation(xT[:, j, :], tr[j][:, 0:P], ACT.Copy).then_inc(act.sem, 1)
                        roots(it, "var1", 0)
                        for j in J:
                            pe.wait(s, it, "h1T", j)
                            if not both and not isinstance(it, int):
                                s.wait_ge(s_store[j], it * (16 * (1 + KD)))
                            s.activation(hT[0][:, j, :], tr[j][:, :], ACT.Relu).then_inc(act.sem, 1)
                        if not both:
                            for j in J:
                                dve.wait(s, it, "h1", j)
                                s.activation(hr[:, j, :], h[0][:, j, :], ACT.Relu).then_inc(act.sem, 1)
                    if second:
                        roots(it, "var2", 1)
                        for j in J:
                            pe.wait(s, it, "h2T", j)
                            s.activation(hT[1][:, j, :], tr[j][:, :], ACT.Relu).then_inc(act.sem, 1)
                        roots(it, "vary", 2)
                        for j in J:
                            pe.wait(s, it, "yT", j)
                            s.activation(yT[:, j, :], tr[j][:, 0:P], ACT.Copy).then_inc(act.sem, 1)
                        for j in J:
                            dve.wait(s, it, "x12", j)
                            if not isinstance(it, int):
                                s.wait_ge(s_store[j], it * 16)
                            s.activation(x2[:, j, :], small[j][:, F:2 * F], ACT.Copy).then_inc(act.sem, 1)
                turns(s, body, HALF_TILES)

            @block.tensor
            def _(t):
                t.wait_ge(s_w, 16 * len(loads))

                def body(it):
                    J = range(2)
                    later = not isinstance(it, int)
                    if first:
                        for j in J:
                            act.wait(t, it, "xs", j)
                            if later and not both:
                                act.wait(t, it - 1, "h1T", j)
                            t.transpose(tr[j][:, 0:P], xs[:, j, :], g.ident[:, :]).then_inc(pe.sem, 1)
                        for j in J:
                            dve.wait(t, it, "agg", j)
                            act.wait(t, it, "xT", j)
                            t.matmul(big[j][:, :], agg[:, j, :], wrel1[:, :], start=True, stop=False)
                            t.matmul(big[j][:, :], xT[:, j, :], wroot1[:, :], start=False, stop=True
                                     ).then_inc(pe.sem, 1)
                        for j in J:
                            dve.wait(t, it, "h1", j)
                            for k in range(KD):
                                ins = t.transpose(tr[j][:, k * P:(k + 1) * P], h[0][:, j, k * P:(k + 1) * P], g.ident[:, :])
                            ins.then_inc(pe.sem, 1)
                    if second:
                        for j in J:
                            if both:
                                act.wait(t, it, "h1T", j)
                            else:
                                t.wait_ge(s_load[j], 32 * (it + 1))
                                dve.wait(t, it, "agg2", j)
                            for k in range(KD):
                                ins = t.matmul(big[j][:, :], hT[0][:, j, k * P:(k + 1) * P], wroot2[:, k, :],
                                               start=k == 0, stop=both and k == KD - 1)
                            if not both:
                                for k in range(KD):
                                    ins = t.matmul(big[j][:, :], agg2[:, j, k * P:(k + 1) * P], wrel2[:, k, :],
                                                   start=False, stop=k == KD - 1)
                            ins.then_inc(pe.sem, 1)
                        for j in J:
                            dve.wait(t, it, "h2", j)
                            for k in range(KD):
                                ins = t.transpose(tr[j][:, k * P:(k + 1) * P], h[1][:, j, k * P:(k + 1) * P], g.ident[:, :])
                            ins.then_inc(pe.sem, 1)
                        for j in J:
                            act.wait(t, it, "h2T", j)
                            if later:
                                act.wait(t, it - 1, "x2", j)
                            for k in range(KD):
                                ins = t.matmul(small[j][:, 0:F], hT[1][:, j, k * P:(k + 1) * P], wcls[:, k, :],
                                               start=k == 0, stop=k == KD - 1)
                            ins.then_inc(pe.sem, 1)
                        for j in J:
                            dve.wait(t, it, "y", j)
                            t.transpose(tr[j][:, 0:P], y[:, j, :], g.ident[:, :]).then_inc(pe.sem, 1)
                        for j in J:
                            act.wait(t, it, "yT", j)
                            t.matmul(small[j][:, 0:2 * F], yT[:, j, :], w12[:, :, :].rearrange("p c f -> p (c f)"),
                                     start=True, stop=True).then_inc(pe.sem, 1)
                turns(t, body, HALF_TILES)

            @block.vector
            def _(v):
                v.wait_ge(s_w, 16 * len(loads))

                def body(it):
                    ch = Chain(v, s_chain, it, LINKS)
                    J = range(2)

                    def stats(j, i, x):
                        ch.link(v.bn_stats(st[:, i, j, :], x))
                        v.sem_inc(s_go, 1)
                        ch.link(v.bn_aggr(mv[:, i, j, :], st[:, i, j, :]))
                        v.tensor_scalar(mv[:, i, j, 1:2], mv[:, i, j, 1:2], EPS, None, ALU.add).then_inc(dve.sem, 1)

                    def norm(j, i, x, root_of):
                        act.wait(v, it, root_of, j)
                        ch.link(v.reciprocal(mv[:, i, j, 1:2], root[:, i, j:j + 1]))
                        ch.link(v.tensor_scalar(x, x, mv[:, i, j, 0:1], mv[:, i, j, 1:2], ALU.subtract, ALU.mult))

                    def affine(i, source, names, root_of):
                        for j in J:
                            pe.wait(v, it, source, j)
                            ch.link(v.tensor_tensor(h[i][:, j, :], big[j][:, :], vec[names[0]][:, :], ALU.add))
                            stats(j, i, h[i][:, j, :])
                        for j in J:
                            norm(j, i, h[i][:, j, :], root_of)
                            ch.link(v.tensor_tensor(h[i][:, j, :], h[i][:, j, :], vec[names[1]][:, :], ALU.mult))
                            v.tensor_tensor(h[i][:, j, :], h[i][:, j, :], vec[names[2]][:, :], ALU.add
                                            ).then_inc(dve.sem, 1)

                    if first:
                        for j in J:
                            part = g.accT[:, bass.ds((it * 2 + j) * P, P)]
                            ch.link(v.tensor_scalar(low[:, j, :], part, HALFBIG, None, ALU.is_lt))
                            ch.link(v.scalar_tensor_tensor(out=finite[:, j, :], in0=part, scalar=-HALFBIG,
                                                           in1=low[:, j, :], op0=ALU.is_gt, op1=ALU.mult))
                            v.tensor_tensor(agg[:, j, :], finite[:, j, :], part, ALU.mult).then_inc(dve.sem, 1)
                        affine(0, "h1", ("brel1", "g1", "b1"), "root1")
                    if second:
                        if not both:
                            for j in J:
                                v.wait_ge(s_load[j], 32 * (it + 1))
                                ch.link(v.tensor_scalar(low2[:, j, :], agg2[:, j, :], HALFBIG, None, ALU.is_lt))
                                ch.link(v.scalar_tensor_tensor(out=low2[:, j, :], in0=agg2[:, j, :], scalar=-HALFBIG,
                                                               in1=low2[:, j, :], op0=ALU.is_gt, op1=ALU.mult))
                                v.tensor_tensor(agg2[:, j, :], low2[:, j, :], agg2[:, j, :], ALU.mult
                                                ).then_inc(dve.sem, 1)
                        affine(1, "h2", ("brel2", "g2", "b2"), "root2")
                        for j in J:
                            pe.wait(v, it, "cls", j)
                            ch.link(v.tensor_tensor(y[:, j, :], small[j][:, 0:F], vec["bcls"][:, :], ALU.add))
                            ch.link(v.tensor_tensor(y[:, j, :], y[:, j, :],
                                                    g.xflat[:, bass.ds((it * 2 + j) * F, F)], ALU.add))
                            stats(j, 2, y[:, j, :])
                        for j in J:
                            norm(j, 2, y[:, j, :], "rooty")
                            v.tensor_scalar(g.xflat[:, bass.ds((it * 2 + j) * F, F)], y[:, j, :], 1.0, None, ALU.mult
                                            ).then_inc(dve.sem, 1)
                        for j in J:
                            pe.wait(v, it, "x12", j)
                            to = g.yflat[:, bass.ds((it * 2 + j) * F, F)]
                            ch.link(v.tensor_tensor(to, small[j][:, 0:F], vec["L1b1"][:, :], ALU.add))
                            v.tensor_tensor(to, to, small[j][:, F:2 * F], ALU.subtract).then_inc(dve.sem, 1)
                    ch.end()
                turns(v, body, HALF_TILES)


def general_tables(nc, g, a):
    with ExitStack() as ctx:
        m = Memory(nc, ctx)
        half = m.sb("half", [P, NTP, F])
        s_half, s_out = m.sem("s_half"), m.sem("s_gout")
        with nc.Block() as block:
            @block.vector
            def _(v):
                v.memset(half[:, :, :], 0.5).then_inc(s_half, 1)

            @block.sync
            def _(s):
                s.wait_ge(s_half, 1)
                for q in range(DH // F):
                    s.dma_start(g.hq[q][:, F:2 * F].rearrange("(t p) f -> p t f", p=P), half[:, :, :]).then_inc(s_out, 16)
                    s.dma_start(g.hq[q][0:N, 2 * F:2 * F + 1], a["node_vec"].unsqueeze(1)).then_inc(s_out, 16)
                s.wait_ge(s_out, 32 * (DH // F))


def keep_agg2(nc, g, q):
    with ExitStack() as ctx:
        s_k = Memory(nc, ctx).sem(f"s_kept_agg{q}")
        with nc.Block() as block:
            @block.sync
            def _(s):
                s.dma_start(g.agg2[q, :, :], g.accT).then_inc(s_k, 16)
                s.wait_ge(s_k, 16)


def all_have_equal(nc, g):
    CH = 512
    chunks = [(lo, min(CH, N - lo)) for lo in range(0, N, CH)]
    with ExitStack() as ctx:
        m = Memory(nc, ctx)
        high = m.sb("high", [P, N])
        none = m.sb("none0", [P, CH])
        lack = m.sb("lack", [P, len(chunks)])
        tot = m.sb("lacktot", [P, 1])
        shown = [m.bank(f"shown{i}") for i in range(2)]
        s_v, s_t = m.sem("s_lv"), m.sem("s_lt")
        with nc.Block() as block:
            @block.vector
            def _(v):
                v.tensor_scalar(high[:, :], g.accT[:, 0:N], HALFBIG, None, ALU.is_gt).then_inc(s_v, 1)
                for c, (lo, n) in enumerate(chunks):
                    v.wait_ge(s_t, c + 1)
                    v.wait_ge(s_v, c + 1)
                    v.tensor_scalar(none[:, 0:n], shown[c % 2][:, 0:n], 0.0, 0.0, ALU.is_equal, ALU.add,
                                    accum_out=lack[:, c:c + 1]).then_inc(s_v, 1)
                v.wait_ge(s_v, len(chunks) + 1)
                v.tensor_reduce(tot[:, :], lack[:, :], AX.X, ALU.add).then_inc(s_v, 1)
                v.wait_ge(s_v, len(chunks) + 2)
                v.tensor_copy(g.lack[:, :], tot[:, :]).then_inc(s_v, 1)
                v.wait_ge(s_v, len(chunks) + 3)

            @block.tensor
            def _(t):
                for c, (lo, n) in enumerate(chunks):
                    t.wait_ge(s_v, max(1, c))
                    t.matmul(shown[c % 2][:, 0:n], g.ones[:, :], high[:, lo:lo + n], start=True, stop=True
                             ).then_inc(s_t, 1)


def sum_pass(nc, g, tag, table, acc):
    with ExitStack() as ctx:
        m = Memory(nc, ctx)
        ring = m.sb(f"ring{tag}", [P, U, FN])
        idx = m.sb(f"idx{tag}", [P, U], I32)
        hot = m.sb(f"hot{tag}", [P, NG, GS, P])
        sel = [[m.bank(f"sel{tag}{i}{j}") for j in range(2)] for i in range(2)]
        s_idx, s_go = m.sem(f"s_idx{tag}"), m.sem(f"s_go{tag}")
        s_g = [m.sem(f"s_g{tag}{i}") for i in range(NG)]
        s_hot, s_sel, s_acc = m.sem(f"s_hot{tag}"), m.sem(f"s_sel{tag}"), m.sem(f"s_acc{tag}")
        s_ini = m.sem(f"s_ini{tag}")
        s_one = m.sem(f"s_one{tag}")
        with nc.Block() as block:
            @block.gpsimd
            def _(p):
                p.memset(ring[:, :, :], 1.0).then_inc(s_one, 1)
                p.wait_ge(s_one, 1)

                def body(it):
                    for k in range(U):
                        q = k // GS
                        if k % GS == 0:
                            if not isinstance(it, int):
                                p.wait_ge(s_sel, it * NG - NG + q + 1)
                                p.sem_inc(s_go, 1)
                            p.tensor_copy(idx[:, k:k + GS], g.src_i[:, bass.ds(it * U + k, GS)]).then_inc(s_idx, 1)
                            p.wait_ge(s_idx, it * NG + q + 1)
                            p.sem_inc(s_go, 1)
                        p.indirect_dma_start(out=ring[:, k, 0:F], out_offset=None, in_=table,
                                             in_offset=bass.IndirectOffsetOnAxis(ap=idx[:, k:k + 1], axis=0)
                                             ).then_inc(s_g[k // GS], 16)
                turns(p, body, TURNS)

            @block.tensor
            def _(t):
                t.wait_ge(s_one, 1)

                def body(it):
                    for q in range(NG):
                        G = it * NG + q
                        wait(t, s_g[q], 64 * (it + 1))
                        wait(t, s_hot, G + 1)
                        wait(t, s_acc, (G - 1) * GS)
                        for k in range(GS):
                            ins = t.matmul(sel[q % 2][k // 2][:, (k % 2) * FN:(k % 2 + 1) * FN], hot[:, q, k, :],
                                           ring[:, q * GS + k, :], start=True, stop=True)
                        ins.then_inc(s_sel, 1)
                turns(t, body, TURNS)

            @block.vector
            def _(v):
                v.memset(acc, 0.0).then_inc(s_ini, 1)
                v.wait_ge(s_ini, 1)
                regs = [v.alloc_register(f"a{tag}{j}") for j in range(GS)]

                def add(G, q):
                    v.load(regs, g.T[0:1, bass.ds(G * GS, GS)])
                    T = [v.snap(r, min_val=0, max_val=NT - 1) for r in regs]
                    wait(v, s_sel, G + 1)
                    for k in range(GS):
                        wait(v, s_acc, G * GS + k)
                        to = acc[:, bass.ds(T[k] * FN, FN)]
                        v.tensor_tensor(to, to, sel[q % 2][k // 2][:, (k % 2) * FN:(k % 2 + 1) * FN], ALU.add
                                        ).then_inc(s_acc, 1)

                def body(it):
                    for q in range(NG):
                        G = it * NG + q
                        wait(v, s_sel, G - NG + 1)
                        v.tensor_tensor(hot[:, q, :, :], bc_mid(g.iota_n[:, :], GS),
                                        bc_last(g.drel[:, bass.ds(G * GS, GS)], P), ALU.is_equal).then_inc(s_hot, 1)
                        if not (isinstance(it, int) and q < 1):
                            add(G - 1, (q - 1) % NG)
                turns(v, body, TURNS)
                add(TURNS * NG - 1, NG - 1)


def finish1(nc, g):
    with ExitStack() as ctx:
        m = Memory(nc, ctx)
        mean, var = m.sb("mean1", [P, NTP]), m.sb("var1", [P, NTP])
        acc = g.acc[:, :].rearrange("p (t f) -> p t f", f=FN)
        s, s_root = m.sem("s_fin1"), m.sem("s_root1")
        ready = []
        with nc.Block() as block:
            @block.vector
            def _(v):
                ch = Chain(v, s, 0, 0)
                ch.link(v.tensor_copy(g.deg[:, :], acc[:, :, F]))
                ch.link(v.tensor_tensor(g.y[:, :, :], g.y[:, :, :], bc_last(g.deg[:, :], F), ALU.mult))
                ch.link(v.tensor_tensor(g.xflat, g.xflat, g.yflat, ALU.add))
                ch.link(v.tensor_tensor(g.x[:, :, :], g.x[:, :, :], acc[:, :, 0:F], ALU.add))
                ready.append(nodes_layernorm(v, ch, g.x[:, :, :], g.y[:, :, :], mean[:, :], var[:, :], s_root))

            root_of_variance(block, ready[0], s, var, s_root)


CHAINS = 8


def scatter_pass(nc, g):
    HP = U * P // 2
    with ExitStack() as ctx:
        m = Memory(nc, ctx)
        zero = m.sb("zero2", [P, NTP + 1, F])
        dstb = m.sb("dstb2", [P, 2, HP])
        srcb = m.sb("srcb2", [P, 2, HP])
        hotT = m.sb("hotT2", [P, 2, GS * P])
        same = m.sb("same2", [P, 2, GS, P])
        junk = m.sb("junk2", [P, GS, P])
        lower = m.sb("lower2", [P, P])
        spare = m.sb("spare2", [P, 1])
        before = m.sb("before2", [P, GS])
        far = m.sb("far2", [P, GS])
        idx_f = m.sb("idx_f2", [P, GS])
        idx = m.sb("idx2", [P, U], I32)
        val = m.sb("val2", [P, 2, GS * F])
        rows = m.sb("rows2", [P, U, F])
        vps = [m.bank(f"vps2{i}") for i in range(2)]
        sps = [m.bank(f"sps2{i}") for i in range(2)]
        s_zero, s_z = m.sem("s_zero2"), m.sem("s_z2")
        s_ini = m.sem("s_ini2")
        s_b = [m.sem(f"s_b2{i}") for i in range(2)]
        s_hot = m.sem("s_hot2")
        s_same = m.sem("s_same2")
        s_c = m.sem("s_c2")
        s_idx = m.sem("s_idx2")
        s_v = m.sem("s_v2")
        s_vc = m.sem("s_vc2")
        s_s = m.sem("s_s2")
        s_sc = m.sem("s_sc2")
        s_add = [m.sem(f"s_add2{i}") for i in range(CHAINS)]
        s_go = m.sem("s_go2")
        LK = 4
        with nc.Block() as block:
            @block.gpsimd
            def _(p):
                p.memset(zero[:, :, :], 0.0).then_inc(s_zero, 1)
                p.memset(lower[:, :], 1.0).then_inc(s_ini, 1)
                p.wait_ge(s_ini, 1)
                p.affine_select(out=lower[:, :], in_=lower[:, :], compare_op=ALU.is_gt, fill=0.0,
                                base=0, pattern=[[-1, P]], channel_multiplier=1).then_inc(s_ini, 1)
                p.wait_ge(s_z, 16 * CHAINS)

                def body(it):
                    for k in range(U):
                        if k % GS == 0:
                            p.wait_ge(s_idx, it * NG + k // GS + 1)
                            p.sem_inc(s_go, 1)
                            p.wait_ge(s_sc, it * NG + k // GS + 1)
                            p.sem_inc(s_go, 1)
                        n = it * (U // CHAINS) + k // CHAINS
                        if not (isinstance(n, int) and n == 0):
                            p.wait_ge(s_add[k % CHAINS], n * 16)
                            p.sem_inc(s_go, 1)
                        p.indirect_dma_start(out=g.sums[k % CHAINS][:, :],
                                             out_offset=bass.IndirectOffsetOnAxis(ap=idx[:, k:k + 1], axis=0),
                                             in_=rows[:, k, :], in_offset=None, compute_op=ALU.add
                                             ).then_inc(s_add[k % CHAINS], 16)
                turns(p, body, TURNS)
                for c in range(CHAINS):
                    p.wait_ge(s_add[c], 16 * (SP_ // CHAINS))

            @block.sync
            def _(s):
                s.wait_ge(s_zero, 1)
                for c in range(CHAINS):
                    s.dma_start(g.sums[c].rearrange("(t p) f -> p t f", p=P), zero[:, :, :]).then_inc(s_z, 16)

                def body(it):
                    for h in range(2):
                        if not isinstance(it, int):
                            s.wait_ge(s_same, it * NG - NG + 2 * h + 2)
                        at = bass.ds(it * (U * P) + h * HP, HP)
                        s.dma_start(dstb[:, h, :], g.drelflat[at].partition_broadcast(P)).then_inc(s_b[h], 16)
                        s.dma_start(srcb[:, h, :], g.srcflat[at].partition_broadcast(P)).then_inc(s_b[h], 16)
                turns(s, body, TURNS)

            @block.scalar
            def _(s):
                def sums(G, q):
                    wait(s, s_s, G + 1)
                    s.activation(rows[:, q * GS:(q + 1) * GS, :].rearrange("p k f -> p (k f)"), sps[q % 2][:, :],
                                 ACT.Copy).then_inc(s_sc, 1)

                def body(it):
                    for q in range(NG):
                        G = it * NG + q
                        wait(s, s_v, G + 1)
                        wait(s, s_s, G - 1)
                        s.activation(val[:, q % 2, :], vps[q % 2][:, :], ACT.Copy).then_inc(s_vc, 1)
                        if not (isinstance(it, int) and q < 1):
                            sums(G - 1, (q - 1) % NG)
                turns(s, body, TURNS)
                sums(TURNS * NG - 1, NG - 1)

            @block.tensor
            def _(t):
                regs = [t.alloc_register(f"v2{j}") for j in range(GS)]

                def sums(G, q):
                    wait(t, s_vc, G + 1)
                    wait(t, s_same, G + 1)
                    wait(t, s_sc, G - 1)
                    for k in range(GS):
                        ins = t.matmul(sps[q % 2][:, k * F:(k + 1) * F], same[:, q % 2, k, :],
                                       val[:, q % 2, k * F:(k + 1) * F], start=True, stop=True)
                    ins.then_inc(s_s, 1)

                def body(it):
                    for q in range(NG):
                        G = it * NG + q
                        t.load(regs, g.T[0:1, bass.ds(G * GS, GS)])
                        T = [t.snap(r, min_val=0, max_val=NT - 1) for r in regs]
                        wait(t, s_hot, G + 1)
                        wait(t, s_vc, G - 1)
                        for k in range(GS):
                            ins = t.matmul(vps[q % 2][:, k * F:(k + 1) * F], hotT[:, q % 2, k * P:(k + 1) * P],
                                           g.xflat[:, bass.ds(T[k] * F, F)], start=True, stop=True)
                        ins.then_inc(s_v, 1)
                        if not (isinstance(it, int) and q < 1):
                            sums(G - 1, (q - 1) % NG)
                turns(t, body, TURNS)
                sums(TURNS * NG - 1, NG - 1)

            @block.vector
            def _(v):
                v.wait_ge(s_ini, 2)
                v.tensor_scalar(spare[:, :], g.iota_p[:, :], float(NP), None, ALU.add).then_inc(s_ini, 1)
                v.wait_ge(s_ini, 3)

                def body(it):
                    for q in range(NG):
                        G = it * NG + q
                        h, off = q // 2, (q % 2) * GS * P
                        srcs = g.src_f[:, bass.ds(G * GS, GS)]
                        if q % 2 == 0:
                            v.wait_ge(s_b[h], 32 * (it + 1))
                        wait(v, s_v, G - 1)
                        v.tensor_scalar(hotT[:, q % 2, :], dstb[:, h, off:off + GS * P], g.iota_p[:, :], None,
                                        ALU.is_equal).then_inc(s_hot, 1)
                        for k in range(GS):
                            ins = v.scalar_tensor_tensor(
                                out=junk[:, k, :], in0=srcb[:, h, off + k * P:off + (k + 1) * P],
                                scalar=g.src_f[:, bass.ds(G * GS + k, 1)], in1=lower[:, :],
                                op0=ALU.is_equal, op1=ALU.mult, accum_out=before[:, k:k + 1])
                        ins.then_inc(s_c, 1)
                        wait(v, s_s, G - 1)
                        if not isinstance(it, int):
                            for c in range(GS):
                                k = q * GS + c
                                v.wait_ge(s_add[k % CHAINS], (it - 1) * 32 + (k // CHAINS + 1) * 16)
                        v.tensor_tensor(same[:, q % 2, :, :],
                                        srcb[:, h, off:off + GS * P].rearrange("p (k e) -> p k e", k=GS),
                                        bc_last(srcs, P), ALU.is_equal).then_inc(s_same, 1)
                        v.tensor_scalar(far[:, :], srcs, spare[:, :], -1.0, ALU.subtract, ALU.mult).then_inc(s_c, 1)
                        v.wait_ge(s_c, G * LK + 2)
                        v.scalar_tensor_tensor(out=idx_f[:, :], in0=before[:, :], scalar=1.0, in1=far[:, :],
                                               op0=ALU.min, op1=ALU.mult).then_inc(s_c, 1)
                        v.wait_ge(s_c, G * LK + 3)
                        v.tensor_tensor(idx_f[:, :], idx_f[:, :], srcs, ALU.add).then_inc(s_c, 1)
                        v.wait_ge(s_c, G * LK + 4)
                        v.tensor_copy(idx[:, q * GS:(q + 1) * GS], idx_f[:, :]).then_inc(s_idx, 1)
                turns(v, body, TURNS)


def finish2(nc, g):
    with ExitStack() as ctx:
        m = Memory(nc, ctx)
        part = [m.sb(f"part{i}", [P, NTP, F]) for i in range(2)]
        mean, var = m.sb("mean2", [P, NTP]), m.sb("var2", [P, NTP])
        ready, s_root = [], m.sem("s_root2")
        s, s_ld = m.sem("s_fin2"), [m.sem(f"s_ld2{i}") for i in range(2)]
        with nc.Block() as block:
            @block.sync
            def _(y):
                for c in range(CHAINS):
                    wait(y, s, c - 1)
                    y.dma_start(part[c % 2][:, :, :], g.sums[c][0:NP, :].rearrange("(t p) f -> p t f", p=P)
                                ).then_inc(s_ld[c % 2], 16)

            @block.vector
            def _(v):
                ch = Chain(v, s, 0, 0)
                for c in range(CHAINS):
                    v.wait_ge(s_ld[c % 2], 16 * (c // 2 + 1))
                    ch.link(v.tensor_tensor(g.x[:, :, :], g.x[:, :, :], part[c % 2][:, :, :], ALU.add))
                ready.append(nodes_layernorm(v, ch, g.x[:, :, :], part[0][:, :, :], mean[:, :], var[:, :], s_root))

            root_of_variance(block, ready[0], s, var, s_root)


def layer3_nodes(nc, g, a):
    with ExitStack() as ctx:
        m = Memory(nc, ctx)
        wlr = m.sb("wlr", [P, 2, F])
        bias = m.sb("bias_lr", [P, 2, F])
        xs, xT = m.sb("xs3", [P, 2, F]), m.sb("xT3", [P, 2, P])
        xl = m.sb("xl3", [P, 2, F])
        tr = [m.bank(f"tr3{j}") for j in range(2)]
        lr = [m.bank(f"lr3{j}") for j in range(2)]
        s_w = m.sem("s_w3")
        s_store = [m.sem(f"s_store3{j}") for j in range(2)]
        pe = Events(m.sem("s_pe3"), ["xT", "lr"])
        act = Events(m.sem("s_act3"), ["xs", "xT"])
        dve = Events(m.sem("s_dve3"), ["xl", "xr"])
        with nc.Block() as block:
            @block.sync
            def _(s):
                for c, (w, b) in enumerate((("L3_gnn_Wl", "L3_gnn_bl"), ("L3_gnn_Wr", "L3_gnn_br"))):
                    s.dma_start(wlr[:, c, :], a[w][:, :]).then_inc(s_w, 16)
                    s.dma_start(bias[:, c, :], a[b].partition_broadcast(P)).then_inc(s_w, 16)

                def body(it):
                    for j in range(2):
                        dve.wait(s, it, "xl", j)
                        s.dma_start(g.xl_rows[bass.ds((it * 2 + j) * P, P), :], xl[:, j, :]).then_inc(s_store[j], 16)
                turns(s, body, HALF_TILES)
                for j in range(2):
                    s.wait_ge(s_store[j], 16 * HALF_TILES)

            @block.scalar
            def _(s):
                def body(it):
                    for j in range(2):
                        if not isinstance(it, int):
                            pe.wait(s, it - 1, "xT", j)
                        s.activation(xs[:, j, :], g.xflat[:, bass.ds((it * 2 + j) * F, F)], ACT.Copy).then_inc(act.sem, 1)
                    for j in range(2):
                        pe.wait(s, it, "xT", j)
                        s.activation(xT[:, j, :], tr[j][:, 0:P], ACT.Copy).then_inc(act.sem, 1)
                turns(s, body, HALF_TILES)

            @block.tensor
            def _(t):
                t.wait_ge(s_w, 64)

                def body(it):
                    for j in range(2):
                        act.wait(t, it, "xs", j)
                        t.transpose(tr[j][:, 0:P], xs[:, j, :], g.ident[:, :]).then_inc(pe.sem, 1)
                    for j in range(2):
                        act.wait(t, it, "xT", j)
                        if not isinstance(it, int):
                            dve.wait(t, it - 1, "xr", j)
                        t.matmul(lr[j][:, 0:2 * F], xT[:, j, :], wlr[:, :, :].rearrange("p c f -> p (c f)"),
                                 start=True, stop=True).then_inc(pe.sem, 1)
                turns(t, body, HALF_TILES)

            @block.vector
            def _(v):
                v.wait_ge(s_w, 64)

                def body(it):
                    for j in range(2):
                        pe.wait(v, it, "lr", j)
                        if not isinstance(it, int):
                            v.wait_ge(s_store[j], it * 16)
                        v.tensor_tensor(xl[:, j, :], lr[j][:, 0:F], bias[:, 0, :], ALU.add).then_inc(dve.sem, 1)
                    for j in range(2):
                        v.tensor_tensor(g.xrflat[:, bass.ds((it * 2 + j) * F, F)], lr[j][:, F:2 * F], bias[:, 1, :],
                                        ALU.add).then_inc(dve.sem, 1)
                turns(v, body, HALF_TILES)


def score_pass(nc, g, a):
    HP = 2 * GS * P
    GH = GS * HEADS
    with ExitStack() as ctx:
        m = Memory(nc, ctx)
        ring = m.sb("ring3", [P, NG, GS, F])
        idx = m.sb("idx3", [P, NG, GS], I32)
        dstb = m.sb("dstb3", [P, 2, HP])
        reset = m.sb("reset3", [HEADS, 2, HP])
        ea = m.sb("ea3", [P, NG, GS, DE])
        eaT = m.sb("eaT3", [DE, NG, GS, P])
        hot = m.sb("hot3", [P, NG3, GS, P])
        hotT = m.sb("hotT3", [P, 2, GS * P])
        fifth = m.sb("fifth3", [P, 2, GS * F])
        leaky = m.sb("leaky3", [P, 2, GS * F])
        weighted = m.sb("weighted3", [P, 2, GS * F])
        sc = m.sb("sc3", [P, 2, GH])
        run = m.sb("run3", [HEADS, 2, GS * P])
        ends = m.sb("ends3", [P, 2, GS, HEADS])
        zps = [m.bank(f"zps3{i}") for i in range(2)]
        eps = [m.bank(f"eps3{i}") for i in range(2)]
        scT, back, top = m.bank("scT3"), m.bank("back3"), [m.bank(f"top3{i}") for i in range(2)]
        s_ini = m.sem("s_ini3")
        s_idx, s_go = m.sem("s_idx3"), m.sem("s_go3")
        s_g = [m.sem(f"s_g3{i}") for i in range(NG)]
        s_b = [m.sem(f"s_b3{i}") for i in range(2)]
        s_rst = [m.sem(f"s_rst3{i}") for i in range(2)]
        s_ea = [m.sem(f"s_ea3{i}") for i in range(NG)]
        s_rows = [m.sem(f"s_rows3{i}") for i in range(NG)]
        s_hotT = m.sem("s_hotT3")
        s_hot = m.sem("s_hot3")
        s_z = m.sem("s_z3")
        s_lk = m.sem("s_lk3")
        s_lz = m.sem("s_lz3")
        s_w = m.sem("s_wt3")
        s_sc = m.sem("s_sc3")
        s_keep = m.sem("s_keep3")
        s_scT = m.sem("s_scT3")
        s_run = m.sem("s_run3")
        s_back = m.sem("s_back3")
        s_end = m.sem("s_end3")
        s_top = m.sem("s_top3")
        s_esum = m.sem("s_esum3")
        s_max = m.sem("s_max3")

        def slot(it, q):
            return it * (NG3 // NG) + q // NG

        with nc.Block() as block:
            @block.gpsimd
            def _(p):
                def body(it):
                    for q in range(NG3):
                        G, c = it * NG3 + q, q % NG
                        if not (isinstance(it, int) and q < NG):
                            p.wait_ge(s_z, G - NG + 1)
                            p.sem_inc(s_go, 1)
                            p.wait_ge(s_rows[c], 16 * slot(it, q))
                            p.sem_inc(s_go, 1)
                        p.tensor_copy(idx[:, c, :], g.src_i[:, bass.ds(G * GS, GS)]).then_inc(s_idx, 1)
                        p.wait_ge(s_idx, G + 1)
                        p.sem_inc(s_go, 1)
                        for k in range(GS):
                            p.indirect_dma_start(out=ring[:, c, k, :], out_offset=None, in_=g.xl_rows[0:N, :],
                                                 in_offset=bass.IndirectOffsetOnAxis(ap=idx[:, c, k:k + 1], axis=0)
                                                 ).then_inc(s_g[c], 16)
                turns(p, body, TURNS3)

            @block.sync
            def _(s):
                regs = [s.alloc_register(f"t3{j}") for j in range(GS)]

                def keep(it, q):
                    s.wait_ge(s_g[q % NG], 64 * (slot(it, q) + 1))
                    s.dma_start(g.rows[bass.ds((it * NG3 + q) * GS, GS), :, :].rearrange("k e f -> e k f"),
                                ring[:, q % NG, :, :]).then_inc(s_rows[q % NG], 16)

                def resets(G, h):
                    wait(s, s_run, G - 2)
                    s.dma_start(reset[:, h, :], g.d0flat[bass.ds(G * (GS * P), HP)].partition_broadcast(HEADS)
                                ).then_inc(s_rst[h], 16)

                def body(it):
                    first = isinstance(it, int)
                    for q in range(NG3):
                        G, c = it * NG3 + q, q % NG
                        if q % 2 == 0:
                            h = q // 2 % 2
                            wait(s, s_hotT, G - 2)
                            s.dma_start(dstb[:, h, :], g.drelflat[bass.ds(G * (GS * P), HP)].partition_broadcast(P)
                                        ).then_inc(s_b[h], 16)
                            if not (first and q < 2):
                                resets(G - 2, 1 - h)
                        s.load(regs, g.t[0:1, bass.ds(G * GS, GS)])
                        t = [s.snap(r, min_val=0, max_val=ET - 1) for r in regs]
                        wait(s, s_z, G - NG + 1)
                        for k in range(GS):
                            s.dma_start(ea[:, c, k, :], a["ea"][bass.ds(t[k] * P, P), :]).then_inc(s_ea[c], 16)
                            s.dma_start(eaT[:, c, k, :], a["eaT"][:, bass.ds(t[k] * P, P)]).then_inc(s_ea[c], 16)
                        if not (first and q < 1):
                            keep(it if q else it - 1, (q - 1) % NG3)
                turns(s, body, TURNS3)
                keep(TURNS3 - 1, NG3 - 1)
                resets(TURNS3 * NG3 - 2, 1)
                for c in range(NG):
                    s.wait_ge(s_rows[c], 16 * TURNS3 * (NG3 // NG))

            @block.scalar
            def _(s):
                def body(it):
                    for q in range(NG3):
                        G = it * NG3 + q
                        wait(s, s_z, G + 1)
                        wait(s, s_lz, G - 1)
                        s.activation(fifth[:, q % 2, :], zps[q % 2][:, :], ACT.Copy, scale=0.2).then_inc(s_lk, 1)
                        if not (isinstance(it, int) and q < 1):
                            wait(s, s_sc, G)
                            s.activation(g.score[:, bass.ds((G - 1) * GH, GH)], sc[:, (q - 1) % 2, :], ACT.Copy
                                         ).then_inc(s_keep, 1)
                turns(s, body, TURNS3)
                s.wait_ge(s_sc, TURNS3 * NG3)
                s.activation(g.score[:, (SPX - GS) * HEADS:SPX * HEADS], sc[:, (NG3 - 1) % 2, :], ACT.Copy
                             ).then_inc(s_keep, 1)

            @block.tensor
            def _(t):
                regs = [t.alloc_register(f"v3{j}") for j in range(GS)]

                def z_of(it, q, T):
                    G, c = it * NG3 + q, q % NG
                    wait(t, s_hotT, G + 1)
                    t.wait_ge(s_g[c], 64 * (slot(it, q) + 1))
                    t.wait_ge(s_ea[c], 128 * (slot(it, q) + 1))
                    wait(t, s_lz, G - 1)
                    for k in range(GS):
                        z = zps[q % 2][:, k * F:(k + 1) * F]
                        t.matmul(z, hotT[:, q % 2, k * P:(k + 1) * P], g.xrflat[:, bass.ds(T[k] * F, F)],
                                 start=True, stop=False)
                        t.matmul(z, eaT[:, c, k, :], g.We[:, :], start=False, stop=False)
                        t.matmul(z, g.ident[:, :], ring[:, c, k, :], start=False, stop=True)
                    wait(t, s_hot, G + 1)
                    wait(t, s_esum, (G - 1) * GS)
                    for k in range(GS):
                        ins = t.matmul(eps[q % 2][:, k * DE:(k + 1) * DE], hot[:, q, k, :], ea[:, c, k, :],
                                       start=True, stop=True)
                    ins.then_inc(s_z, 1)

                def transposed(G, q):
                    wait(t, s_sc, G + 1)
                    wait(t, s_run, G)
                    for k in range(GS):
                        ins = t.transpose(scT[0:HEADS, k * P:(k + 1) * P], sc[:, q % 2, k * HEADS:(k + 1) * HEADS],
                                          g.ident[:, :])
                    ins.then_inc(s_scT, 1)

                def backward(G, q):
                    wait(t, s_run, G + 1)
                    wait(t, s_end, G)
                    t.sem_inc(s_go, 1)
                    for k in range(GS):
                        ins = t.transpose(back[:, k * HEADS:(k + 1) * HEADS], run[:, q % 2, k * P:(k + 1) * P],
                                          g.ident[0:HEADS, 0:HEADS])
                    ins.then_inc(s_back, 1)

                def place(G, q):
                    wait(t, s_end, G + 1)
                    wait(t, s_max, (G - 1) * GS)
                    for k in range(GS):
                        ins = t.matmul(top[q % 2][:, k * HEADS:(k + 1) * HEADS], hot[:, q, k, :], ends[:, q % 2, k, :],
                                       start=True, stop=True)
                    ins.then_inc(s_top, 1)

                def step(it, q, old, new=True):
                    G = it * NG3 + q
                    first = isinstance(it, int) and it == 0
                    if new:
                        t.load(regs, g.T[0:1, bass.ds(G * GS, GS)])
                        z_of(it, q, [t.snap(r, min_val=0, max_val=NT - 1) for r in regs])
                    for lag, stage in ((2, transposed), (3, backward), (4, place)):
                        if lag > 4 - old and not (first and q < lag):
                            stage(G - lag, (q - lag) % NG3)

                def body(it):
                    for q in range(NG3):
                        step(it, q, 3)
                turns(t, body, TURNS3)
                for q, old in enumerate((3, 3, 2, 1)):
                    step(TURNS3, q, old, False)

            @block.vector
            def _(v):
                v.memset(g.easum[:, :], 0.0).then_inc(s_ini, 1)
                v.memset(g.smax[:, :], 0.0).then_inc(s_ini, 1)
                v.memset(run[:, :, :], -BIG).then_inc(s_ini, 1)
                v.wait_ge(s_ini, 3)
                eregs = [v.alloc_register(f"e3{j}") for j in range(GS)]
                mregs = [v.alloc_register(f"m3{j}") for j in range(GS)]

                def tiles_of(G, regs):
                    v.load(regs, g.T[0:1, bass.ds(G * GS, GS)])
                    return [v.snap(r, min_val=0, max_val=NT - 1) for r in regs]

                def esum(G, q, k, T):
                    wait(v, s_esum, G * GS + k)
                    to = g.easum[:, bass.ds(T[k] * DE, DE)]
                    v.tensor_tensor(to, to, eps[q % 2][:, k * DE:(k + 1) * DE], ALU.add).then_inc(s_esum, 1)

                def smax(G, q, k, T):
                    if k == 0:
                        wait(v, s_top, G + 1)
                    wait(v, s_max, G * GS + k)
                    to = g.smax[:, bass.ds(T[k] * HEADS, HEADS)]
                    v.tensor_tensor(to, to, top[q % 2][:, k * HEADS:(k + 1) * HEADS], ALU.add).then_inc(s_max, 1)

                def scan(G, q, it):
                    wait(v, s_scT, G + 1)
                    if q % 2 == 0:
                        v.wait_ge(s_rst[q // 2 % 2], 16 * (it * (NG3 // 4) + q // 4 + 1))
                    wait(v, s_run, G)
                    wait(v, s_back, G - 1)
                    v.tensor_tensor_scan(run[:, q % 2, :], reset[:, q // 2 % 2, (q % 2) * GS * P:(q % 2 + 1) * GS * P],
                                         scT[0:HEADS, :], run[:, (q + 1) % 2, GS * P - 1:GS * P],
                                         ALU.min, ALU.max).then_inc(s_run, 1)

                def ends_of(G, q):
                    wait(v, s_back, G + 1)
                    wait(v, s_top, G - 1)
                    v.tensor_tensor(ends[:, q % 2, :, :], back[:, 0:GH].rearrange("p (k h) -> p k h", k=GS),
                                    bc_last(g.endf[:, bass.ds(G * GS, GS)], HEADS), ALU.mult).then_inc(s_end, 1)

                def step(it, q, last=0):
                    G = it * NG3 + q
                    first = isinstance(it, int) and it == 0
                    on = lambda lag: lag >= last and not (first and q < lag)
                    at = lambda lag: (G - lag, (q - lag) % NG3)
                    c = (q - 2) % 2
                    if on(0) and not last:
                        h, off = q // 2 % 2, (q % 2) * GS * P
                        if q % 2 == 0:
                            v.wait_ge(s_b[h], 16 * (it * (NG3 // 4) + q // 4 + 1))
                        wait(v, s_z, G - 1)
                        v.tensor_scalar(hotT[:, q % 2, :], dstb[:, h, off:off + GS * P], g.iota_p[:, :], None,
                                        ALU.is_equal).then_inc(s_hotT, 1)
                    if on(2):
                        wait(v, s_lk, G - 1)
                        v.tensor_tensor(leaky[:, c, :], zps[c][:, :], fifth[:, c, :], ALU.max).then_inc(s_lz, 1)
                        Te = tiles_of(G - 2, eregs)
                        esum(*at(2), 0, Te)
                    if on(0) and not last:
                        wait(v, s_top, G - NG3 + 1)
                        v.tensor_tensor(hot[:, q, :, :], bc_mid(g.iota_n[:, :], GS),
                                        bc_last(g.drel[:, bass.ds(G * GS, GS)], P), ALU.is_equal).then_inc(s_hot, 1)
                    if on(2):
                        esum(*at(2), 1, Te)
                        wait(v, s_lz, G - 1)
                        v.tensor_tensor(weighted[:, c, :].rearrange("p (k f) -> p k f", k=GS),
                                        leaky[:, c, :].rearrange("p (k f) -> p k f", k=GS), bc_mid(g.att[:, :], GS),
                                        ALU.mult).then_inc(s_w, 1)
                        esum(*at(2), 2, Te)
                    if on(3):
                        scan(*at(3), it if q >= 3 else it - 1)
                    if on(2):
                        esum(*at(2), 3, Te)
                    if on(5):
                        Tm = tiles_of(G - 5, mregs)
                        smax(*at(5), 0, Tm)
                    if on(2):
                        wait(v, s_w, G - 1)
                        wait(v, s_keep, G - 3)
                        wait(v, s_scT, G - 3)
                        v.tensor_reduce(sc[:, c, :], weighted[:, c, :].rearrange("p (k c) -> p k c", c=C), AX.X,
                                        ALU.add).then_inc(s_sc, 1)
                    if on(5):
                        smax(*at(5), 1, Tm)
                    if on(4):
                        ends_of(*at(4))
                    if on(5):
                        smax(*at(5), 2, Tm)
                        smax(*at(5), 3, Tm)

                def body(it):
                    for q in range(NG3):
                        step(it, q)
                turns(v, body, TURNS3)
                for q in range(5):
                    step(TURNS3, q, q + 1)


def self_loops(nc, g, a):
    with ExitStack() as ctx:
        m = Memory(nc, ctx)
        rdeg, none = m.sb("rdeg", [P, NTP]), m.sb("none", [P, NTP])
        ls, lT = m.sb("ls", [P, 2, DE]), m.sb("lT", [DE, 2, P])
        xl = m.sb("xln", [P, NTP, F])
        z, z2 = m.sb("zn", [P, NTP, F]), m.sb("zn2", [P, NTP, F])
        zf = z[:, :, :].rearrange("p t f -> p (t f)")
        sl = m.sb("sl", [P, NTP * HEADS])
        inside = m.sb("inside", [P, SP_])
        tr = [m.bank(f"trl{j}") for j in range(2)]
        zp = [m.bank(f"zl{j}") for j in range(2)]
        s_c, s_x, s_e = m.sem("s_cl"), m.sem("s_xln"), m.sem("s_el")
        pe = Events(m.sem("s_pel"), ["lT", "z"])
        act = Events(m.sem("s_actl"), ["ls", "lT", "z"])
        LINKS = 15
        s_go = m.sem("s_gol")
        with nc.Block() as block:
            @block.sync
            def _(s):
                s.dma_start(xl[:, :, :], g.xl_rows.rearrange("(t p) f -> p t f", p=P)).then_inc(s_x, 16)

            @block.scalar
            def _(s):
                s.wait_ge(s_c, 7)

                def body(it):
                    J = range(2)
                    for j in J:
                        s.activation(ls[:, j, :], g.easum[:, bass.ds((it * 2 + j) * DE, DE)], ACT.Copy).then_inc(act.sem, 1)
                    for j in J:
                        pe.wait(s, it, "lT", j)
                        s.activation(lT[:, j, :], tr[j][0:DE, 0:P], ACT.Copy).then_inc(act.sem, 1)
                    for j in J:
                        pe.wait(s, it, "z", j)
                        s.activation(zf[:, bass.ds((it * 2 + j) * F, F)], zp[j][:, 0:F], ACT.Copy).then_inc(act.sem, 1)
                turns(s, body, HALF_TILES)
                s.wait_ge(s_c, LINKS)
                s.activation(g.eloop[:, :], sl[:, :], ACT.Exp).then_inc(s_e, 1)

            @block.tensor
            def _(t):
                def body(it):
                    J = range(2)
                    for j in J:
                        act.wait(t, it, "ls", j)
                        t.sem_inc(s_go, 1)
                        t.transpose(tr[j][0:DE, 0:P], ls[:, j, :], g.ident[:, :]).then_inc(pe.sem, 1)
                    for j in J:
                        act.wait(t, it, "lT", j)
                        t.matmul(zp[j][:, 0:F], lT[:, j, :], g.We[:, :], start=True, stop=True).then_inc(pe.sem, 1)
                turns(t, body, HALF_TILES)

            @block.vector
            def _(v):
                ch = Chain(v, s_c, 0, 0)
                deg = g.deg[:, :]
                ch.link(v.tensor_scalar(rdeg[:, :], deg, 1.0, None, ALU.max))
                ch.link(v.reciprocal(rdeg[:, :], rdeg[:, :]))
                ch.link(v.tensor_scalar(none[:, :], deg, 0.0, -BIG, ALU.is_equal, ALU.mult))
                drel = g.drel[:, 0:SP_]
                ch.link(v.tensor_scalar(inside[:, :], drel, 0.0, None, ALU.is_ge))
                ch.link(v.scalar_tensor_tensor(out=inside[:, :], in0=drel, scalar=float(P), in1=inside[:, :],
                                               op0=ALU.is_lt, op1=ALU.mult))
                scores = g.score[:, 0:SP_ * HEADS].rearrange("p (k h) -> p k h", h=HEADS)
                ch.link(v.tensor_tensor(scores, scores, bc_last(inside[:, :], HEADS), ALU.mult))
                es = g.easum[:, :].rearrange("p (t d) -> p t d", d=DE)
                ch.link(v.tensor_tensor(es, es, bc_last(rdeg[:, :], DE), ALU.mult))
                sm = g.smax[:, :].rearrange("p (t h) -> p t h", h=HEADS)
                ch.link(v.tensor_tensor(sm, sm, bc_last(none[:, :], HEADS), ALU.add))
                act.wait(v, HALF_TILES - 1, "z", 1)
                v.wait_ge(s_x, 16)
                ch.link(v.tensor_tensor(z[:, :, :], z[:, :, :], xl[:, :, :], ALU.add))
                ch.link(v.tensor_tensor(zf, zf, g.xrflat, ALU.add))
                ch.link(v.scalar_tensor_tensor(out=z2[:, :, :], in0=z[:, :, :], scalar=0.2, in1=z[:, :, :],
                                               op0=ALU.mult, op1=ALU.max))
                ch.link(v.tensor_tensor(z2[:, :, :], z2[:, :, :], bc_mid(g.att[:, :], NTP), ALU.mult))
                ch.link(v.tensor_reduce(sl[:, :], z2[:, :, :].rearrange("p t (h c) -> p (t h) c", c=C), AX.X, ALU.add))
                ch.link(v.tensor_tensor(g.smax[:, :], g.smax[:, :], sl[:, :], ALU.max))
                ch.link(v.tensor_tensor(sl[:, :], sl[:, :], g.smax[:, :], ALU.subtract))
                assert ch.n == LINKS
                v.wait_ge(s_e, 1)


def weighted_pass(nc, g):
    HP = U * P // 2
    GH = GS * HEADS
    with ExitStack() as ctx:
        m = Memory(nc, ctx)
        rows = m.sb("rows4", [P, NG, GS * F])
        dstb = m.sb("dstb4", [P, 2, HP])
        hot = m.sb("hot4", [P, NG, GS, P])
        hotT = m.sb("hotT4", [P, 2, GS * P])
        under = m.sb("under4", [P, 2, GH])
        val = m.sb("val4", [P, NG, GS, FH])
        mps = [m.bank(f"mps4{i}") for i in range(2)]
        ops = [[m.bank(f"ops4{i}{j}") for j in range(2)] for i in range(2)]
        s_ini = m.sem("s_ini4")
        s_b = [m.sem(f"s_b4{i}") for i in range(2)]
        s_r = [m.sem(f"s_r4{i}") for i in range(NG)]
        s_hot = m.sem("s_hot4")
        s_hotT = m.sem("s_hotT4")
        s_m = m.sem("s_m4")
        s_u = m.sem("s_u4")
        s_ex = m.sem("s_ex4")
        s_val = m.sem("s_val4")
        s_o = m.sem("s_o4")
        s_out = m.sem("s_out4")
        with nc.Block() as block:
            @block.sync
            def _(s):
                def body(it):
                    for q in range(NG):
                        if q % 2 == 0:
                            h = q // 2
                            if not isinstance(it, int):
                                s.wait_ge(s_hotT, it * NG - NG + 2 * h + 2)
                            s.dma_start(dstb[:, h, :], g.drelflat[bass.ds(it * (U * P) + h * HP, HP)].partition_broadcast(P)
                                        ).then_inc(s_b[h], 16)
                        if not isinstance(it, int):
                            s.wait_ge(s_val, it * NG - NG + q + 1)
                        s.dma_start(rows[:, q, :].rearrange("p (k f) -> p k f", k=GS),
                                    g.rows[bass.ds((it * NG + q) * GS, GS), :, :].rearrange("k e f -> e k f")
                                    ).then_inc(s_r[q], 16)
                turns(s, body, TURNS)

            @block.gpsimd
            def _(p):
                def body(it):
                    for q in range(NG):
                        G = it * NG + q
                        wait(p, s_ex, G + 1)
                        p.wait_ge(s_r[q], 16 * (it + 1))
                        p.tensor_tensor(val[:, q, :, 0:F].rearrange("p k (h c) -> p k h c", c=C),
                                        rows[:, q, :].rearrange("p (k h c) -> p k h c", k=GS, c=C),
                                        val[:, q, :, F:FH].unsqueeze(3).broadcast_to([P, GS, HEADS, C]),
                                        ALU.mult).then_inc(s_val, 1)
                turns(p, body, TURNS)

            @block.scalar
            def _(s):
                def body(it):
                    for q in range(NG):
                        G = it * NG + q
                        wait(s, s_u, G + 1)
                        wait(s, s_o, G - NG + 1)
                        s.activation(val[:, q, :, F:FH], under[:, q % 2, :].rearrange("p (k h) -> p k h", k=GS),
                                     ACT.Exp).then_inc(s_ex, 1)
                turns(s, body, TURNS)

            @block.tensor
            def _(t):
                regs = [t.alloc_register(f"v4{j}") for j in range(GS)]

                def sums(G, q):
                    wait(t, s_hot, G + 1)
                    wait(t, s_val, G + 1)
                    wait(t, s_out, (G - 1) * GS)
                    for k in range(GS):
                        ins = t.matmul(ops[q % 2][k // 2][:, (k % 2) * FH:(k % 2 + 1) * FH], hot[:, q, k, :],
                                       val[:, q, k, :], start=True, stop=True)
                    ins.then_inc(s_o, 1)

                def body(it):
                    for q in range(NG):
                        G = it * NG + q
                        t.load(regs, g.T[0:1, bass.ds(G * GS, GS)])
                        T = [t.snap(r, min_val=0, max_val=NT - 1) for r in regs]
                        wait(t, s_hotT, G + 1)
                        wait(t, s_u, G - 1)
                        for k in range(GS):
                            ins = t.matmul(mps[q % 2][:, k * HEADS:(k + 1) * HEADS], hotT[:, q % 2, k * P:(k + 1) * P],
                                           g.smax[:, bass.ds(T[k] * HEADS, HEADS)], start=True, stop=True)
                        ins.then_inc(s_m, 1)
                        if not (isinstance(it, int) and q < 2):
                            sums(G - 2, (q - 2) % NG)
                turns(t, body, TURNS)
                for b in (2, 1):
                    sums(TURNS * NG - b, NG - b)

            @block.vector
            def _(v):
                v.memset(g.out[:, :], 0.0).then_inc(s_ini, 1)
                v.wait_ge(s_ini, 1)
                regs = [v.alloc_register(f"a4{j}") for j in range(GS)]

                def add(G, q, k, T):
                    if k == 0:
                        wait(v, s_o, G + 1)
                    wait(v, s_out, G * GS + k)
                    to = g.out[:, bass.ds(T[k] * FH, FH)]
                    v.tensor_tensor(to, to, ops[q % 2][k // 2][:, (k % 2) * FH:(k % 2 + 1) * FH], ALU.add
                                    ).then_inc(s_out, 1)

                def step(it, q, stages):
                    G = it * NG + q
                    h, off = (q // 2) % 2, (q % 2) * GS * P
                    first = isinstance(it, int) and it == 0
                    adds = "a" in stages and not (first and q < 3)
                    if "h" in stages:
                        if q % 2 == 0:
                            v.wait_ge(s_b[h], 16 * (it + 1))
                        wait(v, s_m, G - 1)
                        v.tensor_scalar(hotT[:, q % 2, :], dstb[:, h, off:off + GS * P], g.iota_p[:, :], None,
                                        ALU.is_equal).then_inc(s_hotT, 1)
                    if adds:
                        v.load(regs, g.T[0:1, bass.ds((G - 3) * GS, GS)])
                        T = [v.snap(r, min_val=0, max_val=NT - 1) for r in regs]
                        add(G - 3, (q - 3) % NG, 0, T)
                    if "u" in stages and not (first and q < 1):
                        wait(v, s_m, G)
                        wait(v, s_ex, G - 2)
                        v.tensor_tensor(under[:, (q - 1) % 2, :], g.score[:, bass.ds((G - 1) * GH, GH)],
                                        mps[(q - 1) % 2][:, 0:GH], ALU.subtract).then_inc(s_u, 1)
                    if adds:
                        add(G - 3, (q - 3) % NG, 1, T)
                    if "h" in stages:
                        wait(v, s_o, G - NG + 1)
                        v.tensor_tensor(hot[:, q, :, :], bc_mid(g.iota_n[:, :], GS),
                                        bc_last(g.drel[:, bass.ds(G * GS, GS)], P), ALU.is_equal).then_inc(s_hot, 1)
                    if adds:
                        add(G - 3, (q - 3) % NG, 2, T)
                        add(G - 3, (q - 3) % NG, 3, T)

                def body(it):
                    for q in range(NG):
                        step(it, q, "hua")
                turns(v, body, TURNS)
                step(TURNS, 0, "ua")
                step(TURNS, 1, "a")
                step(TURNS, 2, "a")


def finish3(nc, g, a):
    with ExitStack() as ctx:
        m = Memory(nc, ctx)
        names = ("bias_out", "gn_weight", "gn_bias", "gn_mean_scale")
        vec = {n: m.sb("v" + n, [P, F]) for n in names}
        xl = m.sb("xl5", [P, NTP, F])
        sq = m.sb("sq5", [P, NTP, F])
        sqf = sq[:, :, :].rearrange("p t f -> p (t f)")
        out = m.sb("out5", [P, NTP * F])
        den = m.sb("den5", [P, NTP * HEADS])
        mean, scale = m.sb("gmean", [P, F]), m.sb("gscale", [P, F])
        rmean, var = m.sb("rmean", [P, NTP]), m.sb("rvar", [P, NTP])
        mp, vp = m.bank("mp5"), m.bank("vp5")
        s, s_w, s_root, s_sum, s_groot = m.sem("s5"), m.sem("s_w5"), m.sem("s_root5"), m.sem("s_sum5"), m.sem("s_gr5")
        ready = []
        with nc.Block() as block:
            @block.sync
            def _(e):
                e.dma_start(xl[:, :, :], g.xl_rows.rearrange("(t p) f -> p t f", p=P)).then_inc(s_w, 16)
                for n in names:
                    e.dma_start(vec[n][:, :], a["L3_gnn_" + n].partition_broadcast(P)).then_inc(s_w, 16)

            @block.vector
            def _(v):
                ch = Chain(v, s, 0, 0)
                out3 = out[:, :].rearrange("p (t f) -> p t f", f=F)
                outh = out[:, :].rearrange("p (h c) -> p h c", c=C)
                acc = g.out[:, :].rearrange("p (t f) -> p t f", f=FH)
                v.wait_ge(s_w, 16 * 5)
                ch.link(v.tensor_tensor(sqf.rearrange("p (h c) -> p h c", c=C),
                                        xl[:, :, :].rearrange("p t (h c) -> p (t h) c", c=C),
                                        bc_last(g.eloop[:, :], C), ALU.mult))
                ch.link(v.tensor_tensor(out3, acc[:, :, 0:F], sq[:, :, :], ALU.add))
                ch.link(v.tensor_tensor(den[:, :].rearrange("p (t h) -> p t h", h=HEADS), acc[:, :, F:FH],
                                        g.eloop[:, :].rearrange("p (t h) -> p t h", h=HEADS), ALU.add))
                ch.link(v.tensor_scalar(den[:, :], den[:, :], 1e-16, None, ALU.add))
                ch.link(v.reciprocal(den[:, :], den[:, :]))
                ch.link(v.tensor_tensor(outh, outh, bc_last(den[:, :], C), ALU.mult))
                ch.link(v.tensor_tensor(out3, out3, bc_mid(vec["bias_out"][:, :], NTP), ALU.add))
                ready.append(ch.n)
                v.wait_ge(s_sum, 1)
                ch.link(v.scalar_tensor_tensor(out=mean[:, :], in0=mp[:, 0:F], scalar=1.0 / N,
                                               in1=vec["gn_mean_scale"][:, :], op0=ALU.mult, op1=ALU.mult))
                ch.link(v.tensor_tensor(out3, out3, bc_mid(mean[:, :], NTP), ALU.subtract))
                ch.link(v.tensor_tensor(sqf, out[:, :], out[:, :], ALU.mult))
                ready.append(ch.n)
                v.wait_ge(s_sum, 2)
                ch.link(v.tensor_scalar(scale[:, :], vp[:, 0:F], 1.0 / N, EPS, ALU.mult, ALU.add))
                ready.append(ch.n)
                v.wait_ge(s_groot, 1)
                ch.link(v.reciprocal(scale[:, :], scale[:, :]))
                ch.link(v.tensor_tensor(scale[:, :], scale[:, :], vec["gn_weight"][:, :], ALU.mult))
                ch.link(v.tensor_tensor(out3, out3, bc_mid(scale[:, :], NTP), ALU.mult))
                ch.link(v.tensor_tensor(out3, out3, bc_mid(vec["gn_bias"][:, :], NTP), ALU.add))
                ch.link(v.scalar_tensor_tensor(out=g.xflat, in0=out[:, :], scalar=0.0, in1=g.xflat,
                                               op0=ALU.max, op1=ALU.add))
                ready.append(nodes_layernorm(v, ch, g.x[:, :, :], sq[:, :, :], rmean[:, :], var[:, :], s_root))

            @block.tensor
            def _(t):
                for i, (bank, rows) in enumerate(((mp, out[:, :]), (vp, sqf))):
                    t.wait_ge(s, ready[i])
                    for T in range(NT):
                        w = g.valid if T == NT - 1 else g.ones
                        ins = t.matmul(bank[:, 0:F], w[:, :], rows[:, T * F:(T + 1) * F], start=T == 0, stop=T == NT - 1)
                    ins.then_inc(s_sum, 1)

            @block.scalar
            def _(e):
                e.wait_ge(s, ready[2])
                e.activation(scale[:, :], scale[:, :], ACT.Sqrt).then_inc(s_groot, 1)
                e.wait_ge(s, ready[3])
                e.activation(var[:, :], var[:, :], ACT.Sqrt).then_inc(s_root, 1)


def layer3(nc, g, a):
    with ExitStack() as ctx:
        m = Memory(nc, ctx)
        g.score = m.sb("score", [P, SPX * HEADS])
        g.smax, g.eloop = m.sb("smax", [P, NTP * HEADS]), m.sb("eloop", [P, NTP * HEADS])
        with ExitStack() as c3:
            m3 = Memory(nc, c3)
            g.xr = m3.sb("xr", [P, NTP * F])
            g.xrflat = g.xr[:, :]
            g.easum = m3.sb("easum", [P, NTP * DE])
            g.We, g.att = m3.sb("We", [DE, F]), m3.sb("att", [P, F])
            s_w = m3.sem("s_we")
            with nc.Block() as block:
                @block.sync
                def _(s):
                    s.dma_start(g.We[:, :], a["L3_gnn_We"][:, :]).then_inc(s_w, 16)
                    s.dma_start(g.att[:, :], a["L3_gnn_att"].rearrange("h c -> (h c)").partition_broadcast(P)).then_inc(s_w, 16)
                    s.wait_ge(s_w, 32)
            layer3_nodes(nc, g, a)
            score_pass(nc, g, a)
            self_loops(nc, g, a)
        g.out = m.sb("out3", [P, NTP * FH])
        weighted_pass(nc, g)
        finish3(nc, g, a)


class Shared:
    pass


def build(nc, a, out, stop=None):
    g = Shared()
    dram = lambda name, shape, dt=F32: nc.dram_tensor(name, shape, dt).ap()
    g.ct = dram("edge_rows", (ET, 4 * P), I32)
    g.d0row = dram("resets", (SPX, P))
    g.drelrow = dram("dst_in_tile", (SPX, P))
    g.srcrow = dram("src_rows", (SPX, P))
    g.d0flat, g.drelflat, g.srcflat = (r.rearrange("k e -> (k e)") for r in (g.d0row, g.drelrow, g.srcrow))
    g.trow = dram("node_tile_of_step", (KB * P,), I32)
    g.erow = dram("edge_tile_of_step", (KB * P,), I32)
    g.xp = dram("x_sign_pos", (NP, W))
    g.hq = [dram(f"h_sign_pos{q}", (NP, W)) for q in range(DH // F)]
    g.hT = dram("h_transposed", (NP, DH))
    g.agg2 = dram("agg2", (DH // F, P, NP))
    g.x2 = dram("x2", (NP, F))
    g.sums = [dram(f"sums{c}", (NP + P, F)) for c in range(CHAINS)]
    g.xl_rows = dram("xl_rows", (NP, F))
    g.rows = dram("xl_of_steps", (SPX, P, F))
    with ExitStack() as ctx:
        ctx.enter_context(nc.allow_non_contiguous_dma(reason="columns of positions and node tiles, a few thousand words"))
        m = Memory(nc, ctx)
        g.src_i = m.sb("src_i", [P, KB * P], I32)
        g.src_f = m.sb("src_f", [P, KB * P])
        g.drel = m.sb("drel", [P, KB * P])
        g.endf = m.sb("endf", [P, KB * P])
        g.T = m.sb("T", [1, SPX], I32)
        g.t = m.sb("t", [1, SPX], I32)
        g.iota_n = m.sb("iota_n", [P, P])
        g.iota_p = m.sb("iota_p", [P, 1])
        g.valid = m.sb("valid", [P, P])
        g.ones = m.sb("ones", [P, P])
        g.ident = m.sb("ident", [P, P])
        g.lack = m.sb("lack_i", [P, 1], I32)
        g.deg = m.sb("deg", [P, NTP])
        g.x = m.sb("x_nodes", [P, NTP, F])
        g.xflat = g.x[:, :, :].rearrange("p t f -> p (t f)")
        with ExitStack() as c12:
            m12 = Memory(nc, c12)
            g.acc = m12.sb("acc", [P, NTP * FN])
            g.accT = g.acc[:, 0:NP]
            g.y = m12.sb("y_nodes", [P, NTP, F])
            g.yflat = g.y[:, :, :].rearrange("p t f -> p (t f)")
            with ExitStack() as c0:
                g.posb = Memory(nc, c0).sb("posb", [P, NP])
                prepare(nc, g, a)
                max_pass(nc, g, "a", g.xp[0:N, :], g.accT)
                all_have_equal(nc, g)
                lack = nc.values_load(g.lack[0:1, 0:1], min_val=0, max_val=N)
                with nc.If(lack > 0):
                    nc.all_engine_barrier()
                    layer0(nc, g, a, "f", True, False)
                    general_tables(nc, g, a)
                    for q in range(DH // F):
                        max_pass(nc, g, f"q{q}", g.hq[q][0:N, :], g.accT)
                        keep_agg2(nc, g, q)
                    layer0(nc, g, a, "s", False, True)
                with nc.Else():
                    nc.all_engine_barrier()
                    layer0(nc, g, a, "b", True, True)
            if stop != "L0":
                sum_pass(nc, g, "1", g.x2[0:N, :], g.acc[:, :])
                finish1(nc, g)
        if stop is None or stop == "L2":
            scatter_pass(nc, g)
            finish2(nc, g)
        if stop is None:
            layer3(nc, g, a)
        store(nc, g, out)


def store(nc, g, out):
    with ExitStack() as ctx:
        s_o = Memory(nc, ctx).sem("s_stored")
        with nc.Block() as block:
            @block.sync
            def _(s):
                s.dma_start(out[0:(NT - 1) * P, :].rearrange("(t p) f -> p t f", p=P), g.x[:, 0:NT - 1, :]).then_inc(s_o, 16)
                s.dma_start(out[(NT - 1) * P:N, :], g.x[0:N - (NT - 1) * P, NT - 1, :]).then_inc(s_o, 16)
                s.wait_ge(s_o, 32)


def kernel(**inputs):
    import numpy as np
    import concourse.bacc as bacc
    from concourse.bass_utils import run_bass_kernel_spmd as run
    nc = bacc.Bacc("TRN2", target_bir_lowering=False, num_devices=1)
    arrays, aps = {}, {}
    transposed = {"L0_gnn_Wrel1": "Wrel1T", "L0_gnn_Wroot1": "Wroot1T", "L0_gnn_Wrel2": "Wrel2T",
                  "L0_gnn_Wroot2": "Wroot2T", "L0_gnn_Wcls": "WclsT", "L1_gnn_W1": "W1T", "L1_gnn_W2": "W2T"}
    for name, v in inputs.items():
        v = np.asarray(v)
        if name in transposed:
            v, name = v.T, transposed[name]
        if name == "edge_attr_64":
            rows = np.zeros((ET * P, DE), v.dtype)
            rows[:E] = v
            layouts = {"ea": rows, "eaT": rows.T}
        else:
            layouts = {name: v}
        for name, v in layouts.items():
            v = np.ascontiguousarray(v)
            arrays["in_" + name] = v
            aps[name] = nc.dram_tensor("in_" + name, v.shape, mybir.dt.from_np(v.dtype), kind="ExternalInput").ap()
    out = nc.dram_tensor("out", (N, F), F32, kind="ExternalOutput").ap()
    build(nc, aps, out, None)
    r = run(nc, [arrays], core_ids=[0])
    return r.results[0]["out"]
```
